# Optimizing a Trainium2 kernel written in Bass

```python
import numpy as np
import jax
import jax.numpy as jnp

def _softmax(x, axis=-1):
    return jax.nn.softmax(x, axis=axis)

def _gelu(x):
    return jax.nn.gelu(x, approximate=True)

def _silu(x):
    return jax.nn.silu(x)

def _sigmoid(x):
    return jax.nn.sigmoid(x)

def _layernorm(x, axis=-1, eps=1e-05):
    m = jnp.mean(x, axis=axis, keepdims=True)
    v = jnp.var(x, axis=axis, keepdims=True)
    return (x - m) / jnp.sqrt(v + eps)

def _scatter_add(tgt, idx, src, axis=0):
    return tgt.at[idx].add(src)

def _segment_sum(src, seg, n):
    return jax.ops.segment_sum(src, seg, n)
kernel_name = 'mk_adaln_d1_jaxref_r4_8400cc'

def setup_inputs(seed: int=0):
    np.random.seed(seed)
    _w = jnp.asarray

    def _L0_attn_setup():
        import jax, jax.numpy as jnp
        import numpy as np
        H = 16
        D = 128
        M = 16
        ROPE = 64
        THETA = 10000.0
        WIN = 128
        CAP = 50.0
        G = 4
        HID = 512
        QC = 128
        INTER = 512

        def rope_cache(t):
            inv = 1.0 / THETA ** (jnp.arange(0, ROPE, 2, dtype=jnp.float32) / ROPE)
            ang = jnp.arange(t, dtype=jnp.float32)[:, None] * inv[None, :]
            return (jnp.cos(ang), jnp.sin(ang))

        def apply_partial_rope(x, cos, sin):
            x1 = x[..., :ROPE // 2]
            x2 = x[..., ROPE // 2:ROPE]
            rest = x[..., ROPE:]
            return jnp.concatenate([x1 * cos - x2 * sin, x1 * sin + x2 * cos, rest], axis=-1)

        def rmsnorm(x, w, eps=1e-06):
            return x * jax.lax.rsqrt(jnp.mean(x * x, axis=-1, keepdims=True) + eps) * w

        def attend(scores, mask, sink, v, sub):
            b, h, t, _ = scores.shape
            logits = jnp.where(mask, scores, jnp.float32(-1e+30))
            sink_col = jnp.broadcast_to(sink[None, :, None, None], (b, h, t, 1))
            probs = jax.nn.softmax(jnp.concatenate([logits, sink_col], axis=-1), axis=-1)[..., :-1]
            return jnp.einsum(sub, probs, v)
        key = jax.random.key(seed)
        ks = jax.random.split(key, 12)
        s = 0.02
        return {'h': jax.random.normal(ks[0], (2, 512, HID), dtype=jnp.float32), 'Wq_c': jax.random.normal(ks[1], (HID, QC), dtype=jnp.float32) * s, 'Wq_up': jax.random.normal(ks[2], (QC, H * D), dtype=jnp.float32) * s, 'Wk': jax.random.normal(ks[3], (HID, D), dtype=jnp.float32) * s, 'Wv': jax.random.normal(ks[4], (HID, D), dtype=jnp.float32) * s, 'W_comp': jax.random.normal(ks[5], (M * HID, D), dtype=jnp.float32) * s, 'q_norm_w': jnp.ones((D,), dtype=jnp.float32), 'k_norm_w': jnp.ones((D,), dtype=jnp.float32), 'sink': jnp.zeros((H,), dtype=jnp.float32), 'Wg': jax.random.normal(ks[6], (G, H // G * D, INTER), dtype=jnp.float32) * s, 'Wo': jax.random.normal(ks[7], (G * INTER, HID), dtype=jnp.float32) * s}
    _L0_attn_in = _L0_attn_setup()

    def _L0_ffn_setup():
        import jax, jax.numpy as jnp
        import numpy as np
        DIM = 512
        HID = 1408
        ZERO_POINT = 128.0

        def _qlinear(x, wq, scale):
            W = (wq.astype(jnp.float32) - ZERO_POINT) * scale[:, None]
            return jnp.einsum('bsd,hd->bsh', x, W)
        key = jax.random.key(seed)
        ks = jax.random.split(key, 7)
        B, S = (4, 512)
        sg = jax.random.uniform(ks[1], (HID,)) * (0.02 / np.sqrt(DIM)) + 0.0001
        su = jax.random.uniform(ks[3], (HID,)) * (0.02 / np.sqrt(DIM)) + 0.0001
        sd = jax.random.uniform(ks[5], (DIM,)) * (0.02 / np.sqrt(HID)) + 0.0001
        return {'x': jax.random.normal(ks[0], (B, S, DIM), dtype=jnp.float32), 'wq_gate': jax.random.randint(ks[2], (HID, DIM), 0, 64, dtype=jnp.int32), 's_gate': sg, 'wq_up': jax.random.randint(ks[4], (HID, DIM), 0, 64, dtype=jnp.int32), 's_up': su, 'wq_down': jax.random.randint(ks[6], (DIM, HID), 0, 64, dtype=jnp.int32), 's_down': sd}
    _L0_ffn_in = _L0_ffn_setup()
    _L0_c = _w((lambda *s: np.random.randn(*s).astype(np.float32) * 0.05)(2, 512))
    _L0_wmod = _w((lambda *s: np.random.randn(*s).astype(np.float32) * 0.05)(512, 6 * 512) * 512 ** (-0.5))
    _d = {'L0_attn_h': _L0_attn_in['h'], 'L0_attn_Wq_c': _L0_attn_in['Wq_c'], 'L0_attn_Wq_up': _L0_attn_in['Wq_up'], 'L0_attn_Wk': _L0_attn_in['Wk'], 'L0_attn_Wv': _L0_attn_in['Wv'], 'L0_attn_W_comp': _L0_attn_in['W_comp'], 'L0_attn_q_norm_w': _L0_attn_in['q_norm_w'], 'L0_attn_k_norm_w': _L0_attn_in['k_norm_w'], 'L0_attn_sink': _L0_attn_in['sink'], 'L0_attn_Wg': _L0_attn_in['Wg'], 'L0_attn_Wo': _L0_attn_in['Wo'], 'L0_ffn_wq_gate': _L0_ffn_in['wq_gate'], 'L0_ffn_s_gate': _L0_ffn_in['s_gate'], 'L0_ffn_wq_up': _L0_ffn_in['wq_up'], 'L0_ffn_s_up': _L0_ffn_in['s_up'], 'L0_ffn_wq_down': _L0_ffn_in['wq_down'], 'L0_ffn_s_down': _L0_ffn_in['s_down'], 'L0_c': _L0_c, 'L0_wmod': _L0_wmod}
    _x0 = _d['L0_attn_h']
    _d['L0_attn_h'] = jax.random.normal(jax.random.fold_in(jax.random.key(seed), 1), (2, 1024, 512), dtype=_x0.dtype)
    del _x0
    return _d

def reference(L0_attn_h, L0_attn_Wq_c, L0_attn_Wq_up, L0_attn_Wk, L0_attn_Wv, L0_attn_W_comp, L0_attn_q_norm_w, L0_attn_k_norm_w, L0_attn_sink, L0_attn_Wg, L0_attn_Wo, L0_ffn_wq_gate, L0_ffn_s_gate, L0_ffn_wq_up, L0_ffn_s_up, L0_ffn_wq_down, L0_ffn_s_down, L0_c, L0_wmod):

    def _L0_attn_ref(h, Wq_c, Wq_up, Wk, Wv, W_comp, q_norm_w, k_norm_w, sink, Wg, Wo):
        import jax, jax.numpy as jnp
        import numpy as np
        H = 16
        D = 128
        M = 16
        ROPE = 64
        THETA = 10000.0
        WIN = 128
        CAP = 50.0
        G = 4
        HID = 512
        QC = 128
        INTER = 512

        def rope_cache(t):
            inv = 1.0 / THETA ** (jnp.arange(0, ROPE, 2, dtype=jnp.float32) / ROPE)
            ang = jnp.arange(t, dtype=jnp.float32)[:, None] * inv[None, :]
            return (jnp.cos(ang), jnp.sin(ang))

        def apply_partial_rope(x, cos, sin):
            x1 = x[..., :ROPE // 2]
            x2 = x[..., ROPE // 2:ROPE]
            rest = x[..., ROPE:]
            return jnp.concatenate([x1 * cos - x2 * sin, x1 * sin + x2 * cos, rest], axis=-1)

        def rmsnorm(x, w, eps=1e-06):
            return x * jax.lax.rsqrt(jnp.mean(x * x, axis=-1, keepdims=True) + eps) * w

        def attend(scores, mask, sink, v, sub):
            b, h, t, _ = scores.shape
            logits = jnp.where(mask, scores, jnp.float32(-1e+30))
            sink_col = jnp.broadcast_to(sink[None, :, None, None], (b, h, t, 1))
            probs = jax.nn.softmax(jnp.concatenate([logits, sink_col], axis=-1), axis=-1)[..., :-1]
            return jnp.einsum(sub, probs, v)
        b, t, _ = h.shape
        cos, sin = rope_cache(t)
        q = (h @ Wq_c @ Wq_up).reshape(b, t, H, D).transpose(0, 2, 1, 3)
        q = rmsnorm(apply_partial_rope(q, cos, sin), q_norm_w)
        k_sw = rmsnorm(apply_partial_rope(h @ Wk, cos, sin), k_norm_w)
        v_sw = h @ Wv
        nb = t // M
        ck = rmsnorm(h.reshape(b, nb, M * HID) @ W_comp, k_norm_w)
        scale = 1.0 / jnp.sqrt(jnp.float32(D))
        pos = jnp.arange(t)
        blk_end = jnp.arange(nb) * M + (M - 1)
        valid = blk_end[None, :] < pos[:, None]
        c_scores = jnp.einsum('bhtd,bnd->bhtn', q, ck) * scale
        c_out = attend(c_scores, valid[None, None], sink, ck, 'bhtn,bnd->bhtd')
        sw_scores = jnp.einsum('bhtd,bsd->bhts', q, k_sw) * scale
        sw_scores = CAP * jnp.tanh(sw_scores / CAP)
        sw_mask = (pos[None, :] <= pos[:, None]) & (pos[:, None] - pos[None, :] < WIN)
        sw_out = attend(sw_scores, sw_mask[None, None], sink, v_sw, 'bhts,bsd->bhtd')
        ao = (c_out + sw_out).transpose(0, 2, 1, 3).reshape(b, t, G, H // G * D)
        inter = jnp.einsum('btgf,gfi->btgi', ao, Wg)
        return inter.reshape(b, t, G * INTER) @ Wo

    def _L0_ffn_ref(x, wq_gate, s_gate, wq_up, s_up, wq_down, s_down):
        import jax, jax.numpy as jnp
        import numpy as np
        DIM = 512
        HID = 1408
        ZERO_POINT = 128.0

        def _qlinear(x, wq, scale):
            W = (wq.astype(jnp.float32) - ZERO_POINT) * scale[:, None]
            return jnp.einsum('bsd,hd->bsh', x, W)
        gate = _qlinear(x, wq_gate, s_gate)
        gate = jax.nn.silu(gate)
        up = _qlinear(x, wq_up, s_up)
        return _qlinear(gate * up, wq_down, s_down)
    x = L0_attn_h
    mod = (_silu(L0_c) @ L0_wmod).reshape(L0_c.shape[0], 6, 1, -1)
    sa, ca, ga, sb, cb, gb = (mod[:, 0], mod[:, 1], mod[:, 2], mod[:, 3], mod[:, 4], mod[:, 5])
    ga = (2 * (ga >= 0) - 1) * jnp.maximum(jnp.abs(ga), 0.25)
    gb = (2 * (gb >= 0) - 1) * jnp.maximum(jnp.abs(gb), 0.25)
    h = _layernorm(x, axis=-1) * (1 + ca) + sa
    x = x + ga * _L0_attn_ref(h, L0_attn_Wq_c, L0_attn_Wq_up, L0_attn_Wk, L0_attn_Wv, L0_attn_W_comp, L0_attn_q_norm_w, L0_attn_k_norm_w, L0_attn_sink, L0_attn_Wg, L0_attn_Wo)
    h = _layernorm(x, axis=-1) * (1 + cb) + sb
    x = x + gb * _L0_ffn_ref(h, L0_ffn_wq_gate, L0_ffn_s_gate, L0_ffn_wq_up, L0_ffn_s_up, L0_ffn_wq_down, L0_ffn_s_down)
    return x

_drawn_inputs = setup_inputs


def setup_inputs(seed=0):
    import zlib

    import numpy as np

    out = dict(_drawn_inputs(seed))
    spreads = {'L0_attn_q_norm_w': (1.0, 0.6), 'L0_attn_k_norm_w': (1.0, 0.6), 'L0_attn_sink': (0.0, 2.0)}
    factors = {'L0_attn_Wk': 8.0,
     'L0_attn_Wv': 7.146,
     'L0_ffn_s_gate': 8.0,
     'L0_ffn_s_up': 8.0,
     'L0_ffn_s_down': 8.0}
    for name, (base, spread) in spreads.items():
        noise = np.random.default_rng([zlib.crc32(name.encode()), seed]).standard_normal(out[name].shape)
        drawn = base * np.exp(spread * noise) if base else spread * noise
        out[name] = jnp.asarray(drawn.astype(out[name].dtype))
    for name, factor in factors.items():
        out[name] = (out[name] * factor).astype(out[name].dtype)
    return out
```

```python
from contextlib import ExitStack

import concourse.bass as bass
from concourse import mybir

F32 = mybir.dt.float32
F32R = mybir.dt.float32r
U32 = mybir.dt.uint32
I32 = mybir.dt.int32
ALU = mybir.AluOpType
ACT = mybir.ActivationFunctionType
AX = mybir.AxisListType

P = 128
BATCH, SEQ, C = 2, 1024, 512
KC = C // P
TILES = BATCH * SEQ // P
TPB = SEQ // P
CHUNK = 4
CHUNKS = TILES // CHUNK
W = CHUNK * P
H, D, M = 16, 128, 16
HALF = 32
NB = SEQ // M
HG = 4
GPT = H // HG
GROUPS = TILES * GPT
CAP = 50.0
SCALE = float(D) ** -0.5
INTER = 512
HID = 1408
HB = HID // P
ZERO_POINT = 128.0
LN_EPS, RMS_EPS = 1e-5, 1e-6

K_IDENT, K_LOW, K_UP, K_ROPE = 0, P, 2 * P, 3 * P
K_CMASK = K_ROPE + TPB * P
K_FIRST = K_CMASK + TPB * NB
K_PERSIST = K_FIRST + 2 * P
K_SUMSEL = K_PERSIST
K_ROWSEL = K_SUMSEL + HG * P
K_ALL = K_ROWSEL + HG * P


def since(value):
    return not isinstance(value, int) or value > 0


def build_program(nc, x_in, Wq_c, Wq_up, Wk, Wv, W_comp, q_w, k_w, sink, Wg, Wo,
                  wq_gate, s_gate, wq_up, s_up, wq_down, s_down, cond, wmod, table, out):
    with ExitStack() as whole:
        def sb(scope, name, shape, dt=F32):
            return scope.enter_context(nc.sbuf_tensor(name, shape, dt))

        bank = [whole.enter_context(nc.psum_tensor(f"bank{i}", [P, 512], F32)) for i in range(8)]
        x_mid = nc.dram_tensor("x_mid", [TILES * P, C], F32, kind="Internal").ap()
        x_tok = x_in.rearrange("b t c -> (b t) c")
        out_tok = out.rearrange("b t c -> (b t) c")

        kons = sb(whole, "kons", [P, K_PERSIST])
        ident = kons[:, K_IDENT:K_IDENT + P]
        low = kons[:, K_LOW:K_LOW + P]
        csil = sb(whole, "csil", [P, KC, BATCH])

        with ExitStack() as attn:
            qcT = sb(attn, "qcT", [P, TILES, P])
            kT = sb(attn, "kT", [P, BATCH * (TPB + 1), P])
            v32 = sb(attn, "v32", [P, BATCH * (TPB + 1), P])
            ckT = sb(attn, "ckT", [P, 2, BATCH * NB], F32R)
            ck_pad = sb(attn, "ck_pad", [P, BATCH, 2, 2, P], F32R)
            qw_col = sb(attn, "qw_col", [P, 1])
            sinkb = sb(attn, "sinkb", [P, H])
            sink_r = sb(attn, "sink_r", [P, GPT])
            sink_f = sb(attn, "sink_f", [P, GPT])
            sink_g = sb(attn, "sink_g", [P, GPT])

            with ExitStack() as scope:
                project_block(nc, scope, sb, bank, x_tok, Wq_c, Wk, Wv, W_comp, q_w, k_w, sink, cond,
                              wmod, table, kons, ident, csil, qcT, kT, v32, ckT, ck_pad,
                              qw_col, sinkb, sink_r, sink_f, sink_g)
            fold = sb(attn, "fold", [P, H, 2, C], F32R)
            ga = sb(attn, "ga", [P, BATCH, C])
            wup = sb(attn, "wup", [P, 2, H * D], F32R)
            sumsel = sb(attn, "sumsel", [P, HG, P], F32R)
            rowsel = sb(attn, "rowsel", [P, HG, P], F32R)
            with ExitStack() as scope:
                fold_block(nc, scope, sb, bank, Wg, Wo, wmod, Wq_up, table, csil, ident, fold, ga, wup, sumsel, rowsel)
            with ExitStack() as scope:
                attend_block(nc, scope, sb, bank, x_tok, x_mid, kons, ident, low, qcT, kT, v32, ckT, ck_pad,
                             wup, fold, sumsel, rowsel, qw_col, sinkb, sink_f, sink_g, ga)
        with ExitStack() as scope:
            wT = sb(scope, "wT", [P, HB, 2, 2, KC, P], F32R)
            wd = sb(scope, "wd", [P, HB, 2, C], F32R)
            sg = sb(scope, "sg", [P, 2, HB])
            row = sb(scope, "row", [P, BATCH, C])
            modT = sb(scope, "modT2", [P, 2 * KC, BATCH])
            with ExitStack() as first:
                ffn_prepare(nc, first, sb, bank, wq_gate, s_gate, wq_up, s_up, wq_down, s_down, wmod, ident,
                            csil, wT, wd, sg, row, modT)
            with ExitStack() as second:
                ffn_block(nc, second, sb, bank, x_mid, out_tok, ident, wT, wd, sg, row, modT)


def project_block(nc, scope, sb, bank, x_tok, Wq_c, Wk, Wv, W_comp, q_w, k_w, sink, cond, wmod, table,
                  kons, ident, csil, qcT, kT, v32, ckT, ck_pad, qw_col, sinkb, sink_r, sink_f, sink_g):
    sem = lambda name: scope.enter_context(nc.semaphore(name))
    KV = 2 * D
    RING = 4
    ccol = sb(scope, "ccol", [P, KC, BATCH])
    mod_w = sb(scope, "mod_w", [P, KC, C])
    modT = sb(scope, "modT", [P, 2 * KC, BATCH])
    raw_qc = sb(scope, "raw_qc", [P, KC, P])
    raw_kv = sb(scope, "raw_kv", [P, KC, KV])
    wqc = sb(scope, "wqc", [P, 2, KC, P], F32R)
    wkv = sb(scope, "wkv", [P, 2, KC, KV], F32R)
    xs = sb(scope, "xs", [P, 2, CHUNK, C])
    stats = sb(scope, "stats", [P, CHUNK, 6])
    meanvar = sb(scope, "meanvar", [P, CHUNK, 2])
    rstd = sb(scope, "rstd", [P, CHUNK, 1])
    minus_half = sb(scope, "minus_half", [P, CHUNK])
    hfull = sb(scope, "hfull", [P, KC, W])
    hT = sb(scope, "hT", [P, 2, KC, W], F32R)
    hcomp = sb(scope, "hcomp", [P, 2, KC, M, P], F32R)
    ksq = sb(scope, "ksq", [P, P])
    kss = sb(scope, "kss", [P, CHUNK])
    kr = sb(scope, "kr", [P, CHUNK])
    kn = sb(scope, "kn", [P, CHUNK, D])
    ropa = sb(scope, "ropa", [P, CHUNK, 2 * HALF])
    ropb = sb(scope, "ropb", [P, CHUNK, 2 * HALF])
    kw_col = sb(scope, "kw_col", [P, 1])
    kw_row = sb(scope, "kw_row", [P, D])
    comp_raw = sb(scope, "comp_raw", [P, RING, KC, D])
    comp_w = sb(scope, "comp_w", [P, RING, 2, KC, D], F32R)
    ck_raw = sb(scope, "ck_raw", [P, P])
    ck_nd = sb(scope, "ck_nd", [P, D])
    ck_dup = sb(scope, "ck_dup", [P, BATCH, 2, NB])
    ckT32 = sb(scope, "ckT32", [P, P])
    cs1 = sb(scope, "cs1", [P, 2])

    table_in, cond_in, w_in, mod_in, small_in = map(sem, (
        "table_in", "cond_in", "w_in", "mod_in", "small_in"))
    x_even, x_odd = sem("x_even"), sem("x_odd")
    comp_in = [sem(f"comp_in{r}") for r in range(RING)]
    zeroed, w_split, csil_done, mod_mm, mod_done = map(sem, (
        "zeroed", "w_split", "csil_done", "mod_mm", "mod_done"))
    sink_steps, stats_done, var_done, rstd_done, z_done, hT_mm, h_full, h_hi, h_lo, h_comp = map(sem, (
        "sink_steps", "stats_done", "var_done", "rstd_done", "z_done", "hT_mm", "h_full", "h_hi", "h_lo", "h_comp"))
    qc_mm, kv_mm, qc_out, v_out, k_sq, k_var, k_rs, k_scaled, k_rope1, k_rope, kT_mm, kT_out = map(sem, (
        "qc_mm", "kv_mm", "qc_out", "v_out", "k_sq", "k_var", "k_rs", "k_scaled", "k_rope1", "k_rope", "kT_mm", "kT_out"))
    comp_hi, comp_lo, comp_mm, ck_act, ck_pe, ck_dve, ck_pool = map(sem, (
        "comp_hi", "comp_lo", "comp_mm", "ck_act", "ck_pe", "ck_dve", "ck_pool"))
    block = scope.enter_context(nc.Block())

    shift_w = comp_raw[:].rearrange("p r k d -> p (r k d)").rearrange("p (k n) -> p k n", k=KC)
    comp_view = W_comp.rearrange("(m k p) d -> m p k d", m=M, p=P)

    @block.sync
    def _(sp):
        def load_x(c):
            slot = c % 2
            if c >= 2:
                sp.wait_ge(z_done, 4 * (c - 1))
                sp.wait_ge(hT_mm, c - 1)
            sp.dma_start(xs[:, slot], x_tok[c * W:(c + 1) * W, :].rearrange("(t p) c -> p t c", p=P)
                         ).then_inc((x_even, x_odd)[slot], 16)

        for b in range(BATCH):
            sp.dma_start(ccol[:, :, b], cond[b].rearrange("(k p) -> p k", p=P), allow_slow_non_contiguous=True
                         ).then_inc(cond_in, 16)
        load_x(0)
        for n, place in enumerate((shift_w, mod_w[:])):
            sp.dma_start(place, wmod[:, n * C:(n + 1) * C].rearrange("(k p) n -> p k n", p=P)).then_inc(mod_in, 16)
        load_x(1)
        for c in range(2, CHUNKS):
            load_x(c)
        sp.wait_ge(mod_mm, 1)
        for m in range(RING):
            sp.dma_start(comp_raw[:, m], comp_view[m]).then_inc(comp_in[m], 16)
        with sp.Fori(1, M // RING) as r:
            for s in range(RING):
                sp.wait_ge(comp_lo, RING * r + (s - RING + 1))
                sp.dma_start(comp_raw[:, s],
                             W_comp[bass.ds(r * (RING * C) + s * C, C), :].rearrange("(k p) d -> p k d", p=P)
                             ).then_inc(comp_in[s], 16)

    @block.scalar
    def _(act):
        act.dma_start(kons[:], table[:, 0:K_PERSIST]).then_inc(table_in, 16)
        act.dma_start(raw_qc[:], Wq_c.rearrange("(k p) n -> p k n", p=P)).then_inc(w_in, 16)
        act.dma_start(raw_kv[:, :, 0:D], Wk.rearrange("(k p) n -> p k n", p=P)).then_inc(w_in, 16)
        act.dma_start(raw_kv[:, :, D:KV], Wv.rearrange("(k p) n -> p k n", p=P)).then_inc(w_in, 16)
        act.dma_start(qw_col[:], q_w.rearrange("(p a) -> p a", a=1)).then_inc(small_in, 16)
        act.dma_start(kw_col[:], k_w.rearrange("(p a) -> p a", a=1)).then_inc(small_in, 16)
        act.dma_start(kw_row[:], k_w.partition_broadcast(P)).then_inc(small_in, 16)
        act.dma_start(sinkb[:], sink.partition_broadcast(P)).then_inc(small_in, 16)
        for h in range(HG):
            act.dma_start(sink_r[32 * h:32 * h + 32, :],
                          sink.rearrange("(g h) -> h g", h=HG)[h].partition_broadcast(32),
                          allow_slow_non_contiguous=True).then_inc(small_in, 16)

        act.wait_ge(cond_in, 16 * BATCH)
        act.activation(csil[:], ccol[:], ACT.Silu).then_inc(csil_done, 1)
        act.wait_ge(sink_steps, 2)
        act.activation(sink_f[:], sink_f[:], ACT.Exp, scale=-1.0).then_inc(sink_steps, 1)
        act.activation(sink_g[:], sink_g[:], ACT.Exp).then_inc(sink_steps, 1)
        act.wait_ge(mod_mm, 1)
        act.activation(modT[:, 0:KC], bank[7][:, 0:2 * KC].rearrange("p (k b) -> p k b", b=BATCH),
                       ACT.Copy).then_inc(mod_done, 1)
        act.activation(modT[:, KC:2 * KC], bank[7][:, 2 * KC:4 * KC].rearrange("p (k b) -> p k b", b=BATCH),
                       ACT.Identity, bias=1.0).then_inc(mod_done, 1)
        act.wait_ge(mod_done, 2)

        def chunk(c, b):
            act.wait_ge(hT_mm, c + 1)
            if since(c):
                act.wait_ge(h_lo, c)
            for k in range(KC):
                last = act.activation(hfull[:, k], bank[k][:], ACT.Identity,
                                      scale=modT[:, KC + k, b:b + 1], bias=modT[:, k, b:b + 1])
            last.then_inc(h_full, 1)
            act.wait_ge(qc_mm, c + 1)
            act.activation(qcT[:, bass.ds(c * CHUNK, CHUNK), :], bank[4][:].rearrange("p (t n) -> p t n", t=CHUNK),
                           ACT.Copy).then_inc(qc_out, 1)
            act.wait_ge(kv_mm, c + 1)
            for t in range(CHUNK):
                act.activation(ksq[:], bank[5 + t // 2][:, (t % 2) * KV:(t % 2) * KV + D], ACT.Square,
                               accum_out=kss[:, t:t + 1]).then_inc(k_sq, 1)
                act.wait_ge(k_sq, CHUNK * c + t + 1)
            for t in range(CHUNK):
                last = act.activation(v32[:, bass.ds(c * CHUNK + b + 1 + t, 1), :],
                                      bank[5 + t // 2][:, (t % 2) * KV + D:(t % 2 + 1) * KV].unsqueeze(1), ACT.Copy)
            last.then_inc(v_out, 1)
            act.wait_ge(kT_mm, c + 1)
            act.activation(kT[:, bass.ds(c * CHUNK + b + 1, CHUNK), :], bank[7][:].rearrange("p (t n) -> p t n", t=CHUNK),
                           ACT.Copy, scale=kw_col[:, 0:1]).then_inc(kT_out, 1)

        act.wait_ge(small_in, 16 * 8)
        act.wait_ge(zeroed, 3)
        for c in range(CHUNKS):
            chunk(c, c // (CHUNKS // BATCH))
        def comp(r):
            for s in range(RING):
                act.wait_ge(comp_in[s], 16 * r + 16)
                if since(r):
                    act.wait_ge(comp_mm, RING * r + (s - RING + 1))
                act.activation(comp_w[:, s, 0], comp_raw[:, s], ACT.Copy).then_inc(comp_hi, 1)
        comp(0)
        with act.Fori(1, M // RING) as r:
            comp(r)
        act.wait_ge(comp_mm, M)
        act.activation(ck_raw[:], bank[0][:, 0:P], ACT.Copy).then_inc(ck_act, 1)
        act.wait_ge(ck_pe, 1)
        act.activation(ksq[:], bank[1][:, 0:P], ACT.Square, accum_out=cs1[:, 0:1]).then_inc(ck_act, 1)
        act.wait_ge(ck_pe, 2)
        act.activation(ckT32[:], bank[2][:, 0:P], ACT.Copy).then_inc(ck_act, 1)
        act.wait_ge(ck_act, 3)
        act.activation(ckT[:, 0], ckT32[:], ACT.Copy).then_inc(ck_act, 1)
        for b in range(BATCH):
            for half in range(2):
                last = act.activation(ck_dup[:, b, half], ckT32[:, b * NB:(b + 1) * NB], ACT.Copy)
        last.then_inc(ck_act, 1)
        act.wait_ge(ck_pe, 3)
        for b in range(BATCH):
            for half in range(2):
                rows = slice(half * NB, (half + 1) * NB)
                last = act.activation(ck_pad[rows, b, half, 0], bank[3][rows, b * P:(b + 1) * P], ACT.Copy)
        last.then_inc(ck_act, 1)

    @block.vector
    def _(dve):
        dve.memset(kT[:, 0:BATCH * (TPB + 1):TPB + 1], 0.0).then_inc(zeroed, 1)
        dve.memset(v32[:, 0:BATCH * (TPB + 1):TPB + 1], 0.0).then_inc(zeroed, 1)
        dve.memset(ck_pad[:].bitcast(F32), 0.0).then_inc(zeroed, 1)
        dve.memset(minus_half[:], -0.5).then_inc(zeroed, 1)
        dve.wait_ge(w_in, 48)
        dve.tensor_copy(wqc[:, 0], raw_qc[:]).then_inc(w_split, 1)
        dve.tensor_copy(wkv[:, 0], raw_kv[:]).then_inc(w_split, 1)
        dve.wait_ge(w_split, 2)
        dve.tensor_tensor(wqc[:, 1], raw_qc[:], wqc[:, 0].bitcast(F32), ALU.subtract).then_inc(w_split, 1)
        dve.tensor_tensor(wkv[:, 1], raw_kv[:], wkv[:, 0].bitcast(F32), ALU.subtract).then_inc(w_split, 1)
        dve.wait_ge(small_in, 16 * 8)
        dve.tensor_scalar(sink_f[:], sink_r[:], 0.0, None, ALU.max).then_inc(sink_steps, 1)
        dve.wait_ge(sink_steps, 1)
        dve.tensor_tensor(sink_g[:], sink_r[:], sink_f[:], ALU.subtract).then_inc(sink_steps, 1)

        def chunk(c):
            slot = c % 2
            dve.wait_ge((x_even, x_odd)[slot], 16 * (c // 2 + 1))
            if since(c):
                dve.wait_ge(rstd_done, 2 * c)
            for t in range(CHUNK):
                dve.bn_stats(stats[:, t], xs[:, slot, t]).then_inc(stats_done, 1)
            for t in range(CHUNK):
                dve.wait_ge(stats_done, CHUNK * c + t + 1)
                dve.bn_aggr(meanvar[:, t], stats[:, t]).then_inc(var_done, 1)
            dve.wait_ge(var_done, CHUNK * (c + 1))
            dve.wait_ge(rstd_done, 2 * (c + 1))
            for t in range(CHUNK):
                dve.tensor_scalar(xs[:, slot, t], xs[:, slot, t], meanvar[:, t, 0:1], rstd[:, t, 0:1],
                                  ALU.subtract, ALU.mult).then_inc(z_done, 1)
            dve.wait_ge(h_hi, c + 1)
            if since(c):
                dve.wait_ge(kv_mm, c)
                dve.wait_ge(h_comp, c)
            dve.tensor_tensor(hT[:, 1], hfull[:], hT[:, 0].bitcast(F32), ALU.subtract).then_inc(h_lo, 1)
            dve.wait_ge(k_rs, 2 * (c + 1))
            dve.wait_ge(v_out, c + 1)
            if since(c):
                dve.wait_ge(kT_mm, c)
            for t in range(CHUNK):
                last = dve.tensor_scalar(kn[:, t], bank[5 + t // 2][:, (t % 2) * KV:(t % 2) * KV + D],
                                         kr[:, t:t + 1], None, ALU.mult)
            last.then_inc(k_scaled, 1)

        dve.wait_ge(zeroed, 4)
        for c in range(CHUNKS):
            chunk(c)

        def comp(r):
            for s in range(RING):
                dve.wait_ge(comp_hi, RING * r + (s + 1))
                dve.tensor_tensor(comp_w[:, s, 1], comp_raw[:, s], comp_w[:, s, 0].bitcast(F32),
                                  ALU.subtract).then_inc(comp_lo, 1)
        comp(0)
        with dve.Fori(1, M // RING) as r:
            comp(r)
        dve.wait_ge(ck_pool, 2)
        dve.tensor_scalar(ck_nd[:], bank[1][:, 0:P], cs1[:, 1:2], None, ALU.mult).then_inc(ck_dve, 1)
        dve.wait_ge(ck_dve, 1)
        dve.tensor_tensor(ck_nd[:], ck_nd[:], kw_row[:], ALU.mult).then_inc(ck_dve, 1)
        dve.wait_ge(ck_act, 4)
        dve.tensor_tensor(ckT[:, 1], ckT32[:], ckT[:, 0].bitcast(F32), ALU.subtract).then_inc(ck_dve, 1)
        dve.wait_ge(ck_act, 6)
        for b in range(BATCH):
            for half in range(2):
                rows = slice(half * NB, (half + 1) * NB)
                last = dve.tensor_tensor(ck_pad[rows, b, half, 1], bank[3][rows, b * P:(b + 1) * P],
                                         ck_pad[rows, b, half, 0].bitcast(F32), ALU.subtract)
        last.then_inc(ck_dve, 1)

    @block.gpsimd
    def _(pool):
        pool.wait_ge(zeroed, 4)
        pool.wait_ge(table_in, 16)

        def chunk(c):
            pool.wait_ge(var_done, CHUNK * (c + 1))
            if since(c):
                pool.wait_ge(z_done, CHUNK * c)
            pool.tensor_scalar(rstd[:, :, 0], meanvar[:, :, 1], 1.0, LN_EPS, ALU.mult, ALU.add).then_inc(rstd_done, 1)
            pool.wait_ge(rstd_done, 2 * c + 1)
            pool.tensor_tensor(rstd[:, :, 0], rstd[:, :, 0], minus_half[:], ALU.pow).then_inc(rstd_done, 1)
            pool.wait_ge(h_full, c + 1)
            if since(c):
                pool.wait_ge(kv_mm, c)
            pool.tensor_copy(hT[:, 0], hfull[:]).then_inc(h_hi, 1)
            pool.wait_ge(k_sq, CHUNK * (c + 1))
            if since(c):
                pool.wait_ge(k_scaled, c)
            pool.tensor_scalar(kr[:], kss[:], 1.0 / D, RMS_EPS, ALU.mult, ALU.add).then_inc(k_rs, 1)
            pool.wait_ge(k_rs, 2 * c + 1)
            pool.tensor_tensor(kr[:], kr[:], minus_half[:], ALU.pow).then_inc(k_rs, 1)
            pool.wait_ge(k_scaled, c + 1)
            tile0 = (c % (TPB // CHUNK)) * CHUNK
            rope = kons[:, K_ROPE + tile0 * P:K_ROPE + (tile0 + CHUNK) * P].rearrange("p (t n) -> p t n", n=P)
            pool.tensor_tensor(ropa[:], kn[:, :, 0:2 * HALF], rope[:, :, 0:2 * HALF], ALU.mult).then_inc(k_rope1, 1)
            pool.tensor_tensor(ropb[:, :, 0:HALF], kn[:, :, HALF:2 * HALF],
                               rope[:, :, 2 * HALF:3 * HALF], ALU.mult).then_inc(k_rope1, 1)
            pool.tensor_tensor(ropb[:, :, HALF:], kn[:, :, 0:HALF], rope[:, :, 3 * HALF:], ALU.mult).then_inc(k_rope1, 1)
            pool.wait_ge(k_rope1, 3 * c + 3)
            pool.tensor_tensor(kn[:, :, 0:2 * HALF], ropa[:], ropb[:], ALU.add).then_inc(k_rope, 1)
            pool.wait_ge(h_lo, c + 1)
            per = W // M
            for part in range(2):
                for k in range(KC):
                    last = pool.tensor_copy(hcomp[:, part, k, :, c * per:(c + 1) * per],
                                            hT[:, part, k].rearrange("p (n m) -> p m n", m=M).bitcast(F32))
            last.then_inc(h_comp, 1)

        for c in range(CHUNKS):
            chunk(c)
        pool.wait_ge(ck_act, 2)
        pool.tensor_scalar(cs1[:, 1:2], cs1[:, 0:1], 1.0 / D, RMS_EPS, ALU.mult, ALU.add).then_inc(ck_pool, 1)
        pool.wait_ge(ck_pool, 1)
        pool.tensor_tensor(cs1[:, 1:2], cs1[:, 1:2], minus_half[:, 0:1], ALU.pow).then_inc(ck_pool, 1)

    @block.tensor
    def _(pe):
        pe.wait_ge(mod_in, 32)
        pe.wait_ge(csil_done, 1)
        for n in range(2 * KC):
            for k in range(KC):
                cols = (shift_w, mod_w[:])[n // KC][:, k, (n % KC) * P:(n % KC + 1) * P]
                last = pe.matmul(bank[7][:, 2 * n:2 * n + 2], cols, csil[:, k],
                                 start=(k == 0), stop=(k == KC - 1))
        last.then_inc(mod_mm, 1)
        pe.wait_ge(table_in, 16)
        for c in range(CHUNKS):
            pe.wait_ge(z_done, CHUNK * (c + 1))
            if since(c):
                pe.wait_ge(h_full, c)
            for k in range(KC):
                for t in range(CHUNK):
                    last = pe.transpose(bank[k][:, t * P:(t + 1) * P], xs[:, c % 2, t, k * P:(k + 1) * P], ident)
            last.then_inc(hT_mm, 1)
            pe.wait_ge(h_lo, c + 1)
            pe.wait_ge(w_split, 4)
            if since(c):
                pe.wait_ge(qc_out, c)
            for k in range(KC):
                for n, (a, b) in enumerate(((0, 0), (0, 1), (1, 0))):
                    last = pe.matmul(bank[4][:], wqc[:, a, k], hT[:, b, k], start=(k == 0 and n == 0),
                                     stop=(k == KC - 1 and n == 2))
            last.then_inc(qc_mm, 1)
            if since(c):
                pe.wait_ge(k_scaled, c)
                pe.wait_ge(v_out, c)
            for t in range(CHUNK):
                for k in range(KC):
                    for n, (a, b) in enumerate(((0, 0), (0, 1), (1, 0))):
                        last = pe.matmul(bank[5 + t // 2][:, (t % 2) * KV:(t % 2 + 1) * KV],
                                         hT[:, a, k, t * P:(t + 1) * P], wkv[:, b, k],
                                         start=(k == 0 and n == 0), stop=(k == KC - 1 and n == 2))
            last.then_inc(kv_mm, 1)
            pe.wait_ge(k_rope, c + 1)
            if c == 0:
                pe.wait_ge(mod_done, 2)
            else:
                pe.wait_ge(kT_out, c)
            for t in range(CHUNK):
                last = pe.transpose(bank[7][:, t * P:(t + 1) * P], kn[:, t], ident)
            last.then_inc(kT_mm, 1)

        pe.wait_ge(h_comp, CHUNKS)
        pe.wait_ge(h_full, CHUNKS)

        def comp(r, first, final):
            for s in range(RING):
                pe.wait_ge(comp_lo, RING * r + (s + 1))
                for k in range(KC):
                    for n, (a, b) in enumerate(((0, 0), (0, 1), (1, 0))):
                        last = pe.matmul(bank[0][:, 0:P], comp_w[:, s, a, k],
                                         hcomp[:, b, k, bass.ds(r * RING + s, 1), :].rearrange("p m n -> p (m n)"),
                                         start=first and s == 0 and k == 0 and n == 0,
                                         stop=final and s == RING - 1 and k == KC - 1 and n == 2)
                last.then_inc(comp_mm, 1)
        comp(0, True, False)
        with pe.Fori(1, M // RING - 1) as r:
            comp(r, False, False)
        comp(M // RING - 1, False, True)
        pe.wait_ge(ck_act, 1)
        pe.transpose(bank[1][:, 0:P], ck_raw[:], ident).then_inc(ck_pe, 1)
        pe.wait_ge(ck_dve, 2)
        pe.transpose(bank[2][:, 0:P], ck_nd[:], ident).then_inc(ck_pe, 1)
        pe.wait_ge(ck_act, 5)
        for b in range(BATCH):
            last = pe.transpose(bank[3][:, b * P:(b + 1) * P], ck_dup[:, b].rearrange("p h n -> p (h n)"), ident)
        last.then_inc(ck_pe, 1)


def fold_block(nc, scope, sb, bank, Wg, Wo, wmod, Wq_up, table, csil, ident, fold, ga, wup, sumsel, rowsel):
    sem = lambda name: scope.enter_context(nc.semaphore(name))
    G = H // HG
    IK = INTER // P
    raw_g = sb(scope, "raw_g", [P, HG, INTER])
    raw_o = sb(scope, "raw_o", [P, IK, C])
    wgT = sb(scope, "wgT", [P, 2, IK, HG * D], F32R)
    wo = sb(scope, "wo", [P, 2, IK, C], F32R)
    mod_w = sb(scope, "mod_wa", [P, KC, C])
    raw_up = sb(scope, "raw_up", [P, H * D])
    selraw = sb(scope, "selraw", [P, 2 * HG * P])
    silu_rows = sb(scope, "silu_rows", [P, BATCH, KC, P])
    rows_done = sem("rows_done")
    sign = sb(scope, "sign_a", [P, C])
    mag = sb(scope, "mag_a", [P, C])
    g_in, o_in, m_in, gT_mm, gT_hi, gT_lo, o_hi, o_lo, f_mm, f_hi, f_lo, mod_mm, mod_step = map(sem, (
        "g_in", "o_in", "m_in", "gT_mm", "gT_hi", "gT_lo", "o_hi", "o_lo", "f_mm", "f_hi", "f_lo", "gmod_mm", "gmod_step"))
    up_in, sel_in, up_hi, up_lo = map(sem, ("up_in", "sel_in", "up_hi", "up_lo"))
    block = scope.enter_context(nc.Block())
    wg_rows = Wg.rearrange("g f i -> (g f) i")

    @block.sync
    def _(sp):
        def load(g):
            if since(g):
                sp.wait_ge(gT_mm, g)
            sp.dma_start(raw_g[:], wg_rows[bass.ds(g * (HG * D), HG * D), :].rearrange("(k p) i -> p k i", p=P)
                         ).then_inc(g_in, 16)
            if since(g):
                sp.wait_ge(o_lo, g)
            sp.dma_start(raw_o[:], Wo[bass.ds(g * INTER, INTER), :].rearrange("(k p) n -> p k n", p=P)).then_inc(o_in, 16)
        load(0)
        sp.dma_start(mod_w[:], wmod[:, 2 * C:3 * C].rearrange("(k p) n -> p k n", p=P)).then_inc(m_in, 16)
        with sp.Fori(1, G) as g:
            load(g)

    @block.tensor
    def _(pe):
        def group(g):
            pe.wait_ge(g_in, 16 * g + 16)
            if since(g):
                pe.wait_ge(gT_lo, g)
            for i in range(IK):
                for f in range(HG):
                    last = pe.transpose(bank[i][:, f * P:(f + 1) * P], raw_g[:, f, i * P:(i + 1) * P], ident)
            last.then_inc(gT_mm, 1)
            pe.wait_ge(gT_lo, g + 1)
            pe.wait_ge(o_lo, g + 1)
            if since(g):
                pe.wait_ge(f_lo, HG * g)
            for f in range(HG):
                for i in range(IK):
                    for n, (a, b) in enumerate(((0, 0), (0, 1), (1, 0))):
                        last = pe.matmul(bank[4 + f][:], wgT[:, a, i, f * P:(f + 1) * P], wo[:, b, i],
                                         start=(i == 0 and n == 0), stop=(i == IK - 1 and n == 2))
                last.then_inc(f_mm, 1)
        group(0)
        with pe.Fori(1, G) as g:
            group(g)
        pe.wait_ge(m_in, 16)
        pe.wait_ge(rows_done, 1)
        pe.wait_ge(gT_lo, G)
        for b in range(BATCH):
            for k in range(KC):
                last = pe.matmul(bank[b][:], silu_rows[:, b, k], mod_w[:, k], start=(k == 0), stop=(k == KC - 1))
        last.then_inc(mod_mm, 1)

    @block.scalar
    def _(act):
        def group(g):
            act.wait_ge(o_in, 16 * g + 16)
            if since(g):
                act.wait_ge(f_mm, HG * g)
            act.activation(wo[:, 0], raw_o[:], ACT.Copy).then_inc(o_hi, 1)
            act.wait_ge(gT_mm, g + 1)
            for i in range(IK):
                act.activation(wgT[:, 0, i], bank[i][:], ACT.Copy).then_inc(gT_hi, 1)
            for f in range(HG):
                act.wait_ge(f_mm, HG * g + (f + 1))
                act.activation(fold[:, bass.ds(g * HG + f, 1), 0].rearrange("p a n -> p (a n)"), bank[4 + f][:],
                               ACT.Copy).then_inc(f_hi, 1)
        repeat_rows(act, csil, silu_rows, rows_done)
        act.dma_start(raw_up[:], Wq_up).then_inc(up_in, 16)
        act.dma_start(selraw[:], table[:, K_SUMSEL:K_ALL]).then_inc(sel_in, 16)
        group(0)
        with act.Fori(1, G) as g:
            group(g)

    @block.vector
    def _(dve):
        def group(g):
            if since(g):
                dve.wait_ge(f_mm, HG * g)
            for i in range(IK):
                dve.wait_ge(gT_hi, IK * g + (i + 1))
                last = dve.tensor_tensor(wgT[:, 1, i], bank[i][:], wgT[:, 0, i].bitcast(F32), ALU.subtract)
            last.then_inc(gT_lo, 1)
            for f in range(HG):
                dve.wait_ge(f_hi, HG * g + (f + 1))
                at = bass.ds(g * HG + f, 1)
                dve.tensor_tensor(fold[:, at, 1].rearrange("p a n -> p (a n)"), bank[4 + f][:],
                                  fold[:, at, 0].rearrange("p a n -> p (a n)").bitcast(F32),
                                  ALU.subtract).then_inc(f_lo, 1)
        group(0)
        with dve.Fori(1, G) as g:
            group(g)
        dve.wait_ge(mod_mm, 1)
        gate_steps(dve, bank[0:2], sign[:], mag[:], ga, mod_step)

    @block.gpsimd
    def _(pool):
        def group(g):
            pool.wait_ge(o_hi, g + 1)
            pool.tensor_tensor(wo[:, 1], raw_o[:], wo[:, 0].bitcast(F32), ALU.subtract).then_inc(o_lo, 1)
        group(0)
        with pool.Fori(1, G) as g:
            group(g)
        pool.wait_ge(sel_in, 16)
        pool.tensor_copy(sumsel[:].rearrange("p h n -> p (h n)"), selraw[:, 0:HG * P])
        pool.tensor_copy(rowsel[:].rearrange("p h n -> p (h n)"), selraw[:, HG * P:])
        pool.wait_ge(up_in, 16)
        pool.tensor_copy(wup[:, 0], raw_up[:]).then_inc(up_hi, 1)
        pool.wait_ge(up_hi, 1)
        pool.tensor_tensor(wup[:, 1], raw_up[:], wup[:, 0].bitcast(F32), ALU.subtract).then_inc(up_lo, 1)


def repeat_rows(act, csil, silu_rows, done):
    for b in range(BATCH):
        last = act.activation(silu_rows[:, b], csil[:, :, b:b + 1].broadcast_to([P, KC, P]), ACT.Copy)
    last.then_inc(done, 1)


def gate_steps(dve, bank, sign, mag, gate, step):
    for b in range(BATCH):
        dve.tensor_scalar(sign, bank[b][:], 0.0, 2.0, ALU.is_ge, ALU.mult).then_inc(step, 1)
        dve.tensor_scalar(mag, bank[b][:], -1.0, None, ALU.mult).then_inc(step, 1)
        dve.wait_ge(step, 5 * b + 2)
        dve.tensor_scalar(sign, sign, -1.0, None, ALU.add).then_inc(step, 1)
        dve.scalar_tensor_tensor(mag, bank[b][:], 0.25, mag, ALU.max, ALU.max).then_inc(step, 1)
        dve.wait_ge(step, 5 * b + 4)
        dve.tensor_tensor(gate[:, b], sign, mag, ALU.mult).then_inc(step, 1)
        dve.wait_ge(step, 5 * b + 5)


def attend_block(nc, scope, sb, bank, x_tok, x_mid, kons, ident, low, qcT, kT, v32, ckT, ck_pad, wup, fold,
                 sumsel, rowsel, qw_col, sinkb, sink_f, sink_g, ga):
    sem = lambda name: scope.enter_context(nc.semaphore(name))
    WG = HG * P
    qc_st = sb(scope, "qc_st", [P, 2, 2, P], F32R)
    k_st = sb(scope, "k_st", [P, 2, 2, 2, P], F32R)
    v_st = sb(scope, "v_st", [P, 2, 2, 2, P], F32R)
    v_df = sb(scope, "v_df", [P, P])
    ck_st = sb(scope, "ck_st", [P, 2, 2, 2, P], F32R)
    sq = sb(scope, "sq", [P, HG, D])
    ss = sb(scope, "ss", [P, 2, HG])
    rq = sb(scope, "rq", [P, 2, HG])
    exponent = sb(scope, "exponent", [P, HG])
    spare = {nc.vector: sb(scope, "spare_dve", [P, 64]), nc.gpsimd: sb(scope, "spare_pool", [P, 128])}
    settled = {nc.vector: 0, nc.gpsimd: 0}
    qn = sb(scope, "qn", [P, 2, HG, D])
    ropb = sb(scope, "ropb2", [P, HG, 2 * HALF])
    qT = sb(scope, "qT", [P, 2, 2, WG], F32R)
    prob = sb(scope, "prob", [P, 2, WG])
    ph = sb(scope, "ph", [P, 2, 2, WG], F32R)
    pm = sb(scope, "pm", [P, 2, 2, WG], F32R)
    cs = sb(scope, "cs", [P, 2, HG, NB + 1])
    cmx = sb(scope, "cmx", [P, 2, HG])
    crs = sb(scope, "crs", [P, 2, HG])
    pc = sb(scope, "pc", [P, 2, HG * NB])
    pcT = sb(scope, "pcT", [P, 2, 2, 2 * P], F32R)
    o_sb = sb(scope, "o_sb", [P, 2, WG])
    ao = sb(scope, "ao", [P, WG])
    aoT = sb(scope, "aoT", [P, 2, 2, WG], F32R)
    den = sb(scope, "den", [P, P])
    rden = sb(scope, "rden", [P, 2, P], F32R)
    x_t = sb(scope, "x_t", [P, 2, C])
    y_t = sb(scope, "y_t", [P, C])

    names = ("q_mm q_sq q_ss q_ms q_rs q_sc q_r1 q_rope qT_mm qT_hi qT_lo "
             "st_q st_k st_v st_c sp_a sp_b sc_mm cc_mm merged tanhed exped first p_hi p_lo pm_hi pm_lo "
             "c_sink c_log c_max c_sub c_exp c_sum c_rec c_nrm cT_mm cT_hi cT_lo "
             "pv_mm sm_mm o_out d_st rb_mm cv_mm ao1 ao2 ao_hi ao_lo wp_mm y_st x_done x_in0 x_in1 x_out0 x_out1 expo").split()
    s = {n: sem("a_" + n) for n in names}
    block = scope.enter_context(nc.Block())

    Q, T, SD, SPV, CC, O, RB, Y = bank
    STEP_Q, STEP_T, STEP_S, STEP_V, STEP_C, STEP_W = 0, 2, 3, 4, 5, 6
    UNROLL = 2 * GPT
    PROLOGUE = 1
    DEPTH = STEP_W

    class At:

        def __init__(self, m, r, lag):
            self.m, self.c = m, r - lag
            self.slot, self.j = self.c % 2, self.c % GPT
            self.tile_slot = (self.c // GPT) % 2
            if isinstance(m, int):
                self.group = m * UNROLL + self.c
            self.is_static = isinstance(m, int)

        def live(self):
            return not self.is_static or 0 <= self.group < GROUPS

        def n(self, back=0, per=1):
            return self.m * (UNROLL * per) + (self.c + 1 - back) * per

        def tile(self):
            return self.m * (UNROLL // GPT) + self.c // GPT

        def tiles(self, back=0):
            return self.tile() + (1 - back)

    def steps(engine, step):
        for m in range(PROLOGUE):
            for r in range(UNROLL):
                step(m, r)
        with engine.Fori(PROLOGUE, GROUPS // UNROLL) as m:
            for r in range(UNROLL):
                step(m, r)
        for r in range(DEPTH):
            step(GROUPS // UNROLL, r)

    def wait(engine, name, count):
        if since(count):
            engine.wait_ge(s[name], count)

    def settle(engine):
        room = spare[engine]
        settled[engine] = (settled[engine] + 1) % room.shape[1]
        engine.tensor_tensor(room[:, settled[engine]:settled[engine] + 1], low[:, 0:1], low[:, 0:1], ALU.mult)

    @block.tensor
    def _(pe):
        def three(out, pairs, start=True, stop=True):
            n = len(pairs)
            for q, (lhs, rhs) in enumerate(pairs):
                for u, (a, b) in enumerate(((0, 0), (0, 1), (1, 0))):
                    last = pe.matmul(out, lhs[a], rhs[b], start=start and q == 0 and u == 0,
                                     stop=stop and q == n - 1 and u == 2)
            return last

        def step(m, r):
            g = At(m, r, STEP_C)
            if g.live():
                wait(pe, "d_st", g.n(per=4))
                for h in range(HG):
                    for part in range(2):
                        last = pe.matmul(RB[:, h * P:(h + 1) * P], rowsel[:, h], rden[:, part],
                                         start=(part == 0), stop=(part == 1))
                last.then_inc(s["rb_mm"], 1)
            g = At(m, r, STEP_S)
            if g.live():
                wait(pe, "qT_lo", g.n())
                wait(pe, "st_k", (g.tiles()) * 2)
                wait(pe, "tanhed", g.n(1))
                ks = k_st[:, g.tile_slot]
                three(SPV[:], [((ks[:, 0, 0], ks[:, 1, 0]), (qT[:, g.slot, 0], qT[:, g.slot, 1]))])
                three(SD[:], [((ks[:, 0, 1], ks[:, 1, 1]), (qT[:, g.slot, 0], qT[:, g.slot, 1]))]
                      ).then_inc(s["sc_mm"], 1)
            g = At(m, r, STEP_C)
            if g.live():
                wait(pe, "cT_lo", g.n())
                wait(pe, "st_c", g.tiles())
                wait(pe, "o_out", g.n())
                cp = ck_st[:, g.tile_slot]
                for h in range(HG):
                    pair = slice((h // 2) * P, (h // 2 + 1) * P)
                    last = three(O[:, h * P:(h + 1) * P],
                                 [((cp[:, h % 2, 0], cp[:, h % 2, 1]),
                                   (pcT[:, g.slot, 0, pair], pcT[:, g.slot, 1, pair]))])
                last.then_inc(s["cv_mm"], 1)
            g = At(m, r, STEP_T)
            if g.live():
                wait(pe, "q_rope", g.n())
                wait(pe, "qT_lo", g.n(1))
                for h in range(HG):
                    last = pe.transpose(T[:, h * P:(h + 1) * P], qn[:, g.slot, h], ident)
                last.then_inc(s["qT_mm"], 1)
            g = At(m, r, STEP_S)
            if g.live():
                wait(pe, "c_log", g.n(1))
                wait(pe, "cT_lo", g.n(2))
                batch = g.tile() // TPB
                ckr = [ckT[:, part, bass.ds(batch * NB, NB)] for part in range(2)]
                for h in range(HG):
                    lhs = [qT[:, g.slot, part, h * P:(h + 1) * P] for part in range(2)]
                    last = three(CC[:, h * NB:(h + 1) * NB], [(lhs, ckr)])
                last.then_inc(s["cc_mm"], 1)
            g = At(m, r, STEP_Q)
            if g.live():
                wait(pe, "st_q", g.tiles() * 2)
                wait(pe, "q_sc", g.n(1))
                cols = slice(g.j * WG, (g.j + 1) * WG)
                three(Q[:], [((qc_st[:, g.tile_slot, 0], qc_st[:, g.tile_slot, 1]), (wup[:, 0, cols], wup[:, 1, cols]))]
                      ).then_inc(s["q_mm"], 1)
            g = At(m, r, STEP_V)
            if g.live():
                wait(pe, "st_v", g.tiles() * 5)
                wait(pe, "pm_lo", g.n())
                wait(pe, "p_lo", g.n())
                wait(pe, "pm_hi", g.n())
                wait(pe, "ao2", g.n(1))
                vs = v_st[:, g.tile_slot]
                three(O[:], [((vs[:, 0, 0], vs[:, 0, 1]), (ph[:, g.slot, 0], ph[:, g.slot, 1])),
                             ((vs[:, 1, 0], vs[:, 1, 1]), (pm[:, g.slot, 0], pm[:, g.slot, 1]))]
                      ).then_inc(s["pv_mm"], 1)
                wait(pe, "ao1", g.n(1))
                for h in range(HG):
                    for part in range(2):
                        last = pe.matmul(RB[:, 0:P], sumsel[:, h], ph[:, g.slot, part, h * P:(h + 1) * P],
                                         start=(h == 0 and part == 0), stop=(h == HG - 1 and part == 1))
                last.then_inc(s["sm_mm"], 1)
                wait(pe, "c_nrm", g.n())
                wait(pe, "c_log", At(m, r, STEP_S).n() if At(m, r, STEP_S).live() else 0)
                for q in range(2):
                    last = pe.transpose(CC[:, 2 * P + q * P:2 * P + (q + 1) * P], pc[:, g.slot, q * P:(q + 1) * P], ident)
                last.then_inc(s["cT_mm"], 1)
            g = At(m, r, STEP_W)
            if g.live():
                wait(pe, "ao_lo", g.n())
                if g.j == 0:
                    wait(pe, "y_st", g.tile())
                for h in range(HG):
                    head = g.j * HG + h
                    lhs = [aoT[:, g.slot, part, h * P:(h + 1) * P] for part in range(2)]
                    last = three(Y[:], [(lhs, (fold[:, head, 0], fold[:, head, 1]))],
                                 start=(g.j == 0 and h == 0), stop=(g.j == GPT - 1 and h == HG - 1))
                last.then_inc(s["wp_mm"], 1)
        steps(pe, step)

    @block.scalar
    def _(act):
        def step(m, r):
            g = At(m, r, STEP_Q)
            if g.live():
                wait(act, "q_mm", g.n())
                wait(act, "q_ss", g.n(1))
                act.activation(sq[:], Q[:].rearrange("p (h d) -> p h d", h=HG), ACT.Square).then_inc(s["q_sq"], 1)
            g = At(m, r, STEP_S)
            if g.live():
                wait(act, "merged", g.n())
                wait(act, "pm_lo", g.n(2))
                wait(act, "p_lo", g.n(2))
                act.activation(prob[:, g.slot], SD[:], ACT.Tanh, scale=SCALE / CAP).then_inc(s["tanhed"], 1)
                wait(act, "tanhed", g.n())
                act.activation(prob[:, g.slot], prob[:, g.slot], ACT.Exp, scale=CAP).then_inc(s["exped"], 1)
            g = At(m, r, STEP_T)
            if g.live():
                wait(act, "qT_mm", g.n())
                wait(act, "cc_mm", g.n(2))
                act.activation(qT[:, g.slot, 0], T[:], ACT.Copy, scale=qw_col[:, 0:1]).then_inc(s["qT_hi"], 1)
            g = At(m, r, STEP_S)
            if g.live():
                wait(act, "c_sub", g.n())
                act.activation(cs[:, g.slot], cs[:, g.slot], ACT.Exp).then_inc(s["c_exp"], 1)
                if g.tile_slot == 0:
                    wait(act, "first", g.tile() * (GPT // 2) + (g.j + 1))
                else:
                    wait(act, "exped", g.n())
                wait(act, "sm_mm", g.n(2))
                act.activation(ph[:, g.slot, 0], prob[:, g.slot], ACT.Copy).then_inc(s["p_hi"], 1)
            g = At(m, r, STEP_V)
            if g.live():
                wait(act, "pv_mm", g.n())
                wait(act, "ao1", g.n(2))
                act.activation(o_sb[:, g.slot], O[:], ACT.Copy).then_inc(s["o_out"], 1)
                wait(act, "cT_mm", g.n())
                wait(act, "cv_mm", g.n(2))
                act.activation(pcT[:, g.slot, 0], CC[:, 2 * P:], ACT.Copy).then_inc(s["cT_hi"], 1)
            g = At(m, r, STEP_C)
            if g.live():
                wait(act, "ao2", g.n())
                wait(act, "wp_mm", g.n(2))
                act.activation(aoT[:, g.slot, 0], ao[:], ACT.Copy).then_inc(s["ao_hi"], 1)
        steps(act, step)

    @block.vector
    def _(dve):
        dve.memset(exponent[:], -0.5).then_inc(s["expo"], 1)

        def step(m, r):
            g = At(m, r, STEP_C)
            if g.live():
                wait(dve, "rb_mm", g.n())
                wait(dve, "o_out", g.n())
                wait(dve, "ao_lo", g.n(1))
                dve.tensor_tensor(ao[:], o_sb[:, g.slot], RB[:], ALU.mult).then_inc(s["ao1"], 1)
                wait(dve, "cv_mm", g.n())
                wait(dve, "ao1", g.n())
                dve.tensor_tensor(ao[:], ao[:], O[:], ALU.add).then_inc(s["ao2"], 1)
            g = At(m, r, STEP_S)
            if g.live():
                wait(dve, "sc_mm", g.n())
                up = kons[:, K_UP:K_UP + P].bitcast(U32).unsqueeze(1).broadcast_to([P, HG, P])
                settle(dve)
                dve.copy_predicated(SD[:].rearrange("p (h n) -> p h n", h=HG), up,
                                    SPV[:].rearrange("p (h n) -> p h n", h=HG)).then_inc(s["merged"], 1)
            g = At(m, r, STEP_T)
            if g.live():
                wait(dve, "qT_hi", g.n())
                dve.scalar_tensor_tensor(qT[:, g.slot, 1], T[:], qw_col[:, 0:1], qT[:, g.slot, 0].bitcast(F32),
                                         ALU.mult, ALU.subtract).then_inc(s["qT_lo"], 1)
            g = At(m, r, STEP_S)
            if g.live():
                wait(dve, "cc_mm", g.n())
                wait(dve, "c_nrm", g.n(2))
                cm = kons[:, bass.ds(K_CMASK + (g.tile() % TPB) * NB, NB)].unsqueeze(1).broadcast_to([P, HG, NB])
                dve.scalar_tensor_tensor(cs[:, g.slot, :, 0:NB], CC[:, 0:2 * P].rearrange("p (h n) -> p h n", h=HG),
                                         SCALE, cm, ALU.mult, ALU.add).then_inc(s["c_log"], 1)
                wait(dve, "c_log", g.n())
                wait(dve, "c_sink", g.n())
                dve.tensor_reduce(cmx[:, g.slot], cs[:, g.slot], AX.X, ALU.max).then_inc(s["c_max"], 1)
                if g.tile_slot == 0:
                    wait(dve, "exped", g.n())
                    fm = kons[:, bass.ds(K_FIRST + (g.tile() % TPB + TPB - 1) // TPB * P, P)]
                    fm = fm.unsqueeze(1).broadcast_to([P, HG, P])
                    pr = prob[:, g.slot].rearrange("p (h n) -> p h n", h=HG)
                    dve.tensor_tensor(pr, pr, fm, ALU.mult).then_inc(s["first"], 1)
            g = At(m, r, STEP_Q)
            if g.live():
                wait(dve, "q_sq", g.n())
                wait(dve, "q_ms", g.n(2))
                dve.tensor_reduce(ss[:, g.slot], sq[:], AX.X, ALU.add).then_inc(s["q_ss"], 1)
            g = At(m, r, STEP_S)
            if g.live():
                wait(dve, "c_exp", g.n())
                dve.tensor_reduce(cmx[:, g.slot], cs[:, g.slot], AX.X, ALU.add).then_inc(s["c_sum"], 1)
                wait(dve, "c_sum", g.n())
                dve.reciprocal(crs[:, g.slot], cmx[:, g.slot]).then_inc(s["c_rec"], 1)
            g = At(m, r, STEP_V)
            if g.live():
                wait(dve, "sm_mm", g.n())
                wait(dve, "rb_mm", g.n(1))
                dve.tensor_scalar(den[:], RB[:, 0:P], sink_f[:, g.j:g.j + 1], sink_g[:, g.j:g.j + 1],
                                  ALU.mult, ALU.add).then_inc(s["d_st"], 1)
                wait(dve, "d_st", g.n(1, 4) + 1)
                dve.reciprocal(den[:], den[:]).then_inc(s["d_st"], 1)
                wait(dve, "d_st", g.n(1, 4) + 2)
                dve.tensor_scalar(rden[:, 0], den[:], sink_f[:, g.j:g.j + 1], None, ALU.mult).then_inc(s["d_st"], 1)
                wait(dve, "d_st", g.n(1, 4) + 3)
                dve.scalar_tensor_tensor(rden[:, 1], den[:], sink_f[:, g.j:g.j + 1], rden[:, 0].bitcast(F32),
                                         ALU.mult, ALU.subtract).then_inc(s["d_st"], 1)
            g = At(m, r, STEP_Q)
            if g.live():
                wait(dve, "q_rs", g.n())
                wait(dve, "qT_mm", g.n(2))
                dve.tensor_tensor(qn[:, g.slot], Q[:].rearrange("p (h d) -> p h d", h=HG),
                                  rq[:, g.slot].unsqueeze(2).broadcast_to([P, HG, D]), ALU.mult).then_inc(s["q_sc"], 1)
            g = At(m, r, STEP_V)
            if g.live():
                wait(dve, "cT_hi", g.n())
                dve.tensor_tensor(pcT[:, g.slot, 1], CC[:, 2 * P:], pcT[:, g.slot, 0].bitcast(F32),
                                  ALU.subtract).then_inc(s["cT_lo"], 1)
            g = At(m, r, STEP_C)
            if g.live():
                wait(dve, "ao_hi", g.n())
                wait(dve, "wp_mm", g.n(2))
                dve.tensor_tensor(aoT[:, g.slot, 1], ao[:], aoT[:, g.slot, 0].bitcast(F32),
                                  ALU.subtract).then_inc(s["ao_lo"], 1)
            g = At(m, r, STEP_S)
            if g.live():
                wait(dve, "p_lo", g.n())
                wait(dve, "pv_mm", g.n(2))
                dve.tensor_tensor(pm[:, g.slot, 1].rearrange("p (h n) -> p h n", h=HG),
                                  ph[:, g.slot, 1].bitcast(F32).rearrange("p (h n) -> p h n", h=HG),
                                  low.unsqueeze(1).broadcast_to([P, HG, P]), ALU.mult).then_inc(s["pm_lo"], 1)
            g = At(m, r, STEP_W)
            if g.live() and g.j == GPT - 1:
                slot = g.tile_slot
                wait(dve, "wp_mm", g.n())
                wait(dve, "x_done", g.tile())
                batch = g.tile() // TPB
                dve.tensor_tensor(y_t[:], Y[:], ga[:, bass.ds(batch, 1), :].rearrange("p b c -> p (b c)"),
                                  ALU.mult).then_inc(s["y_st"], 1)
                wait(dve, "y_st", g.tiles())
                wait(dve, f"x_in{slot}", (g.m + g.c // UNROLL) * 16 + 16)
                dve.tensor_tensor(x_t[:, slot], x_t[:, slot], y_t[:], ALU.add).then_inc(s["x_done"], 1)
        steps(dve, step)

    @block.gpsimd
    def _(pool):
        pool.wait_ge(s["expo"], 1)

        def stage_q(tile, slot):
            at = bass.ds(tile, 1)
            settle(pool)
            pool.tensor_copy(qc_st[:, slot, 0:1], qcT[:, at]).then_inc(s["st_q"], 1)
            pool.wait_ge(s["st_q"], tile * 2 + 1)
            settle(pool)
            pool.tensor_tensor(qc_st[:, slot, 1:2], qcT[:, at], qc_st[:, slot, 0:1].bitcast(F32),
                               ALU.subtract).then_inc(s["st_q"], 1)

        def stage_k(tile, slot):
            at = bass.ds(tile + tile // TPB, 2)
            settle(pool)
            pool.tensor_copy(k_st[:, slot, 0], kT[:, at]).then_inc(s["st_k"], 1)
            pool.wait_ge(s["st_k"], tile * 2 + 1)
            settle(pool)
            pool.tensor_tensor(k_st[:, slot, 1], kT[:, at], k_st[:, slot, 0].bitcast(F32),
                               ALU.subtract).then_inc(s["st_k"], 1)

        def stage_v(tile, slot):
            before, own = bass.ds(tile + tile // TPB, 1), bass.ds(tile + tile // TPB + 1, 1)
            settle(pool)
            pool.tensor_copy(v_st[:, slot, 0, 0:1], v32[:, before]).then_inc(s["st_v"], 1)
            pool.tensor_tensor(v_df[:].unsqueeze(1), v32[:, own], v32[:, before], ALU.subtract).then_inc(s["st_v"], 1)
            pool.wait_ge(s["st_v"], tile * 5 + 2)
            settle(pool)
            pool.tensor_tensor(v_st[:, slot, 0, 1:2], v32[:, before], v_st[:, slot, 0, 0:1].bitcast(F32),
                               ALU.subtract).then_inc(s["st_v"], 1)
            pool.tensor_copy(v_st[:, slot, 1, 0], v_df[:]).then_inc(s["st_v"], 1)
            pool.wait_ge(s["st_v"], tile * 5 + 4)
            pool.tensor_tensor(v_st[:, slot, 1, 1], v_df[:], v_st[:, slot, 1, 0].bitcast(F32),
                               ALU.subtract).then_inc(s["st_v"], 1)

        def step(m, r):
            g = At(m, r, STEP_Q)
            if g.live():
                if g.j == 0:
                    wait(pool, "q_mm", g.n(5))
                    stage_q(g.tile(), g.tile_slot)
                elif g.j == 1:
                    wait(pool, "cv_mm", g.n(6))
                    settle(pool)
                    pool.tensor_copy(ck_st[:, g.tile_slot], ck_pad[:, bass.ds(g.tile() // TPB, 1)].rearrange(
                        "p b r s d -> p (b r) s d").bitcast(F32)).then_inc(s["st_c"], 1)
                elif g.j == 2:
                    wait(pool, "sc_mm", g.n(7))
                    stage_k(g.tile(), g.tile_slot)
                else:
                    wait(pool, "pv_mm", g.n(8))
                    stage_v(g.tile(), g.tile_slot)
            g = At(m, r, STEP_S)
            if g.live():
                wait(pool, "c_exp", g.n(1))
                wait(pool, "c_sum", g.n(2))
                wait(pool, "c_nrm", g.n(2))
                settle(pool)
                pool.tensor_copy(cs[:, g.slot, :, NB], sinkb[:, g.j * HG:(g.j + 1) * HG]).then_inc(s["c_sink"], 1)
                wait(pool, "c_max", g.n())
                wait(pool, "c_sink", g.n())
                pool.tensor_tensor(cs[:, g.slot], cs[:, g.slot],
                                   cmx[:, g.slot].unsqueeze(2).broadcast_to([P, HG, NB + 1]),
                                   ALU.subtract).then_inc(s["c_sub"], 1)
                wait(pool, "p_hi", g.n())
                wait(pool, "pv_mm", g.n(2))
                pool.tensor_tensor(ph[:, g.slot, 1], prob[:, g.slot], ph[:, g.slot, 0].bitcast(F32),
                                   ALU.subtract).then_inc(s["p_lo"], 1)
                pool.tensor_tensor(pm[:, g.slot, 0].rearrange("p (h n) -> p h n", h=HG),
                                   ph[:, g.slot, 0].bitcast(F32).rearrange("p (h n) -> p h n", h=HG),
                                   low.unsqueeze(1).broadcast_to([P, HG, P]), ALU.mult).then_inc(s["pm_hi"], 1)
                wait(pool, "c_rec", g.n())
                wait(pool, "cT_mm", g.n(2))
                pool.tensor_tensor(pc[:, g.slot].rearrange("p (h n) -> p h n", h=HG), cs[:, g.slot, :, 0:NB],
                                   crs[:, g.slot].unsqueeze(2).broadcast_to([P, HG, NB]), ALU.mult
                                   ).then_inc(s["c_nrm"], 1)
            g = At(m, r, STEP_Q)
            if g.live():
                wait(pool, "q_ss", g.n())
                wait(pool, "q_sc", g.n(2))
                settle(pool)
                pool.tensor_scalar(rq[:, g.slot], ss[:, g.slot], 1.0 / D, RMS_EPS, ALU.mult, ALU.add
                                   ).then_inc(s["q_ms"], 1)
                wait(pool, "q_ms", g.n())
                pool.tensor_tensor(rq[:, g.slot], rq[:, g.slot], exponent[:], ALU.pow).then_inc(s["q_rs"], 1)
                wait(pool, "q_sc", g.n())
                wait(pool, "q_rope", g.n(1))
                rope = kons[:, bass.ds(K_ROPE + (g.tile() % TPB) * P, P)]
                over = lambda lo, n: rope[:, lo:lo + n].unsqueeze(1).broadcast_to([P, HG, n])
                x = qn[:, g.slot]
                settle(pool)
                pool.tensor_tensor(ropb[:, :, 0:HALF], x[:, :, HALF:2 * HALF], over(2 * HALF, HALF),
                                   ALU.mult).then_inc(s["q_r1"], 1)
                pool.tensor_tensor(ropb[:, :, HALF:], x[:, :, 0:HALF], over(3 * HALF, HALF),
                                   ALU.mult).then_inc(s["q_r1"], 1)
                wait(pool, "q_r1", g.n(1, 3) + 2)
                settle(pool)
                pool.tensor_tensor(x[:, :, 0:2 * HALF], x[:, :, 0:2 * HALF], over(0, 2 * HALF),
                                   ALU.mult).then_inc(s["q_r1"], 1)
                wait(pool, "q_r1", g.n(per=3))
                pool.tensor_tensor(x[:, :, 0:2 * HALF], x[:, :, 0:2 * HALF], ropb[:], ALU.add).then_inc(s["q_rope"], 1)

        steps(pool, step)

    @block.sync
    def _(sp):
        def load(tile, slot):
            sp.dma_start(x_t[:, slot], x_tok[bass.ds(tile * P, P), :]).then_inc(s[f"x_in{slot}"], 16)

        def store(tile, slot, nth):
            sp.wait_ge(s["x_done"], tile + 1)
            sp.dma_start(x_mid[bass.ds(tile * P, P), :], x_t[:, slot]).then_inc(s[f"x_out{slot}"], 16)
            return 16 * nth + 16

        load(0, 0)
        load(1, 1)
        with sp.Fori(0, TILES // 2 - 1) as n:
            for slot in range(2):
                done = store(2 * n + slot, slot, n)
                sp.wait_ge(s[f"x_out{slot}"], done)
                load(2 * n + (slot + 2), slot)
        for slot in range(2):
            done = store(TILES - 2 + slot, slot, TILES // 2 - 1)
            sp.wait_ge(s[f"x_out{slot}"], done)


def ffn_prepare(nc, scope, sb, bank, wq_gate, s_gate, wq_up, s_up, wq_down, s_down, wmod, ident, csil,
                wT, wd, sg, row, modT):
    sem = lambda name: scope.enter_context(nc.semaphore("f_" + name))
    raw_a = sb(scope, "raw_a", [P, HB * C], I32)
    raw_b = sb(scope, "raw_b", [P, HB * C], I32)
    conv_d = sb(scope, "conv_d", [P, HID])
    conv = conv_d[:, 0:2 * C].rearrange("p (w c) -> p w c", w=2)
    mod_w = sb(scope, "mod_w2", [P, KC, C])
    sign = sb(scope, "sign_b", [P, C])
    sdrow = sb(scope, "sdrow", [P, C])
    silu_rows = raw_b[:, 0:BATCH * KC * P].bitcast(F32).rearrange("p (b k n) -> p b k n", b=BATCH, k=KC)
    rows_done = sem("rows_done")
    CUT = (HB + 1) // 2
    gate_in = [sem("gate_in0"), sem("gate_in1")]
    up_in = [sem("up_in0"), sem("up_in1")]
    down_in, small_in, mod_in, conved, tr_mm, w_hi, w_lo, mod_mm, mod_out, row_st = map(sem, (
        "down_in", "small_in", "mod_in", "conved", "tr_mm", "w_hi", "w_lo", "mod_mm", "mod_out", "row_st"))
    block = scope.enter_context(nc.Block())
    rawg = raw_a[:].rearrange("p (h c) -> p h c", h=HB)
    rawu = raw_b[:].rearrange("p (h c) -> p h c", h=HB)
    rawd = raw_a[:].rearrange("p (o h) -> p o h", o=KC)
    gate_v = wq_gate.rearrange("(h p) c -> p h c", p=P)
    up_v = wq_up.rearrange("(h p) c -> p h c", p=P)

    @block.sync
    def _(sp):
        for q, part in enumerate((slice(0, CUT), slice(CUT, HB))):
            sp.dma_start(rawg[:, part], gate_v[:, part]).then_inc(gate_in[q], 16)
            sp.dma_start(rawu[:, part], up_v[:, part]).then_inc(up_in[q], 16)
        sp.wait_ge(conved, 2 * HB)
        sp.dma_start(rawd, wq_down.rearrange("(o p) h -> p o h", p=P)).then_inc(down_in, 16)

    @block.scalar
    def _(act):
        act.dma_start(mod_w[:], wmod[:, 3 * C:4 * C].rearrange("(k p) n -> p k n", p=P)).then_inc(mod_in, 16)
        act.dma_start(sg[:, 0], s_gate.rearrange("(h p) -> p h", p=P), allow_slow_non_contiguous=True).then_inc(small_in, 16)
        act.dma_start(sg[:, 1], s_up.rearrange("(h p) -> p h", p=P), allow_slow_non_contiguous=True).then_inc(small_in, 16)
        act.dma_start(sdrow[:], s_down.partition_broadcast(P)).then_inc(small_in, 16)
        for n in range(1, 3):
            act.wait_ge(mod_mm, n)
            act.dma_start(mod_w[:], wmod[:, (3 + n) * C:(4 + n) * C].rearrange("(k p) n -> p k n", p=P)
                          ).then_inc(mod_in, 16)
        act.activation(modT[:, 0:KC], bank[5][:, 0:2 * KC].rearrange("p (k b) -> p k b", b=BATCH),
                       ACT.Copy).then_inc(mod_out, 1)
        act.activation(modT[:, KC:2 * KC], bank[5][:, 2 * KC:4 * KC].rearrange("p (k b) -> p k b", b=BATCH),
                       ACT.Identity, bias=1.0).then_inc(mod_out, 1)

        def gate_up(h):
            for w in range(2):
                act.wait_ge(tr_mm, 2 * h + (w + 1))
                act.activation(wT[:, bass.ds(h, 1), w, 0].rearrange("p a k n -> p (a k) n"),
                               bank[w][:].rearrange("p (k n) -> p k n", k=KC), ACT.Copy).then_inc(w_hi, 1)
        with act.Fori(0, HB) as h:
            gate_up(h)
        act.wait_ge(conved, 2 * HB)
        repeat_rows(act, csil, silu_rows, rows_done)
        for o in range(KC):
            for n, lo in enumerate(range(0, HB, 4)):
                hi = min(lo + 4, HB)
                act.wait_ge(tr_mm, 2 * HB + 3 * o + n + 1)
                act.activation(wd[:, lo:hi, 0, o * P:(o + 1) * P],
                               bank[2 + n][:, 0:(hi - lo) * P].rearrange("p (h n) -> p h n", n=P),
                               ACT.Copy).then_inc(w_hi, 1)

    @block.vector
    def _(dve):
        def gate_up(h, q):
            dve.wait_ge(gate_in[q], 16)
            dve.wait_ge(up_in[q], 16)
            if since(h):
                dve.wait_ge(tr_mm, 2 * h)
            for w, raw in enumerate((rawg, rawu)):
                dve.tensor_scalar(conv[:, w:w + 1], raw[:, bass.ds(h, 1)], -ZERO_POINT, None,
                                  ALU.add).then_inc(conved, 1)
            for w in range(2):
                dve.wait_ge(w_hi, 2 * h + (w + 1))
                out = wT[:, bass.ds(h, 1), w].rearrange("p a s k n -> p (a s) k n")
                dve.tensor_tensor(out[:, 1], bank[w][:].rearrange("p (k n) -> p k n", k=KC),
                                  out[:, 0].bitcast(F32), ALU.subtract).then_inc(w_lo, 1)
        gate_up(0, 0)
        with dve.Fori(1, CUT) as h:
            gate_up(h, 0)
        with dve.Fori(CUT, HB) as h:
            gate_up(h, 1)
        dve.wait_ge(down_in, 16)
        for o in range(KC):
            dve.wait_ge(tr_mm, 2 * HB + 3 * o)
            dve.tensor_scalar(conv_d[:], rawd[:, o], -ZERO_POINT, None, ALU.add).then_inc(conved, 1)
            for n, lo in enumerate(range(0, HB, 4)):
                hi = min(lo + 4, HB)
                dve.wait_ge(w_hi, 2 * HB + 3 * o + n + 1)
                dve.tensor_tensor(wd[:, lo:hi, 1, o * P:(o + 1) * P],
                                  bank[2 + n][:, 0:(hi - lo) * P].rearrange("p (h n) -> p h n", n=P),
                                  wd[:, lo:hi, 0, o * P:(o + 1) * P].bitcast(F32), ALU.subtract).then_inc(w_lo, 1)
        dve.wait_ge(mod_mm, 3)
        gate_steps(dve, bank[6:8], sign[:], conv_d[:, 0:C], row, row_st)
        dve.wait_ge(small_in, 48)
        for b in range(BATCH):
            dve.tensor_tensor(row[:, b], row[:, b], sdrow[:], ALU.mult)

    @block.tensor
    def _(pe):
        for n in range(2):
            pe.wait_ge(mod_in, 16 * (n + 1))
            for q in range(KC):
                col = 2 * (n * KC + q)
                for k in range(KC):
                    last = pe.matmul(bank[5][:, col:col + 2], mod_w[:, k, q * P:(q + 1) * P], csil[:, k],
                                     start=(k == 0), stop=(k == KC - 1))
            last.then_inc(mod_mm, 1)

        def gate_up(h):
            for w in range(2):
                pe.wait_ge(conved, 2 * h + (w + 1))
                if since(h):
                    pe.wait_ge(w_lo, 2 * h + (w - 1))
                for k in range(KC):
                    last = pe.transpose(bank[w][:, k * P:(k + 1) * P], conv[:, w, k * P:(k + 1) * P], ident)
                last.then_inc(tr_mm, 1)
        gate_up(0)
        with pe.Fori(1, HB) as h:
            gate_up(h)
        pe.wait_ge(mod_in, 48)
        pe.wait_ge(rows_done, 1)
        for b in range(BATCH):
            for k in range(KC):
                last = pe.matmul(bank[6 + b][:], silu_rows[:, b, k], mod_w[:, k], start=(k == 0), stop=(k == KC - 1))
        last.then_inc(mod_mm, 1)
        for o in range(KC):
            pe.wait_ge(conved, 2 * HB + o + 1)
            for n, lo in enumerate(range(0, HB, 4)):
                if o:
                    pe.wait_ge(w_lo, 2 * HB + 3 * (o - 1) + n + 1)
                for h in range(lo, min(lo + 4, HB)):
                    last = pe.transpose(bank[2 + n][:, (h - lo) * P:(h - lo + 1) * P], conv_d[:, h * P:(h + 1) * P], ident)
                last.then_inc(tr_mm, 1)


def ffn_block(nc, scope, sb, bank, x_mid, out_tok, ident, wT, wd, sg, row, modT):
    sem = lambda name: scope.enter_context(nc.semaphore("g_" + name))
    xs = sb(scope, "xs2", [P, 2, CHUNK, C])
    z = sb(scope, "z2", [P, CHUNK, C])
    stats = sb(scope, "stats2", [P, CHUNK, 6])
    meanvar = sb(scope, "meanvar2", [P, CHUNK, 2])
    rstd = sb(scope, "rstd2", [P, CHUNK])
    minus_half = sb(scope, "minus_half2", [P, CHUNK])
    hT = sb(scope, "hT2", [P, 2, KC, W], F32R)
    sl = sb(scope, "sl", [P, 2, W])
    gu = sb(scope, "gu", [P, 2, W])
    sl2 = sb(scope, "sl2", [P, 2, W])
    gus = sb(scope, "gus", [P, 2, 2, W], F32R)
    x_in = [sem("x_in0"), sem("x_in1")]
    x_out = [sem("x_out0"), sem("x_out1")]
    init, stat, var, rs, z_done, tr_mm, h_hi, h_lo, gu_mm, silued, gued, gu_hi, gu_lo, dn_mm, y1, y2 = map(sem, (
        "init stat var rs z_done tr_mm h_hi h_lo gu_mm silued gued gu_hi gu_lo dn_mm y1 y2".split()))
    block = scope.enter_context(nc.Block())
    Y, GU = bank[0:4], bank[4:8]

    @block.sync
    def _(sp):
        for c in range(CHUNKS):
            slot = c % 2
            if c >= 2:
                sp.wait_ge(y2, CHUNK * (c - 1))
                sp.dma_start(out_tok[(c - 2) * W:(c - 1) * W, :].rearrange("(t p) c -> p t c", p=P), xs[:, slot]
                             ).then_inc(x_out[slot], 16)
                sp.wait_ge(x_out[slot], 16 * (c // 2))
            sp.dma_start(xs[:, slot], x_mid[c * W:(c + 1) * W, :].rearrange("(t p) c -> p t c", p=P)
                         ).then_inc(x_in[slot], 16)
        for c in range(CHUNKS - 2, CHUNKS):
            sp.wait_ge(y2, CHUNK * (c + 1))
            sp.dma_start(out_tok[c * W:(c + 1) * W, :].rearrange("(t p) c -> p t c", p=P), xs[:, c % 2]
                         ).then_inc(x_out[c % 2], 16)
            sp.wait_ge(x_out[c % 2], 16 * (CHUNKS // 2))

    @block.tensor
    def _(pe):
        def down(c, h):
            pe.wait_ge(gu_lo, HB * c + h + 1)
            for t in range(CHUNK):
                if h == 0 and c:
                    pe.wait_ge(y1, CHUNK * (c - 1) + t + 1)
                for n, (a, b) in enumerate(((0, 0), (0, 1), (1, 0))):
                    last = pe.matmul(Y[t][:], gus[:, h % 2, a, t * P:(t + 1) * P], wd[:, h, b],
                                     start=(h == 0 and n == 0), stop=(h == HB - 1 and n == 2))
            last.then_inc(dn_mm, 1)

        for c in range(CHUNKS):
            pe.wait_ge(z_done, CHUNK * (c + 1))
            if c:
                pe.wait_ge(gued, HB * c)
            for k in range(KC):
                for t in range(CHUNK):
                    last = pe.transpose(GU[k][:, t * P:(t + 1) * P], z[:, t, k * P:(k + 1) * P], ident)
            last.then_inc(tr_mm, 1)
            if c:
                down(c - 1, HB - 1)
            pe.wait_ge(h_lo, KC * (c + 1))
            for h in range(HB):
                if h >= 2:
                    pe.wait_ge(gued, HB * c + h - 1)
                for w in range(2):
                    for k in range(KC):
                        for n, (a, b) in enumerate(((0, 0), (0, 1), (1, 0))):
                            last = pe.matmul(GU[2 * (h % 2) + w][:], wT[:, h, w, a, k], hT[:, b, k],
                                             start=(k == 0 and n == 0), stop=(k == KC - 1 and n == 2))
                last.then_inc(gu_mm, 1)
                if h:
                    down(c, h - 1)
        down(CHUNKS - 1, HB - 1)

    @block.scalar
    def _(act):
        for c in range(CHUNKS):
            b = c // (CHUNKS // BATCH)
            act.wait_ge(tr_mm, c + 1)
            if c:
                act.wait_ge(gu_mm, HB * c)
                act.wait_ge(gu_lo, HB * c)
            for k in range(KC):
                act.activation(hT[:, 0, k], GU[k][:], ACT.Identity, scale=modT[:, KC + k, b:b + 1],
                               bias=modT[:, k, b:b + 1]).then_inc(h_hi, 1)
                act.activation(gu[:, 0] if k % 2 == 0 else gu[:, 1], GU[k][:], ACT.Identity,
                               scale=modT[:, KC + k, b:b + 1], bias=modT[:, k, b:b + 1]).then_inc(h_hi, 1)
                if k >= 1:
                    act.wait_ge(h_lo, KC * c + k)
            for h in range(HB):
                n = HB * c + h
                act.wait_ge(gu_mm, n + 1)
                if h >= 2 or c:
                    act.wait_ge(gued, n - 1)
                act.activation(sl[:, h % 2], GU[2 * (h % 2)][:], ACT.Silu, scale=sg[:, 0, h:h + 1]).then_inc(silued, 1)
                act.wait_ge(gued, n + 1)
                if n >= 2:
                    act.wait_ge(dn_mm, n - 1)
                act.activation(gus[:, h % 2, 0], gu[:, h % 2], ACT.Copy).then_inc(gu_hi, 1)

    @block.vector
    def _(dve):
        dve.memset(minus_half[:], -0.5).then_inc(init, 1)

        def normal(c):
            slot = c % 2
            dve.wait_ge(x_in[slot], 16 * (c // 2 + 1))
            if c:
                dve.wait_ge(rs, 2 * c)
            for t in range(CHUNK):
                dve.bn_stats(stats[:, t], xs[:, slot, t]).then_inc(stat, 1)
            for t in range(CHUNK):
                dve.wait_ge(stat, CHUNK * c + t + 1)
                dve.bn_aggr(meanvar[:, t], stats[:, t]).then_inc(var, 1)
            dve.wait_ge(var, CHUNK * (c + 1))
            dve.wait_ge(rs, 2 * (c + 1))
            if c:
                dve.wait_ge(tr_mm, c)
            for t in range(CHUNK):
                dve.tensor_scalar(z[:, t], xs[:, slot, t], meanvar[:, t, 0:1], rstd[:, t:t + 1],
                                  ALU.subtract, ALU.mult).then_inc(z_done, 1)

        normal(0)
        for c in range(CHUNKS):
            for k in range(KC):
                dve.wait_ge(h_hi, 2 * (KC * c + k) + 2)
                dve.tensor_tensor(hT[:, 1, k], gu[:, k % 2], hT[:, 0, k].bitcast(F32), ALU.subtract
                                  ).then_inc(h_lo, 1)
            if c == 0:
                dve.wait_ge(h_lo, KC)
            for h in range(HB):
                n = HB * c + h
                if h < 2:
                    dve.wait_ge(h_lo, KC * (c + 1))
                dve.wait_ge(silued, n + 1)
                if n >= 2:
                    dve.wait_ge(gu_lo, n - 1)
                dve.scalar_tensor_tensor(gu[:, h % 2], GU[2 * (h % 2) + 1][:], sg[:, 1, h:h + 1], sl[:, h % 2],
                                         ALU.mult, ALU.mult).then_inc(gued, 1)
                if h == HB // 2 and c + 1 < CHUNKS:
                    normal(c + 1)
            b = c // (CHUNKS // BATCH)
            dve.wait_ge(dn_mm, HB * (c + 1))
            for t in range(CHUNK):
                n = CHUNK * c + t
                if n >= 2:
                    dve.wait_ge(y2, n - 1)
                dve.tensor_tensor(sl2[:, t % 2], Y[t][:], row[:, b], ALU.mult).then_inc(y1, 1)
                dve.wait_ge(y1, n + 1)
                dve.tensor_tensor(xs[:, c % 2, t], xs[:, c % 2, t], sl2[:, t % 2], ALU.add).then_inc(y2, 1)

    @block.gpsimd
    def _(pool):
        pool.wait_ge(init, 1)

        def normal(c):
            pool.wait_ge(var, CHUNK * (c + 1))
            if c:
                pool.wait_ge(z_done, CHUNK * c)
            pool.tensor_scalar(rstd[:], meanvar[:, :, 1], 1.0, LN_EPS, ALU.mult, ALU.add).then_inc(rs, 1)
            pool.wait_ge(rs, 2 * c + 1)
            pool.tensor_tensor(rstd[:], rstd[:], minus_half[:], ALU.pow).then_inc(rs, 1)

        normal(0)
        for c in range(CHUNKS):
            for h in range(HB):
                n = HB * c + h
                pool.wait_ge(gu_hi, n + 1)
                if n >= 2:
                    pool.wait_ge(dn_mm, n - 1)
                pool.tensor_tensor(gus[:, h % 2, 1], gu[:, h % 2], gus[:, h % 2, 0].bitcast(F32), ALU.subtract
                                   ).then_inc(gu_lo, 1)
                if h == HB // 2 and c + 1 < CHUNKS:
                    normal(c + 1)


def _table(np):
    t = np.zeros((P, K_ALL), np.float32)
    i = np.arange(P)
    t[:, K_IDENT:K_IDENT + P] = np.eye(P)
    t[:, K_LOW:K_LOW + P] = i[:, None] <= i[None, :]
    t[:, K_UP:K_UP + P] = i[:, None] > i[None, :]
    inv = np.float32(1.0) / np.float32(10000.0) ** (np.arange(0, 2 * HALF, 2, dtype=np.float32) / np.float32(2 * HALF))
    ang = np.arange(SEQ, dtype=np.float32)[:, None] * inv[None, :].astype(np.float32)
    cos, sin = np.cos(ang), np.sin(ang)
    rope = np.concatenate([cos, cos, -sin, sin], axis=1).reshape(TPB, P, P)
    t[:, K_ROPE:K_CMASK] = rope.transpose(1, 0, 2).reshape(P, TPB * P)
    pos, end = np.arange(SEQ), np.arange(NB) * M + M - 1
    mask = np.where(end[None, :] < pos[:, None], 0.0, -1e30).reshape(TPB, P, NB)
    t[:, K_CMASK:K_FIRST] = mask.transpose(1, 0, 2).reshape(P, TPB * NB)
    t[:, K_FIRST:K_FIRST + 2 * P] = 1.0
    t[:, K_FIRST:K_FIRST + P] = t[:, K_LOW:K_LOW + P]
    for h in range(HG):
        t[:, K_SUMSEL + h * P + 32 * h:K_SUMSEL + h * P + 32 * h + 32] = 1.0
        t[32 * h, K_ROWSEL + h * P:K_ROWSEL + (h + 1) * P] = 1.0
    return t


_INS = ["L0_attn_h", "L0_attn_Wq_c", "L0_attn_Wq_up", "L0_attn_Wk", "L0_attn_Wv", "L0_attn_W_comp",
        "L0_attn_q_norm_w", "L0_attn_k_norm_w", "L0_attn_sink", "L0_attn_Wg", "L0_attn_Wo",
        "L0_ffn_wq_gate", "L0_ffn_s_gate", "L0_ffn_wq_up", "L0_ffn_s_up", "L0_ffn_wq_down", "L0_ffn_s_down",
        "L0_c", "L0_wmod"]


def kernel(**inputs):
    import numpy as np
    import concourse.bacc as bacc
    from concourse.bass_utils import run_bass_kernel_spmd

    nc = bacc.Bacc("TRN2", target_bir_lowering=False, num_devices=1)
    arrays, args = {}, []
    for name, a in [(n, np.ascontiguousarray(inputs[n])) for n in _INS] + [("table", _table(np))]:
        arrays[f"in_{name}"] = a
        args.append(nc.dram_tensor(f"in_{name}", a.shape, mybir.dt.from_np(a.dtype), kind="ExternalInput").ap())
    out = nc.dram_tensor("out", (BATCH, SEQ, C), F32, kind="ExternalOutput").ap()
    build_program(nc, *args, out)
    r = run_bass_kernel_spmd(nc, [arrays], core_ids=[0])
    return r.results[0]["out"]
```

```python
from contextlib import ExitStack

import concourse.bass as bass
from concourse import mybir

F32 = mybir.dt.float32
F32R = mybir.dt.float32r
U32 = mybir.dt.uint32
I32 = mybir.dt.int32
ALU = mybir.AluOpType
ACT = mybir.ActivationFunctionType
AX = mybir.AxisListType

P = 128
BATCH, SEQ, C = 2, 1024, 512
KC = C // P
TILES = BATCH * SEQ // P
TPB = SEQ // P
CHUNK = 4
CHUNKS = TILES // CHUNK
W = CHUNK * P
H, D, M = 16, 128, 16
HALF = 32
NB = SEQ // M
HG = 4
GPT = H // HG
GROUPS = TILES * GPT
UNROLL = 2 * GPT
CAP = 50.0
SCALE = float(D) ** -0.5
INTER = 512
HID = 1408
HB = HID // P
ZERO_POINT = 128.0
LN_EPS, RMS_EPS = 1e-5, 1e-6

K_IDENT, K_LOW, K_UP, K_ROPE = 0, P, 2 * P, 3 * P
K_CMASK = K_ROPE + TPB * P
K_PERSIST = K_CMASK + TPB * NB
K_SUMSEL = K_PERSIST
K_ROWSEL = K_SUMSEL + HG * P
K_ALL = K_ROWSEL + HG * P


def since(value):
    return not isinstance(value, int) or value > 0


def token_rows(x, tile):
    rows = x[bass.ds(tile * P, P), :] if not isinstance(tile, int) else x[tile * P:(tile + 1) * P, :]
    return rows.rearrange("(n m) c -> m n c", m=M)


def build_program(nc, x_in, Wq_c, Wq_up, Wk, Wv, W_comp, q_w, k_w, sink, Wg, Wo,
                  wq_gate, s_gate, wq_up, s_up, wq_down, s_down, cond, wmod, table, out):
    with ExitStack() as whole:
        def sb(scope, name, shape, dt=F32):
            return scope.enter_context(nc.sbuf_tensor(name, shape, dt))

        bank = [whole.enter_context(nc.psum_tensor(f"bank{i}", [P, 512], F32)) for i in range(8)]
        x_mid = nc.dram_tensor("x_mid", [TILES * P, C], F32, kind="Internal").ap()
        dram = lambda name, shape: nc.dram_tensor(name, shape, F32, kind="Internal").ap()
        q_parts = dram("q_parts", [TILES, P, 2, P])
        k_parts = dram("k_parts", [BATCH * (TPB + 1), P, 2, P])
        v_parts = dram("v_parts", [TILES, P, 4, P])
        ck_parts = dram("ck_parts", [BATCH, P, 4, P])
        x_tok = x_in.rearrange("b t c -> (b t) c")
        out_tok = out.rearrange("b t c -> (b t) c")

        kons = sb(whole, "kons", [P, K_PERSIST])
        ident = kons[:, K_IDENT:K_IDENT + P]
        low = kons[:, K_LOW:K_LOW + P]
        csil = sb(whole, "csil", [P, KC, BATCH])

        with ExitStack() as attn:
            ckT = sb(attn, "ckT", [P, BATCH * NB])
            qw_col = sb(attn, "qw_col", [P, 1])
            sinkb = sb(attn, "sinkb", [P, H])
            sink_r = sb(attn, "sink_r", [P, GPT])
            sink_f = sb(attn, "sink_f", [P, GPT])
            sink_g = sb(attn, "sink_g", [P, GPT])

            with ExitStack() as scope:
                project_block(nc, scope, sb, bank, x_tok, Wq_c, Wk, Wv, W_comp, q_w, k_w, sink, cond,
                              wmod, table, kons, ident, csil, q_parts, k_parts, v_parts, ck_parts, ckT,
                              qw_col, sinkb, sink_r, sink_f, sink_g)
            fold = sb(attn, "fold", [P, H, 2, C], F32R)
            ga = sb(attn, "ga", [P, BATCH, C])
            wup = sb(attn, "wup", [P, 2, H * D], F32R)
            sumsel = sb(attn, "sumsel", [P, HG, P], F32R)
            rowsel = sb(attn, "rowsel", [P, HG, P], F32R)
            with ExitStack() as scope:
                fold_block(nc, scope, sb, bank, Wg, Wo, wmod, Wq_up, table, csil, ident, fold, ga, wup, sumsel, rowsel)
            with ExitStack() as scope:
                attend_block(nc, scope, sb, bank, x_tok, x_mid, q_parts, k_parts, v_parts, ck_parts, table,
                             kons, ident, low, ckT, wup, fold, sumsel, rowsel, qw_col, sinkb, sink_f, sink_g, ga)
        with ExitStack() as scope:
            wT = sb(scope, "wT", [P, HB, 2, 2, KC, P], F32R)
            wd = sb(scope, "wd", [P, HB, 2, C], F32R)
            sg = sb(scope, "sg", [P, 2, HB])
            row = sb(scope, "row", [P, BATCH, C])
            modT = sb(scope, "modT2", [P, 2 * KC, BATCH])
            with ExitStack() as first:
                ffn_prepare(nc, first, sb, bank, wq_gate, s_gate, wq_up, s_up, wq_down, s_down, wmod, ident,
                            csil, wT, wd, sg, row, modT)
            with ExitStack() as second:
                ffn_block(nc, second, sb, bank, x_mid, out_tok, ident, wT, wd, sg, row, modT)


def semaphores(nc, scope, prefix=""):
    made = []

    def give_back():
        nc.clear_and_free_semaphores(made)
        nc.all_engine_barrier()
    scope.callback(give_back)

    def sem(name):
        made.append(nc.alloc_semaphore(prefix + name))
        return made[-1]
    return sem


def project_block(nc, scope, sb, bank, x_tok, Wq_c, Wk, Wv, W_comp, q_w, k_w, sink, cond, wmod, table,
                  kons, ident, csil, q_parts, k_parts, v_parts, ck_parts, ckT, qw_col, sinkb, sink_r, sink_f, sink_g):
    sem = semaphores(nc, scope)
    KV = 2 * D
    STORES = 3 * 16
    RING = 4
    ccol = sb(scope, "ccol", [P, KC, BATCH])
    mod_w = sb(scope, "mod_w", [P, KC, C])
    modT = sb(scope, "modT", [P, 2 * KC, BATCH])
    raw_qc = sb(scope, "raw_qc", [P, KC, P])
    raw_kv = sb(scope, "raw_kv", [P, KC, KV])
    wqc = sb(scope, "wqc", [P, 2, KC, P], F32R)
    wkv = sb(scope, "wkv", [P, 2, KC, KV], F32R)
    xs = sb(scope, "xs", [P, 2, CHUNK, C])
    stats = sb(scope, "stats", [P, CHUNK, 6])
    meanvar = sb(scope, "meanvar", [P, CHUNK, 2])
    rstd = sb(scope, "rstd", [P, CHUNK, 1])
    minus_half = sb(scope, "minus_half", [P, CHUNK])
    hfull = sb(scope, "hfull", [P, KC, W])
    hT = sb(scope, "hT", [P, 2, KC, TILES, P], F32R)
    ksq = sb(scope, "ksq", [P, P])
    kss = sb(scope, "kss", [P, CHUNK])
    kr = sb(scope, "kr", [P, CHUNK])
    kn = sb(scope, "kn", [P, 2, CHUNK, D])
    ropa = sb(scope, "ropa", [P, CHUNK, 2 * HALF])
    ropb = sb(scope, "ropb", [P, CHUNK, 2 * HALF])
    kw_col = sb(scope, "kw_col", [P, 1])
    kw_row = sb(scope, "kw_row", [P, D])
    comp_raw = sb(scope, "comp_raw", [P, RING, KC, D])
    comp_w = sb(scope, "comp_w", [P, RING, 2, KC, D], F32R)
    ck_raw = sb(scope, "ck_raw", [P, P])
    ck_nd = sb(scope, "ck_nd", [P, D])
    ck_dup = sb(scope, "ck_dup", [P, BATCH, 2, NB])
    cs1 = sb(scope, "cs1", [P, 2])
    q_out = sb(scope, "q_out", [P, CHUNK, 2, P], F32R)
    k_out = sb(scope, "k_out", [P, CHUNK, 2, P], F32R)
    v_out = sb(scope, "v_out", [P, CHUNK, 2, 2, P], F32R)
    v32 = sb(scope, "v32", [P, BATCH * (TPB + 1), P])
    v_less = sb(scope, "v_less", [P, CHUNK, P])
    zeros = sb(scope, "zeros", [P, 2, P], F32R)
    ck_pad = sb(scope, "ck_pad", [P, BATCH, 2, 2, P], F32R)

    table_in, cond_in, w_in, mod_in, small_in = map(sem, (
        "table_in", "cond_in", "w_in", "mod_in", "small_in"))
    x_even, x_odd = sem("x_even"), sem("x_odd")
    comp_in = [sem(f"comp_in{r}") for r in range(RING)]
    zeroed, w_split, csil_done, mod_mm, mod_done = map(sem, (
        "zeroed", "w_split", "csil_done", "mod_mm", "mod_done"))
    sink_steps, stats_done, var_done, rstd_done, z_done, hT_mm, h_full, h_hi, h_lo = map(sem, (
        "sink_steps", "stats_done", "var_done", "rstd_done", "z_done", "hT_mm", "h_full", "h_hi", "h_lo"))
    qc_mm, kv_mm, v_copied, k_sq, k_var, k_rs, k_scaled, k_rope1, k_rope, kT_mm = map(sem, (
        "qc_mm", "kv_mm", "v_copied", "k_sq", "k_var", "k_rs", "k_scaled", "k_rope1", "k_rope", "kT_mm"))
    q_hi, q_lo, k_hi, k_lo, v_hi, v_lo, v_diff, v_dhi, v_dlo, stored, zero_stored = map(sem, (
        "q_hi", "q_lo", "k_hi", "k_lo", "v_hi", "v_lo", "v_diff", "v_dhi", "v_dlo", "stored", "zero_stored"))
    comp_hi, comp_lo, comp_mm, ck_act, ck_pe, ck_dve, ck_pool = map(sem, (
        "comp_hi", "comp_lo", "comp_mm", "ck_act", "ck_pe", "ck_dve", "ck_pool"))
    block = scope.enter_context(nc.Block())

    shift_w = comp_raw[:].rearrange("p r k d -> p (r k d)").rearrange("p (k n) -> p k n", k=KC)
    comp_view = W_comp.rearrange("(m k p) d -> m p k d", m=M, p=P)

    @block.sync
    def _(sp):
        def load_x(c):
            slot = c % 2
            if c >= 2:
                sp.wait_ge(hT_mm, c - 1)
            for t in range(CHUNK):
                sp.dma_start(xs[:, slot, t], token_rows(x_tok, c * CHUNK + t)).then_inc((x_even, x_odd)[slot], 16)

        def store_parts(c, b):
            tiles = slice(c * CHUNK, (c + 1) * CHUNK)
            sp.wait_ge(q_lo, c + 1)
            sp.dma_start(q_parts[tiles].rearrange("t p a n -> p t a n"), q_out[:].bitcast(F32)).then_inc(stored, 16)
            sp.wait_ge(v_dlo, c + 1)
            sp.wait_ge(v_lo, c + 1)
            sp.dma_start(v_parts[tiles].rearrange("t p a n -> p t a n"), v_out[:].rearrange("p t a b n -> p t (a b) n").bitcast(F32)
                         ).then_inc(stored, 16)
            sp.wait_ge(k_lo, c + 1)
            sp.dma_start(k_parts[c * CHUNK + b + 1:(c + 1) * CHUNK + b + 1].rearrange("t p a n -> p t a n"), k_out[:].bitcast(F32)
                         ).then_inc(stored, 16)

        for b in range(BATCH):
            sp.dma_start(ccol[:, :, b], cond[b].rearrange("(k p) -> p k", p=P), allow_slow_non_contiguous=True
                         ).then_inc(cond_in, 16)
        load_x(0)
        for n, place in enumerate((shift_w, mod_w[:])):
            sp.dma_start(place, wmod[:, n * C:(n + 1) * C].rearrange("(k p) n -> p k n", p=P)).then_inc(mod_in, 16)
        load_x(1)
        sp.wait_ge(zeroed, 1)
        for b in range(BATCH):
            sp.dma_start(k_parts[b * (TPB + 1)], zeros[:].bitcast(F32)).then_inc(zero_stored, 16)
        sp.wait_ge(mod_mm, 1)
        for m in range(RING):
            sp.dma_start(comp_raw[:, m], comp_view[m]).then_inc(comp_in[m], 16)
        for c in range(2, CHUNKS):
            load_x(c)
            store_parts(c - 2, (c - 2) // (CHUNKS // BATCH))
        for c in range(CHUNKS - 2, CHUNKS):
            store_parts(c, c // (CHUNKS // BATCH))
        with sp.Fori(1, M // RING) as r:
            for s in range(RING):
                sp.wait_ge(comp_lo, RING * r + (s - RING + 1))
                sp.dma_start(comp_raw[:, s],
                             W_comp[bass.ds(r * (RING * C) + s * C, C), :].rearrange("(k p) d -> p k d", p=P)
                             ).then_inc(comp_in[s], 16)
        sp.wait_ge(ck_act, 5)
        sp.wait_ge(ck_dve, 3)
        sp.dma_start(ck_parts.rearrange("b p a n -> p b a n"), ck_pad[:].rearrange("p b h a n -> p b (h a) n").bitcast(F32)
                     ).then_inc(zero_stored, 16)
        sp.wait_ge(zero_stored, 16 * (BATCH + 1))
        sp.wait_ge(stored, STORES * CHUNKS)

    @block.scalar
    def _(act):
        act.dma_start(kons[:], table[:, 0:K_PERSIST]).then_inc(table_in, 16)
        act.dma_start(raw_qc[:], Wq_c.rearrange("(k p) n -> p k n", p=P)).then_inc(w_in, 16)
        act.dma_start(raw_kv[:, :, 0:D], Wk.rearrange("(k p) n -> p k n", p=P)).then_inc(w_in, 16)
        act.dma_start(raw_kv[:, :, D:KV], Wv.rearrange("(k p) n -> p k n", p=P)).then_inc(w_in, 16)
        act.dma_start(qw_col[:], q_w.rearrange("(p a) -> p a", a=1)).then_inc(small_in, 16)
        act.dma_start(kw_col[:], k_w.rearrange("(p a) -> p a", a=1)).then_inc(small_in, 16)
        act.dma_start(kw_row[:], k_w.partition_broadcast(P)).then_inc(small_in, 16)
        act.dma_start(sinkb[:], sink.partition_broadcast(P)).then_inc(small_in, 16)
        for h in range(HG):
            act.dma_start(sink_r[32 * h:32 * h + 32, :],
                          sink.rearrange("(g h) -> h g", h=HG)[h].partition_broadcast(32),
                          allow_slow_non_contiguous=True).then_inc(small_in, 16)

        act.wait_ge(cond_in, 16 * BATCH)
        act.activation(csil[:], ccol[:], ACT.Silu).then_inc(csil_done, 1)
        act.wait_ge(sink_steps, 2)
        act.activation(sink_f[:], sink_f[:], ACT.Exp, scale=-1.0).then_inc(sink_steps, 1)
        act.activation(sink_g[:], sink_g[:], ACT.Exp).then_inc(sink_steps, 1)
        act.wait_ge(mod_mm, 1)
        act.activation(modT[:, 0:KC], bank[7][:, 0:2 * KC].rearrange("p (k b) -> p k b", b=BATCH),
                       ACT.Copy).then_inc(mod_done, 1)
        act.activation(modT[:, KC:2 * KC], bank[7][:, 2 * KC:4 * KC].rearrange("p (k b) -> p k b", b=BATCH),
                       ACT.Identity, bias=1.0).then_inc(mod_done, 1)
        act.wait_ge(mod_done, 2)

        def channels(c, b):
            act.wait_ge(hT_mm, c + 1)
            if since(c):
                act.wait_ge(h_lo, c)
            for k in range(KC):
                last = act.activation(hfull[:, k], bank[k][:], ACT.Identity,
                                      scale=modT[:, KC + k, b:b + 1], bias=modT[:, k, b:b + 1])
            last.then_inc(h_full, 1)

        def query_key_value(c, b):
            act.wait_ge(qc_mm, c + 1)
            if since(c):
                act.wait_ge(stored, STORES * c)
            act.activation(q_out[:, :, 0], bank[4][:].rearrange("p (t n) -> p t n", t=CHUNK), ACT.Copy).then_inc(q_hi, 1)
            act.wait_ge(kv_mm, c + 1)
            if since(c):
                act.wait_ge(k_rs, 2 * c)
            for t in range(CHUNK):
                act.activation(ksq[:], bank[5 + t // 2][:, (t % 2) * KV:(t % 2) * KV + D], ACT.Square,
                               accum_out=kss[:, t:t + 1]).then_inc(k_sq, 1)
                act.wait_ge(k_sq, CHUNK * c + t + 1)
            for t in range(CHUNK):
                last = act.activation(v32[:, bass.ds(c * CHUNK + b + 1 + t, 1), :],
                                      bank[5 + t // 2][:, (t % 2) * KV + D:(t % 2 + 1) * KV].unsqueeze(1), ACT.Copy)
            last.then_inc(v_copied, 1)
            act.wait_ge(v_copied, c + 1)
            act.activation(v_out[:, :, 0, 0], v32[:, c * CHUNK + b:(c + 1) * CHUNK + b], ACT.Copy).then_inc(v_hi, 1)
            act.wait_ge(v_diff, c + 1)
            act.activation(v_out[:, :, 1, 0], v_less[:], ACT.Copy).then_inc(v_dhi, 1)

        def key(c):
            act.wait_ge(kT_mm, c + 1)
            act.activation(k_out[:, :, 0], bank[7][:].rearrange("p (t n) -> p t n", t=CHUNK),
                           ACT.Copy, scale=kw_col[:, 0:1]).then_inc(k_hi, 1)

        act.wait_ge(small_in, 16 * 8)
        act.wait_ge(zeroed, 3)
        for i in range(CHUNKS + 2):
            if i >= 2:
                key(i - 2)
            if i < CHUNKS:
                channels(i, i // (CHUNKS // BATCH))
            if 1 <= i <= CHUNKS:
                query_key_value(i - 1, (i - 1) // (CHUNKS // BATCH))
        def comp(r):
            for s in range(RING):
                act.wait_ge(comp_in[s], 16 * r + 16)
                if since(r):
                    act.wait_ge(comp_mm, RING * r + (s - RING + 1))
                act.activation(comp_w[:, s, 0], comp_raw[:, s], ACT.Copy).then_inc(comp_hi, 1)
        comp(0)
        with act.Fori(1, M // RING) as r:
            comp(r)
        act.wait_ge(comp_mm, M)
        act.activation(ck_raw[:], bank[0][:, 0:P], ACT.Copy).then_inc(ck_act, 1)
        act.wait_ge(ck_pe, 1)
        act.activation(ksq[:], bank[1][:, 0:P], ACT.Square, accum_out=cs1[:, 0:1]).then_inc(ck_act, 1)
        act.wait_ge(ck_pe, 2)
        act.activation(ckT[:], bank[2][:, 0:P], ACT.Copy).then_inc(ck_act, 1)
        act.wait_ge(ck_act, 3)
        for b in range(BATCH):
            for half in range(2):
                last = act.activation(ck_dup[:, b, half], ckT[:, b * NB:(b + 1) * NB], ACT.Copy)
        last.then_inc(ck_act, 1)
        act.wait_ge(ck_pe, 3)
        for b in range(BATCH):
            for half in range(2):
                rows = slice(half * NB, (half + 1) * NB)
                last = act.activation(ck_pad[rows, b, half, 0], bank[3][rows, b * P:(b + 1) * P], ACT.Copy)
        last.then_inc(ck_act, 1)

    @block.vector
    def _(dve):
        dve.memset(zeros[:].bitcast(F32), 0.0).then_inc(zeroed, 1)
        dve.memset(v32[:, 0:BATCH * (TPB + 1):TPB + 1], 0.0).then_inc(zeroed, 1)
        dve.memset(ck_pad[:].bitcast(F32), 0.0).then_inc(zeroed, 1)
        dve.memset(minus_half[:], -0.5).then_inc(zeroed, 1)
        dve.wait_ge(w_in, 48)
        dve.tensor_copy(wqc[:, 0], raw_qc[:]).then_inc(w_split, 1)
        dve.tensor_copy(wkv[:, 0], raw_kv[:]).then_inc(w_split, 1)
        dve.wait_ge(w_split, 2)
        dve.tensor_tensor(wqc[:, 1], raw_qc[:], wqc[:, 0].bitcast(F32), ALU.subtract).then_inc(w_split, 1)
        dve.tensor_tensor(wkv[:, 1], raw_kv[:], wkv[:, 0].bitcast(F32), ALU.subtract).then_inc(w_split, 1)
        dve.wait_ge(small_in, 16 * 8)
        dve.tensor_scalar(sink_f[:], sink_r[:], 0.0, None, ALU.max).then_inc(sink_steps, 1)
        dve.wait_ge(sink_steps, 1)
        dve.tensor_tensor(sink_g[:], sink_r[:], sink_f[:], ALU.subtract).then_inc(sink_steps, 1)

        def normal(c):
            slot = c % 2
            dve.wait_ge((x_even, x_odd)[slot], 16 * CHUNK * (c // 2 + 1))
            if since(c):
                dve.wait_ge(rstd_done, 2 * c)
            for t in range(CHUNK):
                dve.bn_stats(stats[:, t], xs[:, slot, t]).then_inc(stats_done, 1)
            for t in range(CHUNK):
                dve.wait_ge(stats_done, CHUNK * c + t + 1)
                dve.bn_aggr(meanvar[:, t], stats[:, t]).then_inc(var_done, 1)
            dve.wait_ge(var_done, CHUNK * (c + 1))
            dve.wait_ge(rstd_done, 2 * (c + 1))
            for t in range(CHUNK):
                dve.tensor_scalar(xs[:, slot, t], xs[:, slot, t], meanvar[:, t, 0:1], rstd[:, t, 0:1],
                                  ALU.subtract, ALU.mult).then_inc(z_done, 1)

        def channels_low(c):
            dve.wait_ge(h_hi, c + 1)
            dve.tensor_tensor(hT[:, 1, :, c * CHUNK:(c + 1) * CHUNK], hfull[:].rearrange("p k (t n) -> p k t n", n=P),
                              hT[:, 0, :, c * CHUNK:(c + 1) * CHUNK].bitcast(F32), ALU.subtract).then_inc(h_lo, 1)

        def query_key_value(c, b):
            dve.wait_ge(q_hi, c + 1)
            dve.tensor_tensor(q_out[:, :, 1], bank[4][:].rearrange("p (t n) -> p t n", t=CHUNK),
                              q_out[:, :, 0].bitcast(F32), ALU.subtract).then_inc(q_lo, 1)
            dve.wait_ge(k_rs, 2 * (c + 1))
            dve.wait_ge(v_copied, c + 1)
            if c >= 2:
                dve.wait_ge(kT_mm, c - 1)
            for t in range(CHUNK):
                last = dve.tensor_scalar(kn[:, c % 2, t], bank[5 + t // 2][:, (t % 2) * KV:(t % 2) * KV + D],
                                         kr[:, t:t + 1], None, ALU.mult)
            last.then_inc(k_scaled, 1)
            dve.wait_ge(v_hi, c + 1)
            dve.tensor_tensor(v_out[:, :, 0, 1], v32[:, c * CHUNK + b:(c + 1) * CHUNK + b],
                              v_out[:, :, 0, 0].bitcast(F32), ALU.subtract).then_inc(v_lo, 1)
            dve.wait_ge(v_dhi, c + 1)
            dve.tensor_tensor(v_out[:, :, 1, 1], v_less[:], v_out[:, :, 1, 0].bitcast(F32),
                              ALU.subtract).then_inc(v_dlo, 1)

        def key(c):
            dve.wait_ge(k_hi, c + 1)
            dve.scalar_tensor_tensor(k_out[:, :, 1], bank[7][:].rearrange("p (t n) -> p t n", t=CHUNK), kw_col[:, 0:1],
                                     k_out[:, :, 0].bitcast(F32), ALU.mult, ALU.subtract).then_inc(k_lo, 1)

        dve.wait_ge(zeroed, 4)
        normal(0)
        for i in range(CHUNKS + 2):
            if i >= 2:
                key(i - 2)
            if i + 1 < CHUNKS:
                normal(i + 1)
            if i < CHUNKS:
                channels_low(i)
            if 1 <= i <= CHUNKS:
                query_key_value(i - 1, (i - 1) // (CHUNKS // BATCH))

        def comp(r):
            for s in range(RING):
                dve.wait_ge(comp_hi, RING * r + (s + 1))
                dve.tensor_tensor(comp_w[:, s, 1], comp_raw[:, s], comp_w[:, s, 0].bitcast(F32),
                                  ALU.subtract).then_inc(comp_lo, 1)
        comp(0)
        with dve.Fori(1, M // RING) as r:
            comp(r)
        dve.wait_ge(ck_pool, 2)
        dve.tensor_scalar(ck_nd[:], bank[1][:, 0:P], cs1[:, 1:2], None, ALU.mult).then_inc(ck_dve, 1)
        dve.wait_ge(ck_dve, 1)
        dve.tensor_tensor(ck_nd[:], ck_nd[:], kw_row[:], ALU.mult).then_inc(ck_dve, 1)
        dve.wait_ge(ck_act, 5)
        for b in range(BATCH):
            for half in range(2):
                rows = slice(half * NB, (half + 1) * NB)
                last = dve.tensor_tensor(ck_pad[rows, b, half, 1], bank[3][rows, b * P:(b + 1) * P],
                                         ck_pad[rows, b, half, 0].bitcast(F32), ALU.subtract)
        last.then_inc(ck_dve, 1)

    @block.gpsimd
    def _(pool):
        pool.wait_ge(zeroed, 4)
        pool.wait_ge(table_in, 16)

        def inverse_deviation(c):
            pool.wait_ge(var_done, CHUNK * (c + 1))
            if since(c):
                pool.wait_ge(z_done, CHUNK * c)
            pool.tensor_scalar(rstd[:, :, 0], meanvar[:, :, 1], 1.0, LN_EPS, ALU.mult, ALU.add).then_inc(rstd_done, 1)
            pool.wait_ge(rstd_done, 2 * c + 1)
            pool.tensor_tensor(rstd[:, :, 0], rstd[:, :, 0], minus_half[:], ALU.pow).then_inc(rstd_done, 1)

        def channels_high(c):
            pool.wait_ge(h_full, c + 1)
            pool.tensor_copy(hT[:, 0, :, c * CHUNK:(c + 1) * CHUNK], hfull[:].rearrange("p k (t n) -> p k t n", n=P)
                             ).then_inc(h_hi, 1)

        def key_value(c, b):
            pool.wait_ge(k_sq, CHUNK * (c + 1))
            if since(c):
                pool.wait_ge(k_scaled, c)
            pool.tensor_scalar(kr[:], kss[:], 1.0 / D, RMS_EPS, ALU.mult, ALU.add).then_inc(k_rs, 1)
            pool.wait_ge(k_rs, 2 * c + 1)
            pool.tensor_tensor(kr[:], kr[:], minus_half[:], ALU.pow).then_inc(k_rs, 1)
            pool.wait_ge(v_copied, c + 1)
            if since(c):
                pool.wait_ge(v_dlo, c)
            pool.tensor_tensor(v_less[:], v32[:, c * CHUNK + b + 1:(c + 1) * CHUNK + b + 1],
                               v32[:, c * CHUNK + b:(c + 1) * CHUNK + b], ALU.subtract).then_inc(v_diff, 1)
            pool.wait_ge(k_scaled, c + 1)
            tile0 = (c % (TPB // CHUNK)) * CHUNK
            rope = kons[:, K_ROPE + tile0 * P:K_ROPE + (tile0 + CHUNK) * P].rearrange("p (t n) -> p t n", n=P)
            x = kn[:, c % 2]
            pool.tensor_tensor(ropa[:], x[:, :, 0:2 * HALF], rope[:, :, 0:2 * HALF], ALU.mult).then_inc(k_rope1, 1)
            pool.tensor_tensor(ropb[:, :, 0:HALF], x[:, :, HALF:2 * HALF],
                               rope[:, :, 2 * HALF:3 * HALF], ALU.mult).then_inc(k_rope1, 1)
            pool.tensor_tensor(ropb[:, :, HALF:], x[:, :, 0:HALF], rope[:, :, 3 * HALF:], ALU.mult).then_inc(k_rope1, 1)
            pool.wait_ge(k_rope1, 3 * c + 3)
            pool.tensor_tensor(x[:, :, 0:2 * HALF], ropa[:], ropb[:], ALU.add).then_inc(k_rope, 1)

        inverse_deviation(0)
        for i in range(CHUNKS + 1):
            if i + 1 < CHUNKS:
                inverse_deviation(i + 1)
            if i < CHUNKS:
                channels_high(i)
            if i >= 1:
                key_value(i - 1, (i - 1) // (CHUNKS // BATCH))
        pool.wait_ge(ck_act, 2)
        pool.tensor_scalar(cs1[:, 1:2], cs1[:, 0:1], 1.0 / D, RMS_EPS, ALU.mult, ALU.add).then_inc(ck_pool, 1)
        pool.wait_ge(ck_pool, 1)
        pool.tensor_tensor(cs1[:, 1:2], cs1[:, 1:2], minus_half[:, 0:1], ALU.pow).then_inc(ck_pool, 1)

    @block.tensor
    def _(pe):
        pe.wait_ge(mod_in, 32)
        pe.wait_ge(csil_done, 1)
        for n in range(2 * KC):
            for k in range(KC):
                cols = (shift_w, mod_w[:])[n // KC][:, k, (n % KC) * P:(n % KC + 1) * P]
                last = pe.matmul(bank[7][:, 2 * n:2 * n + 2], cols, csil[:, k],
                                 start=(k == 0), stop=(k == KC - 1))
        last.then_inc(mod_mm, 1)
        pe.wait_ge(table_in, 16)

        def transpose(c):
            pe.wait_ge(z_done, CHUNK * (c + 1))
            if since(c):
                pe.wait_ge(h_full, c)
            for k in range(KC):
                for t in range(CHUNK):
                    last = pe.transpose(bank[k][:, t * P:(t + 1) * P], xs[:, c % 2, t, k * P:(k + 1) * P], ident)
            last.then_inc(hT_mm, 1)

        def query_key_value(c):
            pe.wait_ge(h_lo, c + 1)
            pe.wait_ge(w_split, 4)
            if since(c):
                pe.wait_ge(q_lo, c)
            for k in range(KC):
                for n, (a, b) in enumerate(((0, 0), (0, 1), (1, 0))):
                    last = pe.matmul(bank[4][:], wqc[:, a, k],
                                     hT[:, b, k, c * CHUNK:(c + 1) * CHUNK].rearrange("p t n -> p (t n)"),
                                     start=(k == 0 and n == 0), stop=(k == KC - 1 and n == 2))
            last.then_inc(qc_mm, 1)
            if since(c):
                pe.wait_ge(k_scaled, c)
                pe.wait_ge(v_copied, c)
            for t in range(CHUNK):
                for k in range(KC):
                    for n, (a, b) in enumerate(((0, 0), (0, 1), (1, 0))):
                        last = pe.matmul(bank[5 + t // 2][:, (t % 2) * KV:(t % 2 + 1) * KV],
                                         hT[:, a, k, c * CHUNK + t], wkv[:, b, k],
                                         start=(k == 0 and n == 0), stop=(k == KC - 1 and n == 2))
            last.then_inc(kv_mm, 1)

        def key(c):
            pe.wait_ge(k_rope, c + 1)
            if c == 0:
                pe.wait_ge(mod_done, 2)
            else:
                pe.wait_ge(k_lo, c)
            for t in range(CHUNK):
                last = pe.transpose(bank[7][:, t * P:(t + 1) * P], kn[:, c % 2, t], ident)
            last.then_inc(kT_mm, 1)

        for i in range(CHUNKS + 2):
            if i < CHUNKS:
                transpose(i)
            if i >= 2:
                key(i - 2)
            if 1 <= i <= CHUNKS:
                query_key_value(i - 1)

        pe.wait_ge(h_lo, CHUNKS)
        PER = P // M

        def comp(r, first, final):
            for s in range(RING):
                pe.wait_ge(comp_lo, RING * r + (s + 1))
                for k in range(KC):
                    for n, (a, b) in enumerate(((0, 0), (0, 1), (1, 0))):
                        last = pe.matmul(bank[0][:, 0:P], comp_w[:, s, a, k],
                                         hT[:, b, k, :, bass.ds((r * RING + s) * PER, PER)],
                                         start=first and s == 0 and k == 0 and n == 0,
                                         stop=final and s == RING - 1 and k == KC - 1 and n == 2)
                last.then_inc(comp_mm, 1)
        comp(0, True, False)
        with pe.Fori(1, M // RING - 1) as r:
            comp(r, False, False)
        comp(M // RING - 1, False, True)
        pe.wait_ge(ck_act, 1)
        pe.transpose(bank[1][:, 0:P], ck_raw[:], ident).then_inc(ck_pe, 1)
        pe.wait_ge(ck_dve, 2)
        pe.transpose(bank[2][:, 0:P], ck_nd[:], ident).then_inc(ck_pe, 1)
        pe.wait_ge(ck_act, 4)
        for b in range(BATCH):
            last = pe.transpose(bank[3][:, b * P:(b + 1) * P], ck_dup[:, b].rearrange("p h n -> p (h n)"), ident)
        last.then_inc(ck_pe, 1)


def fold_block(nc, scope, sb, bank, Wg, Wo, wmod, Wq_up, table, csil, ident, fold, ga, wup, sumsel, rowsel):
    sem = semaphores(nc, scope)
    G = H // HG
    IK = INTER // P
    raw_g = sb(scope, "raw_g", [P, HG, INTER])
    raw_o = sb(scope, "raw_o", [P, IK, C])
    wgT = sb(scope, "wgT", [P, 2, IK, HG * D], F32R)
    wo = sb(scope, "wo", [P, 2, IK, C], F32R)
    mod_w = sb(scope, "mod_wa", [P, KC, C])
    raw_up = sb(scope, "raw_up", [P, H * D])
    selraw = sb(scope, "selraw", [P, 2 * HG * P])
    silu_rows = sb(scope, "silu_rows", [P, BATCH, KC, P])
    rows_done = sem("rows_done")
    sign = sb(scope, "sign_a", [P, C])
    mag = sb(scope, "mag_a", [P, C])
    g_in, o_in, m_in, gT_mm, gT_hi, gT_lo, o_hi, o_lo, f_mm, f_hi, f_lo, mod_mm, mod_step = map(sem, (
        "g_in", "o_in", "m_in", "gT_mm", "gT_hi", "gT_lo", "o_hi", "o_lo", "f_mm", "f_hi", "f_lo", "gmod_mm", "gmod_step"))
    up_in, sel_in, up_hi, up_lo = map(sem, ("up_in", "sel_in", "up_hi", "up_lo"))
    block = scope.enter_context(nc.Block())
    wg_rows = Wg.rearrange("g f i -> (g f) i")

    @block.sync
    def _(sp):
        def load(g):
            if since(g):
                sp.wait_ge(gT_mm, g)
            sp.dma_start(raw_g[:], wg_rows[bass.ds(g * (HG * D), HG * D), :].rearrange("(k p) i -> p k i", p=P)
                         ).then_inc(g_in, 16)
            if since(g):
                sp.wait_ge(o_lo, g)
            sp.dma_start(raw_o[:], Wo[bass.ds(g * INTER, INTER), :].rearrange("(k p) n -> p k n", p=P)).then_inc(o_in, 16)
        load(0)
        sp.dma_start(mod_w[:], wmod[:, 2 * C:3 * C].rearrange("(k p) n -> p k n", p=P)).then_inc(m_in, 16)
        with sp.Fori(1, G) as g:
            load(g)

    @block.tensor
    def _(pe):
        def group(g):
            pe.wait_ge(g_in, 16 * g + 16)
            if since(g):
                pe.wait_ge(gT_lo, g)
            for i in range(IK):
                for f in range(HG):
                    last = pe.transpose(bank[i][:, f * P:(f + 1) * P], raw_g[:, f, i * P:(i + 1) * P], ident)
            last.then_inc(gT_mm, 1)
            pe.wait_ge(gT_lo, g + 1)
            pe.wait_ge(o_lo, g + 1)
            if since(g):
                pe.wait_ge(f_lo, HG * g)
            for f in range(HG):
                for i in range(IK):
                    for n, (a, b) in enumerate(((0, 0), (0, 1), (1, 0))):
                        last = pe.matmul(bank[4 + f][:], wgT[:, a, i, f * P:(f + 1) * P], wo[:, b, i],
                                         start=(i == 0 and n == 0), stop=(i == IK - 1 and n == 2))
                last.then_inc(f_mm, 1)
        group(0)
        with pe.Fori(1, G) as g:
            group(g)
        pe.wait_ge(m_in, 16)
        pe.wait_ge(rows_done, 1)
        pe.wait_ge(gT_lo, G)
        for b in range(BATCH):
            for k in range(KC):
                last = pe.matmul(bank[b][:], silu_rows[:, b, k], mod_w[:, k], start=(k == 0), stop=(k == KC - 1))
        last.then_inc(mod_mm, 1)

    @block.scalar
    def _(act):
        def group(g):
            act.wait_ge(o_in, 16 * g + 16)
            if since(g):
                act.wait_ge(f_mm, HG * g)
            act.activation(wo[:, 0], raw_o[:], ACT.Copy).then_inc(o_hi, 1)
            act.wait_ge(gT_mm, g + 1)
            for i in range(IK):
                act.activation(wgT[:, 0, i], bank[i][:], ACT.Copy).then_inc(gT_hi, 1)
            for f in range(HG):
                act.wait_ge(f_mm, HG * g + (f + 1))
                act.activation(fold[:, bass.ds(g * HG + f, 1), 0].rearrange("p a n -> p (a n)"), bank[4 + f][:],
                               ACT.Copy).then_inc(f_hi, 1)
        repeat_rows(act, csil, silu_rows, rows_done)
        act.dma_start(raw_up[:], Wq_up).then_inc(up_in, 16)
        act.dma_start(selraw[:], table[:, K_SUMSEL:K_ALL]).then_inc(sel_in, 16)
        group(0)
        with act.Fori(1, G) as g:
            group(g)

    @block.vector
    def _(dve):
        def group(g):
            if since(g):
                dve.wait_ge(f_mm, HG * g)
            for i in range(IK):
                dve.wait_ge(gT_hi, IK * g + (i + 1))
                last = dve.tensor_tensor(wgT[:, 1, i], bank[i][:], wgT[:, 0, i].bitcast(F32), ALU.subtract)
            last.then_inc(gT_lo, 1)
            for f in range(HG):
                dve.wait_ge(f_hi, HG * g + (f + 1))
                at = bass.ds(g * HG + f, 1)
                dve.tensor_tensor(fold[:, at, 1].rearrange("p a n -> p (a n)"), bank[4 + f][:],
                                  fold[:, at, 0].rearrange("p a n -> p (a n)").bitcast(F32),
                                  ALU.subtract).then_inc(f_lo, 1)
        group(0)
        with dve.Fori(1, G) as g:
            group(g)
        dve.wait_ge(mod_mm, 1)
        gate_steps(dve, bank[0:2], sign[:], mag[:], ga, mod_step)

    @block.gpsimd
    def _(pool):
        def group(g):
            pool.wait_ge(o_hi, g + 1)
            pool.tensor_tensor(wo[:, 1], raw_o[:], wo[:, 0].bitcast(F32), ALU.subtract).then_inc(o_lo, 1)
        group(0)
        with pool.Fori(1, G) as g:
            group(g)
        pool.wait_ge(sel_in, 16)
        pool.tensor_copy(sumsel[:].rearrange("p h n -> p (h n)"), selraw[:, 0:HG * P])
        pool.tensor_copy(rowsel[:].rearrange("p h n -> p (h n)"), selraw[:, HG * P:])
        pool.wait_ge(up_in, 16)
        pool.tensor_copy(wup[:, 0], raw_up[:]).then_inc(up_hi, 1)
        pool.wait_ge(up_hi, 1)
        pool.tensor_tensor(wup[:, 1], raw_up[:], wup[:, 0].bitcast(F32), ALU.subtract).then_inc(up_lo, 1)


def repeat_rows(act, csil, silu_rows, done):
    for b in range(BATCH):
        last = act.activation(silu_rows[:, b], csil[:, :, b:b + 1].broadcast_to([P, KC, P]), ACT.Copy)
    last.then_inc(done, 1)


def gate_steps(dve, bank, sign, mag, gate, step):
    for b in range(BATCH):
        dve.tensor_scalar(sign, bank[b][:], 0.0, 2.0, ALU.is_ge, ALU.mult).then_inc(step, 1)
        dve.tensor_scalar(mag, bank[b][:], -1.0, None, ALU.mult).then_inc(step, 1)
        dve.wait_ge(step, 5 * b + 2)
        dve.tensor_scalar(sign, sign, -1.0, None, ALU.add).then_inc(step, 1)
        dve.scalar_tensor_tensor(mag, bank[b][:], 0.25, mag, ALU.max, ALU.max).then_inc(step, 1)
        dve.wait_ge(step, 5 * b + 4)
        dve.tensor_tensor(gate[:, b], sign, mag, ALU.mult).then_inc(step, 1)
        dve.wait_ge(step, 5 * b + 5)


def attend_block(nc, scope, sb, bank, x_tok, x_mid, q_parts, k_parts, v_parts, ck_parts, table, kons, ident, low,
                 ckT, wup, fold, sumsel, rowsel, qw_col, sinkb, sink_f, sink_g, ga):
    sem = semaphores(nc, scope)
    WG = HG * P
    q_st = sb(scope, "q_st", [P, 2, 2, P], F32R)
    rope_st = sb(scope, "rope_st", [P, 2, P])
    k_st = sb(scope, "k_st", [P, 2, 2, 2, P], F32R)
    v_st = sb(scope, "v_st", [P, 2, 2, 2, P], F32R)
    ck_st = sb(scope, "ck_st", [P, 2, 2, 2, P], F32R)
    sq = sb(scope, "sq", [P, HG, D])
    ss = sb(scope, "ss", [P, 2, HG])
    rq = sb(scope, "rq", [P, 2, HG])
    exponent = sb(scope, "exponent", [P, HG])
    spare, settled = sb(scope, "spare", [P, 2 * UNROLL]), [0]
    qn = sb(scope, "qn", [P, 2, HG, D])
    ropb = sb(scope, "ropb2", [P, HG, 2 * HALF])
    q32 = sb(scope, "q32", [P, 2, WG])
    qT = sb(scope, "qT", [P, 2, 2, WG], F32R)
    prob = sb(scope, "prob", [P, 2, WG])
    MASKED, WHOLE = 0, 1
    pp = sb(scope, "pp", [P, 2, 2, 2, WG], F32R)
    logits = sb(scope, "logits", [P, GPT, HG, NB + 1])
    cs = sb(scope, "cs", [P, 2, HG, NB + 1])
    cmx = sb(scope, "cmx", [P, 2, HG])
    csm = sb(scope, "csm", [P, 2, HG])
    crs = sb(scope, "crs", [P, 2, HG])
    pc = sb(scope, "pc", [P, 2, HG * NB])
    pcT = sb(scope, "pcT", [P, 2, 2, 2 * P], F32R)
    o_sb = sb(scope, "o_sb", [P, WG])
    ao = sb(scope, "ao", [P, WG])
    aoT = sb(scope, "aoT", [P, 2, 2, WG], F32R)
    den = sb(scope, "den", [P, P])
    rec = sb(scope, "rec", [P, P])
    rden = sb(scope, "rden", [P, 2, 2, P], F32R)
    x_t = sb(scope, "x_t", [P, 2, C])
    y_t = sb(scope, "y_t", [P, C])

    names = ("consts q_mm q_sq q_ms q_rs q_sc q_r1 q_rope qT_mm q32_out qT_hi qT_lo "
             "sc_mm cc_mm merged tanhed exped p_hi p_lo pm_hi pm_lo "
             "c_log c_max c_sub c_exp c_sum c_rec c_nrm cT_mm cT_hi cT_lo "
             "pv_mm o_out sm_mm den_st rec_st r_hi r_lo rb_mm cv_mm ao1 ao2 ao_hi ao_lo wp_mm y_st x_done").split()
    names += [f"{n}{slot}" for n in ("q_in", "rope_in", "k_in", "v_in", "c_in", "x_in", "x_out") for slot in range(2)]
    s = {n: sem("a_" + n) for n in names}
    block = scope.enter_context(nc.Block())

    Q, T, SD, SPV, CC, O, RB, Y = bank
    BODIES = GROUPS // UNROLL
    PROLOGUE = 1
    DEPTH = 4

    class At:

        def __init__(self, m, r, lag):
            self.m, self.c = m, r - lag
            self.slot, self.j = self.c % 2, self.c % GPT
            self.tile_slot = (self.c // GPT) % 2
            self.live = not isinstance(m, int) or 0 <= m * UNROLL + self.c < GROUPS

        def n(self, back=0, per=1):
            return self.m * (UNROLL * per) + (self.c + 1 - back) * per

        def tile(self):
            return self.m * (UNROLL // GPT) + self.c // GPT

        def tiles(self, back=0):
            return self.tile() + (1 - back)

        def loaded(self):
            return (self.m + self.c // UNROLL) * 16 + 16

    def steps(engine, *operations):
        def step(m, r):
            for lag, operation in operations:
                g = At(m, r, lag)
                if g.live:
                    operation(g)
        for m in range(PROLOGUE):
            for r in range(UNROLL):
                step(m, r)
        with engine.Fori(PROLOGUE, BODIES) as m:
            for r in range(UNROLL):
                step(m, r)
        for r in range(DEPTH):
            step(BODIES, r)

    def wait(engine, name, count):
        if since(count):
            engine.wait_ge(s[name], count)

    @block.tensor
    def _(pe):
        def three(out, pairs, start=True, stop=True):
            n = len(pairs)
            for q, (lhs, rhs) in enumerate(pairs):
                for u, (a, b) in enumerate(((0, 0), (0, 1), (1, 0))):
                    last = pe.matmul(out, lhs[a], rhs[b], start=start and q == 0 and u == 0,
                                     stop=stop and q == n - 1 and u == 2)
            return last

        def query(g):
            wait(pe, f"q_in{g.tile_slot}", g.loaded())
            wait(pe, "q_sc", g.n(1))
            cols = slice(g.j * WG, (g.j + 1) * WG)
            three(Q[:], [((q_st[:, g.tile_slot, 0], q_st[:, g.tile_slot, 1]), (wup[:, 0, cols], wup[:, 1, cols]))]
                  ).then_inc(s["q_mm"], 1)

        def compressed_values(g):
            wait(pe, "cT_lo", g.n())
            wait(pe, f"c_in{g.tile_slot}", g.loaded())
            wait(pe, "o_out", g.n())
            cp = ck_st[:, g.tile_slot]
            out = O[:].rearrange("p (pair half n) -> p half pair n", half=2, n=P)
            for half in range(2):
                last = three(out[:, half], [((cp[:, half, 0], cp[:, half, 1]),
                                             tuple(pcT[:, g.slot, part].rearrange("p (pair n) -> p pair n", n=P)
                                                   for part in range(2)))])
            last.then_inc(s["cv_mm"], 1)

        def window_scores(g):
            wait(pe, "qT_lo", g.n())
            wait(pe, f"k_in{g.tile_slot}", g.loaded())
            wait(pe, "tanhed", g.n(1))
            ks = k_st[:, g.tile_slot]
            query_parts = (qT[:, g.slot, 0], qT[:, g.slot, 1])
            three(SPV[:], [((ks[:, 0, 0], ks[:, 0, 1]), query_parts)])
            three(SD[:], [((ks[:, 1, 0], ks[:, 1, 1]), query_parts)]).then_inc(s["sc_mm"], 1)

        def sums(g):
            wait(pe, "p_lo", g.n())
            wait(pe, "pm_lo", g.n())
            wait(pe, "ao1", g.n(1))
            which = (g.tile() % TPB + TPB - 1) // TPB if g.tile_slot == 0 else WHOLE
            for h in range(HG):
                for part in range(2):
                    moving = pp[:, g.slot, bass.ds(which, 1), part, h * P:(h + 1) * P].rearrange("p a n -> p (a n)")
                    last = pe.matmul(RB[:, 0:P], sumsel[:, h], moving,
                                     start=(h == 0 and part == 0), stop=(h == HG - 1 and part == 1))
            last.then_inc(s["sm_mm"], 1)

        def window_values(g):
            wait(pe, f"v_in{g.tile_slot}", g.loaded())
            wait(pe, "ao2", g.n(1))
            vs = v_st[:, g.tile_slot]
            three(O[:], [((vs[:, 0, 0], vs[:, 0, 1]), (pp[:, g.slot, WHOLE, 0], pp[:, g.slot, WHOLE, 1])),
                         ((vs[:, 1, 0], vs[:, 1, 1]), (pp[:, g.slot, MASKED, 0], pp[:, g.slot, MASKED, 1]))]
                  ).then_inc(s["pv_mm"], 1)

        def project(g):
            wait(pe, "ao_lo", g.n())
            if g.j == 0:
                wait(pe, "y_st", g.tile())
            for h in range(HG):
                head = g.j * HG + h
                lhs = [aoT[:, g.slot, part, h * P:(h + 1) * P] for part in range(2)]
                last = three(Y[:], [(lhs, (fold[:, head, 0], fold[:, head, 1]))],
                             start=(g.j == 0 and h == 0), stop=(g.j == GPT - 1 and h == HG - 1))
            last.then_inc(s["wp_mm"], 1)

        def transpose_query(g):
            wait(pe, "q_rope", g.n())
            wait(pe, "cT_lo", g.n(2))
            for h in range(HG):
                last = pe.transpose(T[:, h * P:(h + 1) * P], qn[:, g.slot, h], ident)
            last.then_inc(s["qT_mm"], 1)

        def denominators(g):
            wait(pe, "r_lo", g.n())
            for h in range(HG):
                for part in range(2):
                    last = pe.matmul(RB[:, h * P:(h + 1) * P], rowsel[:, h], rden[:, g.slot, part],
                                     start=(part == 0), stop=(part == 1))
            last.then_inc(s["rb_mm"], 1)

        def compressed_scores(g):
            wait(pe, "q32_out", g.n())
            wait(pe, "c_log", g.n(1))
            keys = ckT[:, bass.ds(g.tile() // TPB * NB, NB)]
            for h in range(HG):
                last = pe.matmul(CC[:, h * NB:(h + 1) * NB], q32[:, g.slot, h * P:(h + 1) * P], keys,
                                 start=True, stop=True)
            last.then_inc(s["cc_mm"], 1)

        def transpose_compressed(g):
            wait(pe, "c_nrm", g.n())
            ahead = At(g.m, g.c + 1, 0)
            if ahead.live:
                wait(pe, "q32_out", ahead.n())
            for pair in range(2):
                cols = slice(pair * P, (pair + 1) * P)
                last = pe.transpose(T[:, cols], pc[:, g.slot, cols], ident)
            last.then_inc(s["cT_mm"], 1)

        wait(pe, "consts", 2)
        steps(pe, (0, query), (4, compressed_values), (1, window_scores), (3, sums), (3, window_values),
              (4, project), (0, transpose_query), (3, denominators), (0, compressed_scores),
              (1, transpose_compressed))

    @block.scalar
    def _(act):
        def probs_high(g):
            wait(act, "exped", g.n())
            wait(act, "pv_mm", g.n(2))
            act.activation(pp[:, g.slot, WHOLE, 0], prob[:, g.slot], ACT.Copy).then_inc(s["p_hi"], 1)

        def squares(g):
            wait(act, "q_mm", g.n())
            wait(act, "q_ms", g.n(2))
            for h in range(HG):
                last = act.activation(sq[:, h], Q[:, h * D:(h + 1) * D], ACT.Square, accum_out=ss[:, g.slot, h:h + 1])
            last.then_inc(s["q_sq"], 1)

        def compressed_high(g):
            wait(act, "cT_mm", g.n())
            wait(act, "cv_mm", g.n(2))
            act.activation(pcT[:, g.slot, 0], T[:, 0:2 * P], ACT.Copy).then_inc(s["cT_hi"], 1)

        def out_high(g):
            wait(act, "ao2", g.n())
            wait(act, "wp_mm", g.n(2))
            act.activation(aoT[:, g.slot, 0], ao[:], ACT.Copy).then_inc(s["ao_hi"], 1)

        def denominator(g):
            wait(act, "sm_mm", g.n())
            wait(act, "rec_st", g.n(1))
            act.activation(den[:], RB[:, 0:P], ACT.Identity, scale=sink_f[:, g.j:g.j + 1],
                           bias=sink_g[:, g.j:g.j + 1]).then_inc(s["den_st"], 1)

        def compressed_exp(g):
            wait(act, "c_sub", g.n())
            act.activation(cs[:, g.slot], cs[:, g.slot], ACT.Exp).then_inc(s["c_exp"], 1)

        def window_out(g):
            wait(act, "pv_mm", g.n())
            wait(act, "ao1", g.n(1))
            act.activation(o_sb[:], O[:], ACT.Copy).then_inc(s["o_out"], 1)

        def reciprocal_high(g):
            wait(act, "rec_st", g.n())
            wait(act, "rb_mm", g.n(2))
            act.activation(rden[:, g.slot, 0], rec[:], ACT.Copy, scale=sink_f[:, g.j:g.j + 1]).then_inc(s["r_hi"], 1)

        def tanh(g):
            wait(act, "merged", g.n())
            wait(act, "p_lo", g.n(2))
            act.activation(prob[:, g.slot], SD[:], ACT.Tanh, scale=SCALE / CAP).then_inc(s["tanhed"], 1)

        def exp(g):
            wait(act, "tanhed", g.n())
            act.activation(prob[:, g.slot], prob[:, g.slot], ACT.Exp, scale=CAP).then_inc(s["exped"], 1)

        def query_out(g):
            wait(act, "qT_mm", g.n())
            wait(act, "cc_mm", g.n(2))
            wait(act, "qT_lo", g.n(2))
            act.activation(q32[:, g.slot], T[:], ACT.Copy, scale=qw_col[:, 0:1]).then_inc(s["q32_out"], 1)

        def query_high(g):
            wait(act, "q32_out", g.n())
            wait(act, "sc_mm", g.n(2))
            act.activation(qT[:, g.slot, 0], q32[:, g.slot], ACT.Copy).then_inc(s["qT_hi"], 1)

        steps(act, (2, probs_high), (0, squares), (2, compressed_high), (4, out_high), (3, denominator),
              (1, compressed_exp), (3, window_out), (3, reciprocal_high), (1, tanh), (0, query_out), (0, query_high), (1, exp))

    @block.vector
    def _(dve):
        def compressed_logits(g):
            wait(dve, "cc_mm", g.n())
            wait(dve, "c_sub", g.n(4))
            mask = kons[:, bass.ds(K_CMASK + (g.tile() % TPB) * NB, NB)].unsqueeze(1).broadcast_to([P, HG, NB])
            dve.scalar_tensor_tensor(logits[:, g.j, :, 0:NB], CC[:, 0:2 * P].rearrange("p (h n) -> p h n", h=HG),
                                     SCALE, mask, ALU.mult, ALU.add).then_inc(s["c_log"], 1)

        def query_low(g):
            wait(dve, "qT_hi", g.n())
            dve.tensor_tensor(qT[:, g.slot, 1], q32[:, g.slot], qT[:, g.slot, 0].bitcast(F32),
                              ALU.subtract).then_inc(s["qT_lo"], 1)

        def compressed_max(g):
            wait(dve, "c_log", g.n())
            wait(dve, "c_sub", g.n(2))
            dve.tensor_reduce(cmx[:, g.slot], logits[:, g.j], AX.X, ALU.max).then_inc(s["c_max"], 1)

        def add_compressed(g):
            wait(dve, "cv_mm", g.n())
            wait(dve, "ao1", g.n())
            dve.tensor_tensor(ao[:], ao[:], O[:], ALU.add).then_inc(s["ao2"], 1)

        def mean_square(g):
            wait(dve, "q_sq", g.n())
            wait(dve, "q_sc", g.n(2))
            dve.tensor_scalar(rq[:, g.slot], ss[:, g.slot], 1.0 / D, RMS_EPS, ALU.mult, ALU.add
                              ).then_inc(s["q_ms"], 1)

        def compressed_low(g):
            wait(dve, "cT_hi", g.n())
            dve.tensor_tensor(pcT[:, g.slot, 1], T[:, 0:2 * P], pcT[:, g.slot, 0].bitcast(F32),
                              ALU.subtract).then_inc(s["cT_lo"], 1)

        def out_low(g):
            wait(dve, "ao_hi", g.n())
            dve.tensor_tensor(aoT[:, g.slot, 1], ao[:], aoT[:, g.slot, 0].bitcast(F32),
                              ALU.subtract).then_inc(s["ao_lo"], 1)

        def scale_query(g):
            wait(dve, "q_rs", g.n())
            wait(dve, "qT_mm", g.n(2))
            dve.tensor_tensor(qn[:, g.slot], Q[:].rearrange("p (h d) -> p h d", h=HG),
                              rq[:, g.slot].unsqueeze(2).broadcast_to([P, HG, D]), ALU.mult).then_inc(s["q_sc"], 1)

        def merge(g):
            wait(dve, "sc_mm", g.n())
            settled[0] = (settled[0] + 1) % spare.shape[1]
            dve.tensor_tensor(spare[:, settled[0]:settled[0] + 1], low[:, 0:1], low[:, 0:1], ALU.mult)
            up = kons[:, K_UP:K_UP + P].bitcast(U32).unsqueeze(1).broadcast_to([P, HG, P])
            dve.copy_predicated(SD[:].rearrange("p (h n) -> p h n", h=HG), up,
                                SPV[:].rearrange("p (h n) -> p h n", h=HG)).then_inc(s["merged"], 1)

        def reciprocal(g):
            wait(dve, "den_st", g.n())
            wait(dve, "r_lo", g.n(1))
            dve.reciprocal(rec[:], den[:]).then_inc(s["rec_st"], 1)

        def compressed_sum(g):
            wait(dve, "c_exp", g.n())
            dve.tensor_reduce(csm[:, g.slot], cs[:, g.slot], AX.X, ALU.add).then_inc(s["c_sum"], 1)
            wait(dve, "c_sum", g.n())
            wait(dve, "c_nrm", g.n(2))
            dve.reciprocal(crs[:, g.slot], csm[:, g.slot]).then_inc(s["c_rec"], 1)

        def reciprocal_low(g):
            wait(dve, "r_hi", g.n())
            dve.scalar_tensor_tensor(rden[:, g.slot, 1], rec[:], sink_f[:, g.j:g.j + 1],
                                     rden[:, g.slot, 0].bitcast(F32), ALU.mult, ALU.subtract).then_inc(s["r_lo"], 1)

        def tile_out(g):
            if g.j == GPT - 1:
                slot = g.tile_slot
                wait(dve, "wp_mm", g.n())
                wait(dve, "x_done", g.tile())
                dve.tensor_tensor(y_t[:], Y[:], ga[:, bass.ds(g.tile() // TPB, 1), :].rearrange("p b c -> p (b c)"),
                                  ALU.mult).then_inc(s["y_st"], 1)
                wait(dve, "y_st", g.tiles())
                wait(dve, f"x_in{slot}", g.loaded())
                dve.tensor_tensor(x_t[:, slot], x_t[:, slot], y_t[:], ALU.add).then_inc(s["x_done"], 1)

        def masked_low(g):
            wait(dve, "p_lo", g.n())
            dve.tensor_tensor(pp[:, g.slot, MASKED, 1].rearrange("p (h n) -> p h n", h=HG),
                              pp[:, g.slot, WHOLE, 1].bitcast(F32).rearrange("p (h n) -> p h n", h=HG),
                              low.unsqueeze(1).broadcast_to([P, HG, P]), ALU.mult).then_inc(s["pm_lo"], 1)

        def divide(g):
            wait(dve, "o_out", g.n())
            wait(dve, "rb_mm", g.n())
            wait(dve, "ao_lo", g.n(1))
            dve.tensor_tensor(ao[:], o_sb[:], RB[:], ALU.mult).then_inc(s["ao1"], 1)

        dve.memset(exponent[:], -0.5).then_inc(s["consts"], 1)
        dve.tensor_copy(logits[:].rearrange("p g h n -> p (g h) n")[:, :, NB], sinkb[:]).then_inc(s["consts"], 1)
        wait(dve, "consts", 2)
        steps(dve, (1, compressed_logits), (1, query_low), (1, compressed_max), (4, add_compressed), (0, mean_square),
              (2, compressed_low), (4, out_low), (0, scale_query), (1, merge), (3, reciprocal), (1, compressed_sum),
              (3, reciprocal_low), (4, tile_out), (2, masked_low), (3, divide))

    @block.gpsimd
    def _(pool):
        def masked_high(g):
            wait(pool, "p_hi", g.n())
            pool.tensor_tensor(pp[:, g.slot, MASKED, 0].rearrange("p (h n) -> p h n", h=HG),
                               pp[:, g.slot, WHOLE, 0].bitcast(F32).rearrange("p (h n) -> p h n", h=HG),
                               low.unsqueeze(1).broadcast_to([P, HG, P]), ALU.mult).then_inc(s["pm_hi"], 1)

        def rsqrt(g):
            wait(pool, "q_ms", g.n())
            pool.tensor_tensor(rq[:, g.slot], rq[:, g.slot], exponent[:], ALU.pow).then_inc(s["q_rs"], 1)

        def compressed_less_max(g):
            wait(pool, "c_max", g.n())
            wait(pool, "c_sum", g.n(2))
            wait(pool, "c_nrm", g.n(2))
            pool.tensor_tensor(cs[:, g.slot], logits[:, g.j], cmx[:, g.slot].unsqueeze(2).broadcast_to([P, HG, NB + 1]),
                               ALU.subtract).then_inc(s["c_sub"], 1)

        def rotate(g):
            wait(pool, "q_sc", g.n())
            wait(pool, "q_rope", g.n(1))
            wait(pool, f"rope_in{g.tile_slot}", g.loaded())
            over = lambda lo, n: rope_st[:, g.tile_slot, lo:lo + n].unsqueeze(1).broadcast_to([P, HG, n])
            x = qn[:, g.slot]
            pool.tensor_tensor(ropb[:, :, 0:HALF], x[:, :, HALF:2 * HALF], over(2 * HALF, HALF),
                               ALU.mult).then_inc(s["q_r1"], 1)
            pool.tensor_tensor(ropb[:, :, HALF:], x[:, :, 0:HALF], over(3 * HALF, HALF), ALU.mult).then_inc(s["q_r1"], 1)
            wait(pool, "q_r1", g.n(1, 3) + 2)
            pool.tensor_tensor(x[:, :, 0:2 * HALF], x[:, :, 0:2 * HALF], over(0, 2 * HALF), ALU.mult).then_inc(s["q_r1"], 1)
            wait(pool, "q_r1", g.n(per=3))
            pool.tensor_tensor(x[:, :, 0:2 * HALF], x[:, :, 0:2 * HALF], ropb[:], ALU.add).then_inc(s["q_rope"], 1)

        def probs_low(g):
            wait(pool, "p_hi", g.n())
            pool.tensor_tensor(pp[:, g.slot, WHOLE, 1], prob[:, g.slot], pp[:, g.slot, WHOLE, 0].bitcast(F32),
                               ALU.subtract).then_inc(s["p_lo"], 1)

        def compressed_over_sum(g):
            wait(pool, "c_rec", g.n())
            wait(pool, "cT_mm", g.n(2))
            pool.tensor_tensor(pc[:, g.slot].rearrange("p (h n) -> p h n", h=HG), cs[:, g.slot, :, 0:NB],
                               crs[:, g.slot].unsqueeze(2).broadcast_to([P, HG, NB]), ALU.mult
                               ).then_inc(s["c_nrm"], 1)

        wait(pool, "consts", 2)
        steps(pool, (2, masked_high), (0, rsqrt), (1, compressed_less_max), (0, rotate), (2, probs_low),
              (1, compressed_over_sum))

    @block.sync
    def _(sp):
        def load(t, slot, nth):
            def free(name, count):
                if since(count):
                    sp.wait_ge(s[name], count)
            free("q_mm", GPT * (t - 1))
            sp.dma_start(q_st[:, slot].bitcast(F32), q_parts[bass.ds(t, 1)].rearrange("t p a n -> (t p) a n")
                         ).then_inc(s[f"q_in{slot}"], 16)
            free("q_rope", GPT * (t - 1))
            sp.dma_start(rope_st[:, slot], table[:, bass.ds(K_ROPE + (t % TPB) * P, P)]).then_inc(s[f"rope_in{slot}"], 16)
            free("sc_mm", GPT * (t - 1))
            sp.dma_start(k_st[:, slot].bitcast(F32), k_parts[bass.ds(t + t // TPB, 2)].rearrange("t p a n -> p t a n")
                         ).then_inc(s[f"k_in{slot}"], 16)
            free("pv_mm", GPT * (t - 1))
            sp.dma_start(v_st[:, slot].rearrange("p a b n -> p (a b) n").bitcast(F32),
                         v_parts[bass.ds(t, 1)].rearrange("t p a n -> (t p) a n")).then_inc(s[f"v_in{slot}"], 16)
            free("cv_mm", GPT * (t - 1))
            sp.dma_start(ck_st[:, slot].rearrange("p a b n -> p (a b) n").bitcast(F32),
                         ck_parts[bass.ds(t // TPB, 1)].rearrange("t p a n -> (t p) a n")).then_inc(s[f"c_in{slot}"], 16)

        def store(t, slot, nth):
            sp.wait_ge(s["x_done"], t + 1)
            sp.dma_start(token_rows(x_mid, t), x_t[:, slot]).then_inc(s[f"x_out{slot}"], 16)
            sp.wait_ge(s[f"x_out{slot}"], 16 * nth + 16)

        def load_x(t, slot):
            sp.dma_start(x_t[:, slot], token_rows(x_tok, t)).then_inc(s[f"x_in{slot}"], 16)

        for t in range(4):
            if t == 3:
                store(0, 0, 0)
                load_x(2, 0)
            load(t, t % 2, t // 2)
            if t < 2:
                load_x(t, t)
        with sp.Fori(2, TILES // 2) as n:
            for slot in range(2):
                t = 2 * n + slot
                store(2 * n + (slot - 3), 1 - slot, n + (slot - 3) // 2)
                load_x(2 * n + (slot - 1), 1 - slot)
                load(t, slot, n)
        for t in range(TILES - 3, TILES):
            store(t, t % 2, t // 2)
            if t == TILES - 3:
                load_x(TILES - 1, (TILES - 1) % 2)


def ffn_prepare(nc, scope, sb, bank, wq_gate, s_gate, wq_up, s_up, wq_down, s_down, wmod, ident, csil,
                wT, wd, sg, row, modT):
    sem = semaphores(nc, scope, "f_")
    raw_a = sb(scope, "raw_a", [P, HB * C], I32)
    raw_b = sb(scope, "raw_b", [P, HB * C], I32)
    conv_d = sb(scope, "conv_d", [P, HID])
    conv = conv_d[:, 0:2 * C].rearrange("p (w c) -> p w c", w=2)
    mod_w = sb(scope, "mod_w2", [P, KC, C])
    sign = sb(scope, "sign_b", [P, C])
    sdrow = sb(scope, "sdrow", [P, C])
    silu_rows = raw_b[:, 0:BATCH * KC * P].bitcast(F32).rearrange("p (b k n) -> p b k n", b=BATCH, k=KC)
    rows_done = sem("rows_done")
    CUT = (HB + 1) // 2
    gate_in = [sem("gate_in0"), sem("gate_in1")]
    up_in = [sem("up_in0"), sem("up_in1")]
    down_in, small_in, mod_in, conved, tr_mm, w_hi, w_lo, mod_mm, mod_out, row_st = map(sem, (
        "down_in", "small_in", "mod_in", "conved", "tr_mm", "w_hi", "w_lo", "mod_mm", "mod_out", "row_st"))
    block = scope.enter_context(nc.Block())
    rawg = raw_a[:].rearrange("p (h c) -> p h c", h=HB)
    rawu = raw_b[:].rearrange("p (h c) -> p h c", h=HB)
    rawd = raw_a[:].rearrange("p (o h) -> p o h", o=KC)
    gate_v = wq_gate.rearrange("(h p) c -> p h c", p=P)
    up_v = wq_up.rearrange("(h p) c -> p h c", p=P)

    @block.sync
    def _(sp):
        for q, part in enumerate((slice(0, CUT), slice(CUT, HB))):
            sp.dma_start(rawg[:, part], gate_v[:, part]).then_inc(gate_in[q], 16)
            sp.dma_start(rawu[:, part], up_v[:, part]).then_inc(up_in[q], 16)
        sp.wait_ge(conved, 2 * HB)
        sp.dma_start(rawd, wq_down.rearrange("(o p) h -> p o h", p=P)).then_inc(down_in, 16)

    @block.scalar
    def _(act):
        act.dma_start(mod_w[:], wmod[:, 3 * C:4 * C].rearrange("(k p) n -> p k n", p=P)).then_inc(mod_in, 16)
        act.dma_start(sg[:, 0], s_gate.rearrange("(h p) -> p h", p=P), allow_slow_non_contiguous=True).then_inc(small_in, 16)
        act.dma_start(sg[:, 1], s_up.rearrange("(h p) -> p h", p=P), allow_slow_non_contiguous=True).then_inc(small_in, 16)
        act.dma_start(sdrow[:], s_down.partition_broadcast(P)).then_inc(small_in, 16)
        for n in range(1, 3):
            act.wait_ge(mod_mm, n)
            act.dma_start(mod_w[:], wmod[:, (3 + n) * C:(4 + n) * C].rearrange("(k p) n -> p k n", p=P)
                          ).then_inc(mod_in, 16)
        act.activation(modT[:, 0:KC], bank[5][:, 0:2 * KC].rearrange("p (k b) -> p k b", b=BATCH),
                       ACT.Copy).then_inc(mod_out, 1)
        act.activation(modT[:, KC:2 * KC], bank[5][:, 2 * KC:4 * KC].rearrange("p (k b) -> p k b", b=BATCH),
                       ACT.Identity, bias=1.0).then_inc(mod_out, 1)

        def gate_up(h):
            for w in range(2):
                act.wait_ge(tr_mm, 2 * h + (w + 1))
                act.activation(wT[:, bass.ds(h, 1), w, 0].rearrange("p a k n -> p (a k) n"),
                               bank[w][:].rearrange("p (k n) -> p k n", k=KC), ACT.Copy).then_inc(w_hi, 1)
        with act.Fori(0, HB) as h:
            gate_up(h)
        act.wait_ge(conved, 2 * HB)
        repeat_rows(act, csil, silu_rows, rows_done)
        for o in range(KC):
            for n, lo in enumerate(range(0, HB, 4)):
                hi = min(lo + 4, HB)
                act.wait_ge(tr_mm, 2 * HB + 3 * o + n + 1)
                act.activation(wd[:, lo:hi, 0, o * P:(o + 1) * P],
                               bank[2 + n][:, 0:(hi - lo) * P].rearrange("p (h n) -> p h n", n=P),
                               ACT.Copy).then_inc(w_hi, 1)

    @block.vector
    def _(dve):
        def gate_up(h, q):
            dve.wait_ge(gate_in[q], 16)
            dve.wait_ge(up_in[q], 16)
            if since(h):
                dve.wait_ge(tr_mm, 2 * h)
            for w, raw in enumerate((rawg, rawu)):
                dve.tensor_scalar(conv[:, w:w + 1], raw[:, bass.ds(h, 1)], -ZERO_POINT, None,
                                  ALU.add).then_inc(conved, 1)
            for w in range(2):
                dve.wait_ge(w_hi, 2 * h + (w + 1))
                out = wT[:, bass.ds(h, 1), w].rearrange("p a s k n -> p (a s) k n")
                dve.tensor_tensor(out[:, 1], bank[w][:].rearrange("p (k n) -> p k n", k=KC),
                                  out[:, 0].bitcast(F32), ALU.subtract).then_inc(w_lo, 1)
        gate_up(0, 0)
        with dve.Fori(1, CUT) as h:
            gate_up(h, 0)
        with dve.Fori(CUT, HB) as h:
            gate_up(h, 1)
        dve.wait_ge(down_in, 16)
        for o in range(KC):
            dve.wait_ge(tr_mm, 2 * HB + 3 * o)
            dve.tensor_scalar(conv_d[:], rawd[:, o], -ZERO_POINT, None, ALU.add).then_inc(conved, 1)
            for n, lo in enumerate(range(0, HB, 4)):
                hi = min(lo + 4, HB)
                dve.wait_ge(w_hi, 2 * HB + 3 * o + n + 1)
                dve.tensor_tensor(wd[:, lo:hi, 1, o * P:(o + 1) * P],
                                  bank[2 + n][:, 0:(hi - lo) * P].rearrange("p (h n) -> p h n", n=P),
                                  wd[:, lo:hi, 0, o * P:(o + 1) * P].bitcast(F32), ALU.subtract).then_inc(w_lo, 1)
        dve.wait_ge(mod_mm, 3)
        gate_steps(dve, bank[6:8], sign[:], conv_d[:, 0:C], row, row_st)
        dve.wait_ge(small_in, 48)
        for b in range(BATCH):
            dve.tensor_tensor(row[:, b], row[:, b], sdrow[:], ALU.mult)

    @block.tensor
    def _(pe):
        for n in range(2):
            pe.wait_ge(mod_in, 16 * (n + 1))
            for q in range(KC):
                col = 2 * (n * KC + q)
                for k in range(KC):
                    last = pe.matmul(bank[5][:, col:col + 2], mod_w[:, k, q * P:(q + 1) * P], csil[:, k],
                                     start=(k == 0), stop=(k == KC - 1))
            last.then_inc(mod_mm, 1)

        def gate_up(h):
            for w in range(2):
                pe.wait_ge(conved, 2 * h + (w + 1))
                if since(h):
                    pe.wait_ge(w_lo, 2 * h + (w - 1))
                for k in range(KC):
                    last = pe.transpose(bank[w][:, k * P:(k + 1) * P], conv[:, w, k * P:(k + 1) * P], ident)
                last.then_inc(tr_mm, 1)
        gate_up(0)
        with pe.Fori(1, HB) as h:
            gate_up(h)
        pe.wait_ge(mod_in, 48)
        pe.wait_ge(rows_done, 1)
        for b in range(BATCH):
            for k in range(KC):
                last = pe.matmul(bank[6 + b][:], silu_rows[:, b, k], mod_w[:, k], start=(k == 0), stop=(k == KC - 1))
        last.then_inc(mod_mm, 1)
        for o in range(KC):
            pe.wait_ge(conved, 2 * HB + o + 1)
            for n, lo in enumerate(range(0, HB, 4)):
                if o:
                    pe.wait_ge(w_lo, 2 * HB + 3 * (o - 1) + n + 1)
                for h in range(lo, min(lo + 4, HB)):
                    last = pe.transpose(bank[2 + n][:, (h - lo) * P:(h - lo + 1) * P], conv_d[:, h * P:(h + 1) * P], ident)
                last.then_inc(tr_mm, 1)


def ffn_block(nc, scope, sb, bank, x_mid, out_tok, ident, wT, wd, sg, row, modT):
    sem = semaphores(nc, scope, "g_")
    xs = sb(scope, "xs2", [P, 2, CHUNK, C])
    z = sb(scope, "z2", [P, CHUNK, C])
    stats = sb(scope, "stats2", [P, CHUNK, 6])
    meanvar = sb(scope, "meanvar2", [P, CHUNK, 2])
    rstd = sb(scope, "rstd2", [P, CHUNK])
    minus_half = sb(scope, "minus_half2", [P, CHUNK])
    hT = sb(scope, "hT2", [P, 2, KC, W], F32R)
    sl = sb(scope, "sl", [P, 2, W])
    gu = sb(scope, "gu", [P, 2, W])
    sl2 = sb(scope, "sl2", [P, 2, W])
    gus = sb(scope, "gus", [P, 2, 2, W], F32R)
    x_in = [sem("x_in0"), sem("x_in1")]
    x_out = [sem("x_out0"), sem("x_out1")]
    init, stat, var, rs, z_done, tr_mm, h_hi, h_lo, gu_mm, silued, gued, gu_hi, gu_lo, dn_mm, y1, y2 = map(sem, (
        "init stat var rs z_done tr_mm h_hi h_lo gu_mm silued gued gu_hi gu_lo dn_mm y1 y2".split()))
    block = scope.enter_context(nc.Block())
    Y, GU = bank[0:4], bank[4:8]

    @block.sync
    def _(sp):
        for c in range(CHUNKS):
            slot = c % 2
            if c >= 2:
                sp.wait_ge(y2, CHUNK * (c - 1))
                sp.dma_start(out_tok[(c - 2) * W:(c - 1) * W, :].rearrange("(t p) c -> p t c", p=P), xs[:, slot]
                             ).then_inc(x_out[slot], 16)
                sp.wait_ge(x_out[slot], 16 * (c // 2))
            sp.dma_start(xs[:, slot], x_mid[c * W:(c + 1) * W, :].rearrange("(t p) c -> p t c", p=P)
                         ).then_inc(x_in[slot], 16)
        for c in range(CHUNKS - 2, CHUNKS):
            sp.wait_ge(y2, CHUNK * (c + 1))
            sp.dma_start(out_tok[c * W:(c + 1) * W, :].rearrange("(t p) c -> p t c", p=P), xs[:, c % 2]
                         ).then_inc(x_out[c % 2], 16)
            sp.wait_ge(x_out[c % 2], 16 * (CHUNKS // 2))

    @block.tensor
    def _(pe):
        def down(c, h):
            pe.wait_ge(gu_lo, HB * c + h + 1)
            for t in range(CHUNK):
                if h == 0 and c:
                    pe.wait_ge(y1, CHUNK * (c - 1) + t + 1)
                for n, (a, b) in enumerate(((0, 0), (0, 1), (1, 0))):
                    last = pe.matmul(Y[t][:], gus[:, h % 2, a, t * P:(t + 1) * P], wd[:, h, b],
                                     start=(h == 0 and n == 0), stop=(h == HB - 1 and n == 2))
            last.then_inc(dn_mm, 1)

        for c in range(CHUNKS):
            pe.wait_ge(z_done, CHUNK * (c + 1))
            if c:
                pe.wait_ge(gued, HB * c)
            for k in range(KC):
                for t in range(CHUNK):
                    last = pe.transpose(GU[k][:, t * P:(t + 1) * P], z[:, t, k * P:(k + 1) * P], ident)
            last.then_inc(tr_mm, 1)
            if c:
                down(c - 1, HB - 1)
            pe.wait_ge(h_lo, KC * (c + 1))
            for h in range(HB):
                if h >= 2:
                    pe.wait_ge(gued, HB * c + h - 1)
                for w in range(2):
                    for k in range(KC):
                        for n, (a, b) in enumerate(((0, 0), (0, 1), (1, 0))):
                            last = pe.matmul(GU[2 * (h % 2) + w][:], wT[:, h, w, a, k], hT[:, b, k],
                                             start=(k == 0 and n == 0), stop=(k == KC - 1 and n == 2))
                last.then_inc(gu_mm, 1)
                if h:
                    down(c, h - 1)
        down(CHUNKS - 1, HB - 1)

    @block.scalar
    def _(act):
        for c in range(CHUNKS):
            b = c // (CHUNKS // BATCH)
            act.wait_ge(tr_mm, c + 1)
            if c:
                act.wait_ge(gu_mm, HB * c)
                act.wait_ge(gu_lo, HB * c)
            for k in range(KC):
                act.activation(hT[:, 0, k], GU[k][:], ACT.Identity, scale=modT[:, KC + k, b:b + 1],
                               bias=modT[:, k, b:b + 1]).then_inc(h_hi, 1)
                act.activation(gu[:, 0] if k % 2 == 0 else gu[:, 1], GU[k][:], ACT.Identity,
                               scale=modT[:, KC + k, b:b + 1], bias=modT[:, k, b:b + 1]).then_inc(h_hi, 1)
                if k >= 1:
                    act.wait_ge(h_lo, KC * c + k)
            for h in range(HB):
                n = HB * c + h
                act.wait_ge(gu_mm, n + 1)
                if h >= 2 or c:
                    act.wait_ge(gued, n - 1)
                act.activation(sl[:, h % 2], GU[2 * (h % 2)][:], ACT.Silu, scale=sg[:, 0, h:h + 1]).then_inc(silued, 1)
                act.wait_ge(gued, n + 1)
                if n >= 2:
                    act.wait_ge(dn_mm, n - 1)
                act.activation(gus[:, h % 2, 0], gu[:, h % 2], ACT.Copy).then_inc(gu_hi, 1)

    @block.vector
    def _(dve):
        dve.memset(minus_half[:], -0.5).then_inc(init, 1)

        def normal(c):
            slot = c % 2
            dve.wait_ge(x_in[slot], 16 * (c // 2 + 1))
            if c:
                dve.wait_ge(rs, 2 * c)
            for t in range(CHUNK):
                dve.bn_stats(stats[:, t], xs[:, slot, t]).then_inc(stat, 1)
            for t in range(CHUNK):
                dve.wait_ge(stat, CHUNK * c + t + 1)
                dve.bn_aggr(meanvar[:, t], stats[:, t]).then_inc(var, 1)
            dve.wait_ge(var, CHUNK * (c + 1))
            dve.wait_ge(rs, 2 * (c + 1))
            if c:
                dve.wait_ge(tr_mm, c)
            for t in range(CHUNK):
                dve.tensor_scalar(z[:, t], xs[:, slot, t], meanvar[:, t, 0:1], rstd[:, t:t + 1],
                                  ALU.subtract, ALU.mult).then_inc(z_done, 1)

        normal(0)
        for c in range(CHUNKS):
            for k in range(KC):
                dve.wait_ge(h_hi, 2 * (KC * c + k) + 2)
                dve.tensor_tensor(hT[:, 1, k], gu[:, k % 2], hT[:, 0, k].bitcast(F32), ALU.subtract
                                  ).then_inc(h_lo, 1)
            if c == 0:
                dve.wait_ge(h_lo, KC)
            for h in range(HB):
                n = HB * c + h
                if h < 2:
                    dve.wait_ge(h_lo, KC * (c + 1))
                dve.wait_ge(silued, n + 1)
                if n >= 2:
                    dve.wait_ge(gu_lo, n - 1)
                dve.scalar_tensor_tensor(gu[:, h % 2], GU[2 * (h % 2) + 1][:], sg[:, 1, h:h + 1], sl[:, h % 2],
                                         ALU.mult, ALU.mult).then_inc(gued, 1)
                if h == HB // 2 and c + 1 < CHUNKS:
                    normal(c + 1)
            b = c // (CHUNKS // BATCH)
            dve.wait_ge(dn_mm, HB * (c + 1))
            for t in range(CHUNK):
                n = CHUNK * c + t
                if n >= 2:
                    dve.wait_ge(y2, n - 1)
                dve.tensor_tensor(sl2[:, t % 2], Y[t][:], row[:, b], ALU.mult).then_inc(y1, 1)
                dve.wait_ge(y1, n + 1)
                dve.tensor_tensor(xs[:, c % 2, t], xs[:, c % 2, t], sl2[:, t % 2], ALU.add).then_inc(y2, 1)

    @block.gpsimd
    def _(pool):
        pool.wait_ge(init, 1)

        def normal(c):
            pool.wait_ge(var, CHUNK * (c + 1))
            if c:
                pool.wait_ge(z_done, CHUNK * c)
            pool.tensor_scalar(rstd[:], meanvar[:, :, 1], 1.0, LN_EPS, ALU.mult, ALU.add).then_inc(rs, 1)
            pool.wait_ge(rs, 2 * c + 1)
            pool.tensor_tensor(rstd[:], rstd[:], minus_half[:], ALU.pow).then_inc(rs, 1)

        normal(0)
        for c in range(CHUNKS):
            for h in range(HB):
                n = HB * c + h
                pool.wait_ge(gu_hi, n + 1)
                if n >= 2:
                    pool.wait_ge(dn_mm, n - 1)
                pool.tensor_tensor(gus[:, h % 2, 1], gu[:, h % 2], gus[:, h % 2, 0].bitcast(F32), ALU.subtract
                                   ).then_inc(gu_lo, 1)
                if h == HB // 2 and c + 1 < CHUNKS:
                    normal(c + 1)


def _table(np):
    t = np.zeros((P, K_ALL), np.float32)
    p = np.arange(P)
    i = (p % (P // M)) * M + p // (P // M)
    t[:, K_IDENT:K_IDENT + P] = np.eye(P)
    t[:, K_LOW:K_LOW + P] = i[:, None] <= i[None, :]
    t[:, K_UP:K_UP + P] = i[:, None] > i[None, :]
    inv = np.float32(1.0) / np.float32(10000.0) ** (np.arange(0, 2 * HALF, 2, dtype=np.float32) / np.float32(2 * HALF))
    ang = np.arange(SEQ, dtype=np.float32)[:, None] * inv[None, :].astype(np.float32)
    cos, sin = np.cos(ang), np.sin(ang)
    rope = np.concatenate([cos, cos, -sin, sin], axis=1).reshape(TPB, P, P)[:, i]
    t[:, K_ROPE:K_CMASK] = rope.transpose(1, 0, 2).reshape(P, TPB * P)
    pos, end = np.arange(SEQ), np.arange(NB) * M + M - 1
    mask = np.where(end[None, :] < pos[:, None], 0.0, -1e30).reshape(TPB, P, NB)[:, i]
    t[:, K_CMASK:K_PERSIST] = mask.transpose(1, 0, 2).reshape(P, TPB * NB)
    for h in range(HG):
        t[:, K_SUMSEL + h * P + 32 * h:K_SUMSEL + h * P + 32 * h + 32] = 1.0
        t[32 * h, K_ROWSEL + h * P:K_ROWSEL + (h + 1) * P] = 1.0
    return t


_INS = ["L0_attn_h", "L0_attn_Wq_c", "L0_attn_Wq_up", "L0_attn_Wk", "L0_attn_Wv", "L0_attn_W_comp",
        "L0_attn_q_norm_w", "L0_attn_k_norm_w", "L0_attn_sink", "L0_attn_Wg", "L0_attn_Wo",
        "L0_ffn_wq_gate", "L0_ffn_s_gate", "L0_ffn_wq_up", "L0_ffn_s_up", "L0_ffn_wq_down", "L0_ffn_s_down",
        "L0_c", "L0_wmod"]


def kernel(**inputs):
    import numpy as np
    import concourse.bacc as bacc
    from concourse.bass_utils import run_bass_kernel_spmd

    nc = bacc.Bacc("TRN2", target_bir_lowering=False, num_devices=1)
    arrays, args = {}, []
    for name, a in [(n, np.ascontiguousarray(inputs[n])) for n in _INS] + [("table", _table(np))]:
        arrays[f"in_{name}"] = a
        args.append(nc.dram_tensor(f"in_{name}", a.shape, mybir.dt.from_np(a.dtype), kind="ExternalInput").ap())
    out = nc.dram_tensor("out", (BATCH, SEQ, C), F32, kind="ExternalOutput").ap()
    build_program(nc, *args, out)
    r = run_bass_kernel_spmd(nc, [arrays], core_ids=[0])
    return r.results[0]["out"]
```

```python
from contextlib import ExitStack

import concourse.bass as bass
from concourse import mybir

F32 = mybir.dt.float32
F32R = mybir.dt.float32r
U32 = mybir.dt.uint32
I32 = mybir.dt.int32
ALU = mybir.AluOpType
ACT = mybir.ActivationFunctionType
AX = mybir.AxisListType

P = 128
BATCH, SEQ, C = 2, 1024, 512
KC = C // P
TILES = BATCH * SEQ // P
TPB = SEQ // P
CHUNK = 4
CHUNKS = TILES // CHUNK
W = CHUNK * P
H, D, M = 16, 128, 16
HALF = 32
NB = SEQ // M
HG = 4
GPT = H // HG
GROUPS = TILES * GPT
UNROLL = 2 * GPT
CAP = 50.0
SCALE = float(D) ** -0.5
INTER = 512
HID = 1408
HB = HID // P
EARLY = 5
ZERO_POINT = 128.0
LN_EPS, RMS_EPS = 1e-5, 1e-6

K_LOW, K_UP, K_CMASK = 0, P, 2 * P
K_SIGN = K_CMASK + TPB * NB
K_PERSIST = K_SIGN + 2
K_ROPE = K_PERSIST
K_IDENT = K_ROPE + TPB * P
K_SUMSEL = K_IDENT + P
K_ROWSEL = K_SUMSEL + HG * P
K_ALL = K_ROWSEL + HG * P


def since(value):
    return not isinstance(value, int) or value > 0


def token_rows(x, tile):
    rows = x[bass.ds(tile * P, P), :] if not isinstance(tile, int) else x[tile * P:(tile + 1) * P, :]
    return rows.rearrange("(n m) c -> m n c", m=M)


def build_program(nc, x_in, Wq_c, Wq_up, Wk, Wv, W_comp, q_w, k_w, sink, Wg, Wo,
                  wq_gate, s_gate, wq_up, s_up, wq_down, s_down, cond, wmod, table, out):
    with ExitStack() as whole:
        def sb(scope, name, shape, dt=F32):
            return scope.enter_context(nc.sbuf_tensor(name, shape, dt))

        bank = [whole.enter_context(nc.psum_tensor(f"bank{i}", [P, 512], F32)) for i in range(8)]
        x_mid = nc.dram_tensor("x_mid", [TILES * P, C], F32, kind="Internal").ap()
        dram = lambda name, shape: nc.dram_tensor(name, shape, F32, kind="Internal").ap()
        q_parts = dram("q_parts", [TILES, P, 2, P])
        k_parts = dram("k_parts", [BATCH * (TPB + 1), P, 2, P])
        v_parts = dram("v_parts", [TILES, P, 4, P])
        ck_parts = dram("ck_parts", [BATCH, P, 4, P])
        x_tok = x_in.rearrange("b t c -> (b t) c")
        out_tok = out.rearrange("b t c -> (b t) c")

        identity = sb(whole, "identity", [P, P])
        ident = identity[:]
        arena = sb(whole, "arena", [P, 2 * EARLY * C])
        raw_early = arena[:].bitcast(I32).rearrange("p (w h c) -> p w h c", w=2, h=EARLY)
        gate_in, up_in = (whole.enter_context(nc.semaphore(n)) for n in ("gate_in", "up_in"))
        xs_ffn = arena[:, 0:2 * CHUNK * C].rearrange("p (s t c) -> p s t c", s=2, t=CHUNK)
        xs_in = [whole.enter_context(nc.semaphore(f"xs_in{slot}")) for slot in range(2)]
        modT2 = sb(whole, "modT2", [P, 2 * KC, BATCH])
        row = sb(whole, "row", [P, BATCH, C])
        csil = sb(whole, "csil", [P, KC, BATCH])

        with ExitStack() as attn:
            kons = sb(attn, "kons", [P, K_PERSIST])
            low = kons[:, K_LOW:K_LOW + P]
            ckT = sb(attn, "ckT", [P, BATCH * NB])
            qw_col = sb(attn, "qw_col", [P, 1])
            sinkb = sb(attn, "sinkb", [P, H])
            sink_r = sb(attn, "sink_r", [P, GPT])
            sink_f = sb(attn, "sink_f", [P, GPT])
            sink_g = sb(attn, "sink_g", [P, GPT])

            with ExitStack() as scope:
                project_block(nc, scope, sb, bank, x_tok, Wq_c, Wk, Wv, W_comp, q_w, k_w, sink, cond,
                              wmod, table, kons, ident, csil, arena, q_parts, k_parts, v_parts, ck_parts, ckT,
                              qw_col, sinkb, sink_r, sink_f, sink_g)
            fold = sb(attn, "fold", [P, H, 2, C], F32R)
            ga = sb(attn, "ga", [P, BATCH, C])
            wup = sb(attn, "wup", [P, 2, H * D], F32R)
            sumsel = sb(attn, "sumsel", [P, HG, P], F32R)
            rowsel = sb(attn, "rowsel", [P, HG, P], F32R)
            with ExitStack() as scope:
                fold_block(nc, scope, sb, bank, Wg, Wo, wmod, Wq_up, table, csil, ident, fold, ga, wup, sumsel, rowsel,
                           s_down, modT2, row, arena)
            with ExitStack() as scope:
                attend_block(nc, scope, sb, bank, x_tok, x_mid, q_parts, k_parts, v_parts, ck_parts, table,
                             kons, ident, low, ckT, wup, fold, sumsel, rowsel, qw_col, sinkb, sink_f, sink_g, ga,
                             wq_gate, wq_up, raw_early, gate_in, up_in)
        with ExitStack() as scope:
            wT = sb(scope, "wT", [P, HB, 2, 2, KC, P], F32R)
            wd = sb(scope, "wd", [P, HB, 2, C], F32R)
            sg = sb(scope, "sg", [P, 2, HB])
            inexact = sb(scope, "inexact", [P, 1], I32)
            with ExitStack() as first:
                ffn_prepare(nc, first, sb, bank, wq_gate, wq_up, s_gate, s_up, wq_down, ident, raw_early, gate_in, up_in,
                            wT, wd, sg, inexact, x_mid, xs_ffn, xs_in)
            with ExitStack() as second:
                ffn_block(nc, second, sb, bank, x_mid, out_tok, ident, arena, xs_ffn, xs_in, wT, wd, sg, row, modT2,
                          inexact)


def semaphores(nc, scope, prefix=""):
    made = []

    def give_back():
        nc.clear_and_free_semaphores(made)
        nc.all_engine_barrier()
    scope.callback(give_back)

    def sem(name):
        made.append(nc.alloc_semaphore(prefix + name))
        return made[-1]
    return sem


def project_block(nc, scope, sb, bank, x_tok, Wq_c, Wk, Wv, W_comp, q_w, k_w, sink, cond, wmod, table,
                  kons, ident, csil, arena, q_parts, k_parts, v_parts, ck_parts, ckT, qw_col, sinkb, sink_r, sink_f, sink_g):
    sem = semaphores(nc, scope)
    KV = 2 * D
    STORES = 2 * 16
    RING = 4
    ccol = sb(scope, "ccol", [P, KC, BATCH])
    mod_w = sb(scope, "mod_w", [P, KC, C])
    modT = sb(scope, "modT", [P, 2 * KC, BATCH])
    raw_qc = sb(scope, "raw_qc", [P, KC, P])
    raw_kv = sb(scope, "raw_kv", [P, KC, KV])
    wqc = sb(scope, "wqc", [P, 2, KC, P], F32R)
    wkv = sb(scope, "wkv", [P, 2, KC, KV], F32R)
    xs = arena[:, 0:2 * CHUNK * C].rearrange("p (s t c) -> p s t c", s=2, t=CHUNK)
    stats = sb(scope, "stats", [P, CHUNK, 6])
    meanvar = sb(scope, "meanvar", [P, CHUNK, 2])
    rstd = sb(scope, "rstd", [P, CHUNK, 1])
    minus_half = sb(scope, "minus_half", [P, CHUNK])
    hfull = sb(scope, "hfull", [P, KC, W])
    hT = sb(scope, "hT", [P, 2, KC, TILES, P], F32R)
    ksq = sb(scope, "ksq", [P, P])
    kss = sb(scope, "kss", [P, CHUNK])
    kr = sb(scope, "kr", [P, CHUNK])
    kn = sb(scope, "kn", [P, 2, CHUNK, D])
    rope_all = sb(scope, "rope_all", [P, TPB * P])
    ropa = sb(scope, "ropa", [P, CHUNK, 2 * HALF])
    ropb = sb(scope, "ropb", [P, CHUNK, 2 * HALF])
    kw_col = sb(scope, "kw_col", [P, 1])
    kw_row = sb(scope, "kw_row", [P, D])
    comp_raw = sb(scope, "comp_raw", [P, RING, KC, D])
    comp_w = sb(scope, "comp_w", [P, RING, 2, KC, D], F32R)
    ck_raw = sb(scope, "ck_raw", [P, P])
    ck_nd = sb(scope, "ck_nd", [P, D])
    ck_dup = sb(scope, "ck_dup", [P, BATCH, 2, NB])
    cs1 = sb(scope, "cs1", [P, 2])
    q_out = sb(scope, "q_out", [P, CHUNK, 2, P], F32R)
    k_out = sb(scope, "k_out", [P, CHUNK, 2, P], F32R)
    v_out = sb(scope, "v_out", [P, CHUNK, 2, 2, P], F32R)
    v32 = sb(scope, "v32", [P, BATCH * (TPB + 1), P])
    v_less = sb(scope, "v_less", [P, CHUNK, P])
    zeros = sb(scope, "zeros", [P, 2, P], F32R)
    ck_pad = sb(scope, "ck_pad", [P, BATCH, 2, 2, P], F32R)

    table_in, cond_in, w_in, mod_in, small_in = map(sem, (
        "table_in", "cond_in", "w_in", "mod_in", "small_in"))
    x_even, x_odd = sem("x_even"), sem("x_odd")
    comp_in = [sem(f"comp_in{r}") for r in range(RING)]
    zeroed, w_split, csil_done, mod_mm, mod_done = map(sem, (
        "zeroed", "w_split", "csil_done", "mod_mm", "mod_done"))
    sink_steps, stats_done, var_done, rstd_done, z_done, hT_mm, h_hi, h_lo = map(sem, (
        "sink_steps", "stats_done", "var_done", "rstd_done", "z_done", "hT_mm", "h_hi", "h_lo"))
    qc_mm, kv_mm, v_copied, k_sq, k_rs, k_scaled, k_rope1, k_rope, kT_mm = map(sem, (
        "qc_mm", "kv_mm", "v_copied", "k_sq", "k_rs", "k_scaled", "k_rope1", "k_rope", "kT_mm"))
    q_hi, q_lo, k_hi, k_lo, v_hi, v_lo, v_diff, v_dhi, v_dlo, stored, k_stored, zero_stored = map(sem, (
        "q_hi", "q_lo", "k_hi", "k_lo", "v_hi", "v_lo", "v_diff", "v_dhi", "v_dlo", "stored", "k_stored", "zero_stored"))
    comp_hi, comp_lo, comp_mm, ck_act, ck_sum, ck_pe, ck_dve, ck_pool = map(sem, (
        "comp_hi", "comp_lo", "comp_mm", "ck_act", "ck_sum", "ck_pe", "ck_dve", "ck_pool"))
    block = scope.enter_context(nc.Block())

    shift_w = comp_raw[:].rearrange("p r k d -> p (r k d)").rearrange("p (k n) -> p k n", k=KC)
    comp_view = W_comp.rearrange("(m k p) d -> m p k d", m=M, p=P)

    @block.sync
    def _(sp):
        def load_x(c):
            slot = c % 2
            if c >= 2:
                sp.wait_ge(hT_mm, c - 1)
            for t in range(CHUNK):
                sp.dma_start(xs[:, slot, t], token_rows(x_tok, c * CHUNK + t)).then_inc((x_even, x_odd)[slot], 16)

        def store_query_value(c):
            tiles = slice(c * CHUNK, (c + 1) * CHUNK)
            sp.wait_ge(q_lo, c + 1)
            sp.dma_start(q_parts[tiles].rearrange("t p a n -> p t a n"), q_out[:].bitcast(F32)).then_inc(stored, 16)
            sp.wait_ge(v_dlo, c + 1)
            sp.wait_ge(v_lo, c + 1)
            sp.dma_start(v_parts[tiles].rearrange("t p a n -> p t a n"), v_out[:].rearrange("p t a b n -> p t (a b) n").bitcast(F32)
                         ).then_inc(stored, 16)

        def store_key(c, b):
            sp.wait_ge(k_lo, c + 1)
            sp.dma_start(k_parts[c * CHUNK + b + 1:(c + 1) * CHUNK + b + 1].rearrange("t p a n -> p t a n"), k_out[:].bitcast(F32)
                         ).then_inc(k_stored, 16)

        for b in range(BATCH):
            sp.dma_start(ccol[:, :, b], cond[b].rearrange("(k p) -> p k", p=P), allow_slow_non_contiguous=True
                         ).then_inc(cond_in, 16)
        load_x(0)
        for n, place in enumerate((shift_w, mod_w[:])):
            sp.dma_start(place, wmod[:, n * C:(n + 1) * C].rearrange("(k p) n -> p k n", p=P)).then_inc(mod_in, 16)
        load_x(1)
        sp.wait_ge(zeroed, 1)
        for b in range(BATCH):
            sp.dma_start(k_parts[b * (TPB + 1)], zeros[:].bitcast(F32)).then_inc(zero_stored, 16)
        sp.wait_ge(mod_mm, 1)
        for m in range(RING):
            sp.dma_start(comp_raw[:, m], comp_view[m]).then_inc(comp_in[m], 16)
        for c in range(2, CHUNKS):
            load_x(c)
        for c in range(CHUNKS + 1):
            if c < CHUNKS:
                store_query_value(c)
            if c:
                store_key(c - 1, (c - 1) // (CHUNKS // BATCH))
        with sp.Fori(1, M // RING) as r:
            for s in range(RING):
                sp.wait_ge(comp_lo, RING * r + (s - RING + 1))
                sp.dma_start(comp_raw[:, s],
                             W_comp[bass.ds(r * (RING * C) + s * C, C), :].rearrange("(k p) d -> p k d", p=P)
                             ).then_inc(comp_in[s], 16)
        sp.wait_ge(ck_act, 5)
        sp.wait_ge(ck_dve, 3)
        sp.dma_start(ck_parts.rearrange("b p a n -> p b a n"), ck_pad[:].rearrange("p b h a n -> p b (h a) n").bitcast(F32)
                     ).then_inc(zero_stored, 16)
        sp.wait_ge(zero_stored, 16 * (BATCH + 1))
        sp.wait_ge(stored, STORES * CHUNKS)
        sp.wait_ge(k_stored, 16 * CHUNKS)

    @block.scalar
    def _(act):
        act.dma_start(kons[:], table[:, 0:K_PERSIST]).then_inc(table_in, 16)
        act.dma_start(ident, table[:, K_IDENT:K_IDENT + P]).then_inc(table_in, 16)
        act.dma_start(rope_all[:], table[:, K_ROPE:K_ROPE + TPB * P]).then_inc(table_in, 16)
        act.dma_start(raw_qc[:], Wq_c.rearrange("(k p) n -> p k n", p=P)).then_inc(w_in, 16)
        act.dma_start(raw_kv[:, :, 0:D], Wk.rearrange("(k p) n -> p k n", p=P)).then_inc(w_in, 16)
        act.dma_start(raw_kv[:, :, D:KV], Wv.rearrange("(k p) n -> p k n", p=P)).then_inc(w_in, 16)
        act.dma_start(qw_col[:], q_w.rearrange("(p a) -> p a", a=1)).then_inc(small_in, 16)
        act.dma_start(kw_col[:], k_w.rearrange("(p a) -> p a", a=1)).then_inc(small_in, 16)
        act.dma_start(kw_row[:], k_w.partition_broadcast(P)).then_inc(small_in, 16)
        act.dma_start(sinkb[:], sink.partition_broadcast(P)).then_inc(small_in, 16)
        for h in range(HG):
            act.dma_start(sink_r[32 * h:32 * h + 32, :],
                          sink.rearrange("(g h) -> h g", h=HG)[h].partition_broadcast(32),
                          allow_slow_non_contiguous=True).then_inc(small_in, 16)

        act.wait_ge(cond_in, 16 * BATCH)
        act.activation(csil[:], ccol[:], ACT.Silu).then_inc(csil_done, 1)
        act.wait_ge(sink_steps, 2)
        act.activation(sink_f[:], sink_f[:], ACT.Exp, scale=-1.0).then_inc(sink_steps, 1)
        act.activation(sink_g[:], sink_g[:], ACT.Exp).then_inc(sink_steps, 1)
        act.wait_ge(mod_mm, 1)
        act.activation(modT[:, 0:KC], bank[7][:, 0:2 * KC].rearrange("p (k b) -> p k b", b=BATCH),
                       ACT.Copy).then_inc(mod_done, 1)
        act.activation(modT[:, KC:2 * KC], bank[7][:, 2 * KC:4 * KC].rearrange("p (k b) -> p k b", b=BATCH),
                       ACT.Identity, bias=1.0).then_inc(mod_done, 1)
        act.wait_ge(mod_done, 2)

        def channels(c, b):
            act.wait_ge(hT_mm, c + 1)
            for k in range(KC):
                if c:
                    act.wait_ge(h_lo, KC * (c - 1) + k + 1)
                for out in (hT[:, 0, k, c * CHUNK:(c + 1) * CHUNK].rearrange("p t n -> p (t n)"), hfull[:, k]):
                    act.activation(out, bank[k][:], ACT.Identity, scale=modT[:, KC + k, b:b + 1],
                                   bias=modT[:, k, b:b + 1]).then_inc(h_hi, 1)

        def query_key_value(c, b):
            act.wait_ge(qc_mm, c + 1)
            if since(c):
                act.wait_ge(stored, STORES * c)
            act.activation(q_out[:, :, 0], bank[4][:].rearrange("p (t n) -> p t n", t=CHUNK), ACT.Copy).then_inc(q_hi, 1)
            act.wait_ge(kv_mm, c + 1)
            if since(c):
                act.wait_ge(k_rs, 2 * c)
            for t in range(CHUNK):
                act.activation(ksq[:], bank[5 + t // 2][:, (t % 2) * KV:(t % 2) * KV + D], ACT.Square,
                               accum_out=kss[:, t:t + 1]).then_inc(k_sq, 1)
                act.wait_ge(k_sq, CHUNK * c + t + 1)
            for t in range(CHUNK):
                last = act.activation(v32[:, bass.ds(c * CHUNK + b + 1 + t, 1), :],
                                      bank[5 + t // 2][:, (t % 2) * KV + D:(t % 2 + 1) * KV].unsqueeze(1), ACT.Copy)
            last.then_inc(v_copied, 1)
            act.wait_ge(v_copied, c + 1)
            act.activation(v_out[:, :, 0, 0], v32[:, c * CHUNK + b:(c + 1) * CHUNK + b], ACT.Copy).then_inc(v_hi, 1)
            act.wait_ge(v_diff, c + 1)
            act.activation(v_out[:, :, 1, 0], v_less[:], ACT.Copy).then_inc(v_dhi, 1)

        def key(c):
            act.wait_ge(kT_mm, c + 1)
            if c:
                act.wait_ge(k_stored, 16 * c)
            act.activation(k_out[:, :, 0], bank[7][:].rearrange("p (t n) -> p t n", t=CHUNK),
                           ACT.Copy, scale=kw_col[:, 0:1]).then_inc(k_hi, 1)

        act.wait_ge(small_in, 16 * 8)
        act.wait_ge(zeroed, 3)
        for i in range(CHUNKS + 1):
            if i < CHUNKS:
                channels(i, i // (CHUNKS // BATCH))
            if i >= 1:
                query_key_value(i - 1, (i - 1) // (CHUNKS // BATCH))
            if i >= 2:
                key(i - 2)
        def comp(r):
            for s in range(RING):
                act.wait_ge(comp_in[s], 16 * r + 16)
                if since(r):
                    act.wait_ge(comp_mm, RING * r + (s - RING + 1))
                act.activation(comp_w[:, s, 0], comp_raw[:, s], ACT.Copy).then_inc(comp_hi, 1)
        comp(0)
        key(CHUNKS - 1)
        with act.Fori(1, M // RING) as r:
            comp(r)
        act.wait_ge(comp_mm, M)
        act.activation(ck_raw[:], bank[0][:, 0:P], ACT.Copy).then_inc(ck_act, 1)
        act.wait_ge(ck_pe, 1)
        act.activation(ksq[:], bank[1][:, 0:P], ACT.Square, accum_out=cs1[:, 0:1]).then_inc(ck_act, 1)
        act.wait_ge(ck_pe, 2)
        act.activation(ckT[:], bank[2][:, 0:P], ACT.Copy).then_inc(ck_act, 1)
        act.wait_ge(ck_act, 3)
        for b in range(BATCH):
            for half in range(2):
                last = act.activation(ck_dup[:, b, half], ckT[:, b * NB:(b + 1) * NB], ACT.Copy)
        last.then_inc(ck_act, 1)
        act.wait_ge(ck_pe, 3)
        for b in range(BATCH):
            for half in range(2):
                rows = slice(half * NB, (half + 1) * NB)
                last = act.activation(ck_pad[rows, b, half, 0], bank[3][rows, b * P:(b + 1) * P], ACT.Copy)
        last.then_inc(ck_act, 1)

    @block.vector
    def _(dve):
        dve.memset(zeros[:].bitcast(F32), 0.0).then_inc(zeroed, 1)
        dve.memset(v32[:, 0:BATCH * (TPB + 1):TPB + 1], 0.0).then_inc(zeroed, 1)
        dve.memset(ck_pad[:].bitcast(F32), 0.0).then_inc(zeroed, 1)
        dve.memset(minus_half[:], -0.5).then_inc(zeroed, 1)
        def normal(c):
            slot = c % 2
            dve.wait_ge((x_even, x_odd)[slot], 16 * CHUNK * (c // 2 + 1))
            if since(c):
                dve.wait_ge(rstd_done, 2 * c)
            for t in range(CHUNK):
                dve.bn_stats(stats[:, t], xs[:, slot, t]).then_inc(stats_done, 1)
            for t in range(CHUNK):
                dve.wait_ge(stats_done, CHUNK * c + t + 1)
                dve.bn_aggr(meanvar[:, t], stats[:, t]).then_inc(var_done, 1)
            dve.wait_ge(var_done, CHUNK * (c + 1))
            dve.wait_ge(rstd_done, 2 * (c + 1))
            for t in range(CHUNK):
                dve.tensor_scalar(xs[:, slot, t], xs[:, slot, t], meanvar[:, t, 0:1], rstd[:, t, 0:1],
                                  ALU.subtract, ALU.mult).then_inc(z_done, 1)

        def channels_low(c):
            for k in range(KC):
                dve.wait_ge(h_hi, 2 * (KC * c + k) + 2)
                at = hT[:, :, k, c * CHUNK:(c + 1) * CHUNK].rearrange("p a t n -> p a (t n)")
                dve.tensor_tensor(at[:, 1], hfull[:, k], at[:, 0].bitcast(F32), ALU.subtract).then_inc(h_lo, 1)

        def query_key_value(c, b):
            dve.wait_ge(q_hi, c + 1)
            dve.tensor_tensor(q_out[:, :, 1], bank[4][:].rearrange("p (t n) -> p t n", t=CHUNK),
                              q_out[:, :, 0].bitcast(F32), ALU.subtract).then_inc(q_lo, 1)
            dve.wait_ge(k_rs, 2 * (c + 1))
            dve.wait_ge(v_copied, c + 1)
            if c >= 2:
                dve.wait_ge(kT_mm, c - 1)
            for t in range(CHUNK):
                last = dve.tensor_scalar(kn[:, c % 2, t], bank[5 + t // 2][:, (t % 2) * KV:(t % 2) * KV + D],
                                         kr[:, t:t + 1], None, ALU.mult)
            last.then_inc(k_scaled, 1)
            dve.wait_ge(v_hi, c + 1)
            dve.tensor_tensor(v_out[:, :, 0, 1], v32[:, c * CHUNK + b:(c + 1) * CHUNK + b],
                              v_out[:, :, 0, 0].bitcast(F32), ALU.subtract).then_inc(v_lo, 1)
            dve.wait_ge(v_dhi, c + 1)
            dve.tensor_tensor(v_out[:, :, 1, 1], v_less[:], v_out[:, :, 1, 0].bitcast(F32),
                              ALU.subtract).then_inc(v_dlo, 1)

        def key(c):
            dve.wait_ge(k_hi, c + 1)
            dve.scalar_tensor_tensor(k_out[:, :, 1], bank[7][:].rearrange("p (t n) -> p t n", t=CHUNK), kw_col[:, 0:1],
                                     k_out[:, :, 0].bitcast(F32), ALU.mult, ALU.subtract).then_inc(k_lo, 1)

        dve.wait_ge(zeroed, 4)
        normal(0)
        dve.wait_ge(w_in, 48)
        dve.tensor_copy(wqc[:, 0], raw_qc[:]).then_inc(w_split, 1)
        dve.tensor_copy(wkv[:, 0], raw_kv[:]).then_inc(w_split, 1)
        dve.wait_ge(w_split, 2)
        dve.tensor_tensor(wqc[:, 1], raw_qc[:], wqc[:, 0].bitcast(F32), ALU.subtract).then_inc(w_split, 1)
        dve.tensor_tensor(wkv[:, 1], raw_kv[:], wkv[:, 0].bitcast(F32), ALU.subtract).then_inc(w_split, 1)
        dve.wait_ge(small_in, 16 * 8)
        dve.tensor_scalar(sink_f[:], sink_r[:], 0.0, None, ALU.max).then_inc(sink_steps, 1)
        dve.wait_ge(sink_steps, 1)
        dve.tensor_tensor(sink_g[:], sink_r[:], sink_f[:], ALU.subtract).then_inc(sink_steps, 1)

        for i in range(CHUNKS + 1):
            if i + 1 < CHUNKS:
                normal(i + 1)
            if i < CHUNKS:
                channels_low(i)
            if i >= 1:
                query_key_value(i - 1, (i - 1) // (CHUNKS // BATCH))
            if i >= 2:
                key(i - 2)

        def comp(r):
            for s in range(RING):
                dve.wait_ge(comp_hi, RING * r + (s + 1))
                dve.tensor_tensor(comp_w[:, s, 1], comp_raw[:, s], comp_w[:, s, 0].bitcast(F32),
                                  ALU.subtract).then_inc(comp_lo, 1)
        comp(0)
        key(CHUNKS - 1)
        with dve.Fori(1, M // RING) as r:
            comp(r)
        dve.wait_ge(ck_act, 1)
        dve.tensor_tensor(ck_raw[:], ck_raw[:], bank[0][:, P:2 * P], ALU.add).then_inc(ck_sum, 1)
        dve.wait_ge(ck_pool, 2)
        dve.tensor_scalar(ck_nd[:], bank[1][:, 0:P], cs1[:, 1:2], None, ALU.mult).then_inc(ck_dve, 1)
        dve.wait_ge(ck_dve, 1)
        dve.tensor_tensor(ck_nd[:], ck_nd[:], kw_row[:], ALU.mult).then_inc(ck_dve, 1)
        dve.wait_ge(ck_act, 5)
        for b in range(BATCH):
            for half in range(2):
                rows = slice(half * NB, (half + 1) * NB)
                last = dve.tensor_tensor(ck_pad[rows, b, half, 1], bank[3][rows, b * P:(b + 1) * P],
                                         ck_pad[rows, b, half, 0].bitcast(F32), ALU.subtract)
        last.then_inc(ck_dve, 1)

    @block.gpsimd
    def _(pool):
        pool.wait_ge(zeroed, 4)
        pool.wait_ge(table_in, 48)

        def inverse_deviation(c):
            pool.wait_ge(var_done, CHUNK * (c + 1))
            if since(c):
                pool.wait_ge(z_done, CHUNK * c)
            pool.tensor_scalar(rstd[:, :, 0], meanvar[:, :, 1], 1.0, LN_EPS, ALU.mult, ALU.add).then_inc(rstd_done, 1)
            pool.wait_ge(rstd_done, 2 * c + 1)
            pool.tensor_tensor(rstd[:, :, 0], rstd[:, :, 0], minus_half[:], ALU.pow).then_inc(rstd_done, 1)

        def key_value(c, b):
            pool.wait_ge(k_sq, CHUNK * (c + 1))
            if since(c):
                pool.wait_ge(k_scaled, c)
            pool.tensor_scalar(kr[:], kss[:], 1.0 / D, RMS_EPS, ALU.mult, ALU.add).then_inc(k_rs, 1)
            pool.wait_ge(k_rs, 2 * c + 1)
            pool.tensor_tensor(kr[:], kr[:], minus_half[:], ALU.pow).then_inc(k_rs, 1)
            pool.wait_ge(v_copied, c + 1)
            if since(c):
                pool.wait_ge(v_dlo, c)
            pool.tensor_tensor(v_less[:], v32[:, c * CHUNK + b + 1:(c + 1) * CHUNK + b + 1],
                               v32[:, c * CHUNK + b:(c + 1) * CHUNK + b], ALU.subtract).then_inc(v_diff, 1)
            pool.wait_ge(k_scaled, c + 1)
            tile0 = (c % (TPB // CHUNK)) * CHUNK
            rope = rope_all[:, tile0 * P:(tile0 + CHUNK) * P].rearrange("p (t n) -> p t n", n=P)
            x = kn[:, c % 2]
            pool.tensor_tensor(ropa[:], x[:, :, 0:2 * HALF], rope[:, :, 0:2 * HALF], ALU.mult).then_inc(k_rope1, 1)
            pool.tensor_tensor(ropb[:, :, 0:HALF], x[:, :, HALF:2 * HALF],
                               rope[:, :, 2 * HALF:3 * HALF], ALU.mult).then_inc(k_rope1, 1)
            pool.tensor_tensor(ropb[:, :, HALF:], x[:, :, 0:HALF], rope[:, :, 3 * HALF:], ALU.mult).then_inc(k_rope1, 1)
            pool.wait_ge(k_rope1, 3 * c + 3)
            pool.tensor_tensor(x[:, :, 0:2 * HALF], ropa[:], ropb[:], ALU.add).then_inc(k_rope, 1)

        inverse_deviation(0)
        for i in range(CHUNKS + 1):
            if i + 1 < CHUNKS:
                inverse_deviation(i + 1)
            if i >= 1:
                key_value(i - 1, (i - 1) // (CHUNKS // BATCH))
        pool.wait_ge(ck_act, 2)
        pool.tensor_scalar(cs1[:, 1:2], cs1[:, 0:1], 1.0 / D, RMS_EPS, ALU.mult, ALU.add).then_inc(ck_pool, 1)
        pool.wait_ge(ck_pool, 1)
        pool.tensor_tensor(cs1[:, 1:2], cs1[:, 1:2], minus_half[:, 0:1], ALU.pow).then_inc(ck_pool, 1)

    @block.tensor
    def _(pe):
        pe.wait_ge(mod_in, 32)
        pe.wait_ge(csil_done, 1)
        for n in range(2 * KC):
            for k in range(KC):
                cols = (shift_w, mod_w[:])[n // KC][:, k, (n % KC) * P:(n % KC + 1) * P]
                last = pe.matmul(bank[7][:, 2 * n:2 * n + 2], cols, csil[:, k],
                                 start=(k == 0), stop=(k == KC - 1))
        last.then_inc(mod_mm, 1)
        pe.wait_ge(table_in, 48)

        def transpose(c):
            pe.wait_ge(z_done, CHUNK * (c + 1))
            if since(c):
                pe.wait_ge(h_hi, 2 * KC * c)
            for k in range(KC):
                for t in range(CHUNK):
                    last = pe.transpose(bank[k][:, t * P:(t + 1) * P], xs[:, c % 2, t, k * P:(k + 1) * P], ident)
            last.then_inc(hT_mm, 1)

        def query_key_value(c):
            pe.wait_ge(h_lo, KC * (c + 1))
            pe.wait_ge(w_split, 4)
            if since(c):
                pe.wait_ge(q_lo, c)
            for k in range(KC):
                for n, (a, b) in enumerate(((0, 0), (0, 1), (1, 0))):
                    last = pe.matmul(bank[4][:], wqc[:, a, k],
                                     hT[:, b, k, c * CHUNK:(c + 1) * CHUNK].rearrange("p t n -> p (t n)"),
                                     start=(k == 0 and n == 0), stop=(k == KC - 1 and n == 2))
            last.then_inc(qc_mm, 1)
            if since(c):
                pe.wait_ge(k_scaled, c)
                pe.wait_ge(v_copied, c)
            for t in range(CHUNK):
                for k in range(KC):
                    for n, (a, b) in enumerate(((0, 0), (0, 1), (1, 0))):
                        last = pe.matmul(bank[5 + t // 2][:, (t % 2) * KV:(t % 2 + 1) * KV],
                                         hT[:, a, k, c * CHUNK + t], wkv[:, b, k],
                                         start=(k == 0 and n == 0), stop=(k == KC - 1 and n == 2))
            last.then_inc(kv_mm, 1)

        def key(c):
            pe.wait_ge(k_rope, c + 1)
            if c == 0:
                pe.wait_ge(mod_done, 2)
            else:
                pe.wait_ge(k_lo, c)
            for t in range(CHUNK):
                last = pe.transpose(bank[7][:, t * P:(t + 1) * P], kn[:, c % 2, t], ident)
            last.then_inc(kT_mm, 1)

        for i in range(CHUNKS + 1):
            if i < CHUNKS:
                transpose(i)
            if i >= 1:
                query_key_value(i - 1)
            if i >= 2:
                key(i - 2)

        pe.wait_ge(h_lo, KC * CHUNKS)
        PER = P // M

        def comp(r, first, final):
            for s in range(RING):
                pe.wait_ge(comp_lo, RING * r + (s + 1))
                at = bass.ds((r * RING + s) * PER, PER)
                for k in range(KC):
                    pe.matmul(bank[0][:, 0:2 * P].rearrange("p (a t n) -> p a t n", a=2, n=PER), comp_w[:, s, 0, k],
                              hT[:, :, k, :, at], start=first and s == 0 and k == 0, stop=False)
                    last = pe.matmul(bank[0][:, 0:P], comp_w[:, s, 1, k], hT[:, 0, k, :, at], start=False,
                                     stop=final and s == RING - 1 and k == KC - 1)
                last.then_inc(comp_mm, 1)
        comp(0, True, False)
        key(CHUNKS - 1)
        with pe.Fori(1, M // RING - 1) as r:
            comp(r, False, False)
        comp(M // RING - 1, False, True)
        pe.wait_ge(ck_sum, 1)
        pe.transpose(bank[1][:, 0:P], ck_raw[:], ident).then_inc(ck_pe, 1)
        pe.wait_ge(ck_dve, 2)
        pe.transpose(bank[2][:, 0:P], ck_nd[:], ident).then_inc(ck_pe, 1)
        pe.wait_ge(ck_act, 4)
        for b in range(BATCH):
            last = pe.transpose(bank[3][:, b * P:(b + 1) * P], ck_dup[:, b].rearrange("p h n -> p (h n)"), ident)
        last.then_inc(ck_pe, 1)


def fold_block(nc, scope, sb, bank, Wg, Wo, wmod, Wq_up, table, csil, ident, fold, ga, wup, sumsel, rowsel,
               s_down, modT2, row, arena):
    sem = semaphores(nc, scope)
    G = H // HG
    IK = INTER // P
    raw_g = sb(scope, "raw_g", [P, HG, INTER])
    raw_o = sb(scope, "raw_o", [P, IK, C])
    wgT = sb(scope, "wgT", [P, 2, 2, IK, HG * D], F32R)
    wo = sb(scope, "wo", [P, 2, 2, IK, C], F32R)
    TWO = 2 * KC * C
    silu_rows = arena[:, TWO:TWO + BATCH * KC * P].rearrange("p (b k n) -> p b k n", b=BATCH, k=KC)
    mod_two = arena[:, 0:TWO].rearrange("p (n k c) -> p n k c", n=2, k=KC)
    mod_w = [mod_two[:, 0], mod_two[:, 1], raw_g[:], raw_o[:]]
    raw_up = sb(scope, "raw_up", [P, H * D])
    sign, mag, sdrow, selraw = (raw_up[:, n * C:(n + 1) * C] for n in range(4))
    g_in, o_in, m_in, gT_mm, gT_hi, gT_lo, o_hi, o_lo, f_mm, f_hi, f_lo, mod_mm, mod_step, rows_done = map(sem, (
        "g_in", "o_in", "m_in", "gT_mm", "gT_hi", "gT_lo", "o_hi", "o_lo", "f_mm", "f_hi", "f_lo", "gmod_mm",
        "gmod_step", "rows_done"))
    up_in, sel_in, sel_done, up_hi, up_lo, row_step = map(sem, (
        "wup_in", "sel_in", "sel_done", "up_hi", "up_lo", "row_step"))
    block = scope.enter_context(nc.Block())
    wg_rows = Wg.rearrange("g f i -> (g f) i")

    @block.sync
    def _(sp):
        def load_mod(n):
            sp.dma_start(mod_w[n], wmod[:, (2 + n) * C:(3 + n) * C].rearrange("(k p) n -> p k n", p=P)).then_inc(m_in, 16)

        for g in range(G):
            if g:
                sp.wait_ge(o_lo, g)
            sp.dma_start(raw_o[:], Wo[g * INTER:(g + 1) * INTER, :].rearrange("(k p) n -> p k n", p=P)).then_inc(o_in, 16)
            if g:
                sp.wait_ge(gT_mm, g)
            sp.dma_start(raw_g[:], wg_rows[g * HG * D:(g + 1) * HG * D, :].rearrange("(k p) i -> p k i", p=P)
                         ).then_inc(g_in, 16)
            if g == 0:
                sp.dma_start(raw_up[:], Wq_up).then_inc(up_in, 16)
            elif g < 3:
                load_mod(g - 1)
        sp.wait_ge(gT_mm, G)
        load_mod(2)
        sp.wait_ge(o_lo, G)
        load_mod(3)
        sp.wait_ge(up_lo, 1)
        sp.dma_start(sdrow, s_down.partition_broadcast(P)).then_inc(m_in, 16)
        sp.dma_start(selraw, table[:, K_SUMSEL:K_ROWSEL]).then_inc(sel_in, 16)
        sp.wait_ge(sel_done, 1)
        sp.dma_start(selraw, table[:, K_ROWSEL:K_ALL]).then_inc(sel_in, 16)

    @block.tensor
    def _(pe):
        def transpose(g):
            pe.wait_ge(g_in, 16 * (g + 1))
            if g:
                pe.wait_ge(gT_lo, g)
            for i in range(IK):
                for f in range(HG):
                    last = pe.transpose(bank[i][:, f * P:(f + 1) * P], raw_g[:, f, i * P:(i + 1) * P], ident)
            last.then_inc(gT_mm, 1)

        transpose(0)
        for g in range(G):
            pe.wait_ge(gT_lo, g + 1)
            pe.wait_ge(o_lo, g + 1)
            for f in range(HG):
                if f == HG - 1 and g + 1 < G:
                    transpose(g + 1)
                if g:
                    pe.wait_ge(f_lo, HG * (g - 1) + f + 1)
                for i in range(IK):
                    for n, (a, b) in enumerate(((0, 0), (0, 1), (1, 0))):
                        last = pe.matmul(bank[4 + f][:], wgT[:, g % 2, a, i, f * P:(f + 1) * P], wo[:, g % 2, b, i],
                                         start=(i == 0 and n == 0), stop=(i == IK - 1 and n == 2))
                last.then_inc(f_mm, 1)
        pe.wait_ge(m_in, 5 * 16)
        pe.wait_ge(rows_done, 1)
        pe.wait_ge(gT_lo, G)
        for n, where in ((0, bank[0:2]), (3, bank[2:4])):
            for b in range(BATCH):
                for k in range(KC):
                    last = pe.matmul(where[b][:], silu_rows[:, b, k], mod_w[n][:, k], start=(k == 0), stop=(k == KC - 1))
            last.then_inc(mod_mm, 1)
        pe.wait_ge(f_lo, HG * (G - 1) + 1)
        for q in range(2 * KC):
            for k in range(KC):
                cols = mod_w[1 + q // KC][:, k, (q % KC) * P:(q % KC + 1) * P]
                last = pe.matmul(bank[4][:, 2 * q:2 * q + 2], cols, csil[:, k], start=(k == 0), stop=(k == KC - 1))
        last.then_inc(mod_mm, 1)

    @block.scalar
    def _(act):
        def wg_high(g):
            act.wait_ge(gT_mm, g + 1)
            if g >= 2:
                act.wait_ge(f_mm, HG * (g - 1))
            for i in range(IK):
                act.activation(wgT[:, g % 2, 0, i], bank[i][:], ACT.Copy).then_inc(gT_hi, 1)

        def wo_high(g):
            act.wait_ge(o_in, 16 * (g + 1))
            if g >= 2:
                act.wait_ge(f_mm, HG * (g - 1))
            act.activation(wo[:, g % 2, 0], raw_o[:], ACT.Copy).then_inc(o_hi, 1)

        repeat_rows(act, csil, silu_rows, rows_done)
        wo_high(0)
        wg_high(0)
        act.wait_ge(up_in, 16)
        act.activation(wup[:, 0], raw_up[:], ACT.Copy).then_inc(up_hi, 1)
        for g in range(G):
            for f in range(HG):
                if f == 1 and g + 1 < G:
                    wo_high(g + 1)
                if f == HG - 1 and g + 1 < G:
                    wg_high(g + 1)
                act.wait_ge(f_mm, HG * g + (f + 1))
                act.activation(fold[:, g * HG + f, 0], bank[4 + f][:], ACT.Copy).then_inc(f_hi, 1)
        act.wait_ge(mod_mm, 3)
        act.activation(modT2[:, 0:KC], bank[4][:, 0:2 * KC].rearrange("p (k b) -> p k b", b=BATCH), ACT.Copy)
        act.activation(modT2[:, KC:2 * KC], bank[4][:, 2 * KC:4 * KC].rearrange("p (k b) -> p k b", b=BATCH),
                       ACT.Identity, bias=1.0)

    @block.vector
    def _(dve):
        def wg_low(g):
            for i in range(IK):
                dve.wait_ge(gT_hi, IK * g + (i + 1))
                last = dve.tensor_tensor(wgT[:, g % 2, 1, i], bank[i][:], wgT[:, g % 2, 0, i].bitcast(F32), ALU.subtract)
            last.then_inc(gT_lo, 1)

        wg_low(0)
        dve.wait_ge(up_hi, 1)
        dve.tensor_tensor(wup[:, 1], raw_up[:], wup[:, 0].bitcast(F32), ALU.subtract).then_inc(up_lo, 1)
        for g in range(G):
            for f in range(HG):
                if f == HG - 1 and g + 1 < G:
                    wg_low(g + 1)
                dve.wait_ge(f_hi, HG * g + (f + 1))
                dve.tensor_tensor(fold[:, g * HG + f, 1], bank[4 + f][:], fold[:, g * HG + f, 0].bitcast(F32),
                                  ALU.subtract).then_inc(f_lo, 1)
        dve.wait_ge(up_lo, 1)
        dve.wait_ge(mod_mm, 1)
        gate_steps(dve, bank[0:2], sign, mag, ga, mod_step)
        dve.wait_ge(mod_mm, 2)
        gate_steps(dve, bank[2:4], sign, mag, row, row_step)
        dve.wait_ge(m_in, 5 * 16)
        for b in range(BATCH):
            dve.tensor_tensor(row[:, b], row[:, b], sdrow, ALU.mult)

    @block.gpsimd
    def _(pool):
        for g in range(G):
            pool.wait_ge(o_hi, g + 1)
            pool.tensor_tensor(wo[:, g % 2, 1], raw_o[:], wo[:, g % 2, 0].bitcast(F32), ALU.subtract).then_inc(o_lo, 1)
        for n, selector in enumerate((sumsel, rowsel)):
            pool.wait_ge(sel_in, 16 * (n + 1))
            pool.tensor_copy(selector[:].rearrange("p h n -> p (h n)"), selraw).then_inc(sel_done, 1)


def repeat_rows(act, csil, silu_rows, done):
    for b in range(BATCH):
        last = act.activation(silu_rows[:, b], csil[:, :, b:b + 1].broadcast_to([P, KC, P]), ACT.Copy)
    last.then_inc(done, 1)


def gate_steps(dve, bank, sign, mag, gate, step):
    for b in range(BATCH):
        dve.tensor_scalar(sign, bank[b][:], 0.0, 2.0, ALU.is_ge, ALU.mult).then_inc(step, 1)
        dve.tensor_scalar(mag, bank[b][:], -1.0, None, ALU.mult).then_inc(step, 1)
        dve.wait_ge(step, 5 * b + 2)
        dve.tensor_scalar(sign, sign, -1.0, None, ALU.add).then_inc(step, 1)
        dve.scalar_tensor_tensor(mag, bank[b][:], 0.25, mag, ALU.max, ALU.max).then_inc(step, 1)
        dve.wait_ge(step, 5 * b + 4)
        dve.tensor_tensor(gate[:, b], sign, mag, ALU.mult).then_inc(step, 1)
        dve.wait_ge(step, 5 * b + 5)


def attend_block(nc, scope, sb, bank, x_tok, x_mid, q_parts, k_parts, v_parts, ck_parts, table, kons, ident, low,
                 ckT, wup, fold, sumsel, rowsel, qw_col, sinkb, sink_f, sink_g, ga,
                 wq_gate, wq_up, raw_early, gate_in, up_in):
    sem = semaphores(nc, scope)
    WG = HG * P
    q_st = sb(scope, "q_st", [P, 2, 2, P], F32R)
    rope_st = sb(scope, "rope_st", [P, 2, P])
    k_st = sb(scope, "k_st", [P, 2, 2, 2, P], F32R)
    v_st = sb(scope, "v_st", [P, 2, 2, 2, P], F32R)
    ck_st = sb(scope, "ck_st", [P, 2, 2, 2, P], F32R)
    sq = sb(scope, "sq", [P, HG, D])
    ss = sb(scope, "ss", [P, 2, HG])
    rq = sb(scope, "rq", [P, 2, HG])
    exponent = sb(scope, "exponent", [P, HG])
    spare, settled = sb(scope, "spare", [P, 2 * UNROLL]), [0]
    qn = sb(scope, "qn", [P, 2, HG, D])
    ropb = sb(scope, "ropb2", [P, HG, 2 * HALF])
    q32 = sb(scope, "q32", [P, WG])
    qT = sb(scope, "qT", [P, 2, 2, WG], F32R)
    prob = sb(scope, "prob", [P, 2, WG])
    MASKED, WHOLE = 0, 1
    pp = sb(scope, "pp", [P, 2, 2, 2, WG], F32R)
    logits = sb(scope, "logits", [P, GPT, HG, NB + 1])
    cs = sb(scope, "cs", [P, 2, HG, NB + 1])
    cmx = sb(scope, "cmx", [P, 2, HG])
    csm = sb(scope, "csm", [P, 2, HG])
    crs = sb(scope, "crs", [P, 2, HG])
    pc = sb(scope, "pc", [P, 2, HG * NB])
    pcT = sb(scope, "pcT", [P, 2, 2, 2 * P], F32R)
    o_sb = sb(scope, "o_sb", [P, WG])
    ao = sb(scope, "ao", [P, WG])
    aoT = sb(scope, "aoT", [P, 2, 2, WG], F32R)
    den = sb(scope, "den", [P, P])
    rec = sb(scope, "rec", [P, P])
    rec_hi = sb(scope, "rec_hi", [P, P], F32R)
    rec_odd = sb(scope, "rec_odd", [P, P])
    sink_f_odd = sb(scope, "sink_f_odd", [P, GPT])
    rden = sb(scope, "rden", [P, 2, P], F32R)
    x_t = sb(scope, "x_t", [P, 2, C])
    y_t = sb(scope, "y_t", [P, C])

    names = ("consts q_mm q_sq q_ms q_rs q_sc q_r1 q_rope qT_mm q32_out qT_hi qT_lo "
             "sc_mm cc_mm merged tanhed exped p_hi p_lo pm_hi pm_lo "
             "c_log c_max c_sub c_exp c_sum c_rec c_nrm cT_mm cT_hi cT_lo "
             "pv_mm o_out sm_mm den_st den_full rec_st r_hi r_lo rb_mm cv_mm ao1 ao2 ao_hi ao_lo wp_mm y_st x_done").split()
    names += [f"{n}{slot}" for n in ("q_in", "rope_in", "k_in", "v_in", "c_in", "x_in", "x_out") for slot in range(2)]
    s = {n: sem("a_" + n) for n in names}
    block = scope.enter_context(nc.Block())

    Q, T, SD, SPV, CC, O, RB, Y = bank
    BODIES = GROUPS // UNROLL
    PROLOGUE = 1
    DEPTH = 5

    class At:

        def __init__(self, m, r, lag):
            self.m, self.c = m, r - lag
            self.slot, self.j = self.c % 2, self.c % GPT
            self.tile_slot = (self.c // GPT) % 2
            self.live = not isinstance(m, int) or 0 <= m * UNROLL + self.c < GROUPS

        def n(self, back=0, per=1):
            return self.m * (UNROLL * per) + (self.c + 1 - back) * per

        def tile(self):
            return self.m * (UNROLL // GPT) + self.c // GPT

        def tiles(self, back=0):
            return self.tile() + (1 - back)

        def loaded(self):
            return (self.m + self.c // UNROLL) * 16 + 16

    def steps(engine, *operations):
        def step(m, r):
            for lag, operation in operations:
                g = At(m, r, lag)
                if g.live:
                    operation(g)
        for m in range(PROLOGUE):
            for r in range(UNROLL):
                step(m, r)
        with engine.Fori(PROLOGUE, BODIES) as m:
            for r in range(UNROLL):
                step(m, r)
        for r in range(DEPTH):
            step(BODIES, r)

    def wait(engine, name, count):
        if since(count):
            engine.wait_ge(s[name], count)

    @block.tensor
    def _(pe):
        def three(out, pairs, start=True, stop=True):
            n = len(pairs)
            for q, (lhs, rhs) in enumerate(pairs):
                for u, (a, b) in enumerate(((0, 0), (0, 1), (1, 0))):
                    last = pe.matmul(out, lhs[a], rhs[b], start=start and q == 0 and u == 0,
                                     stop=stop and q == n - 1 and u == 2)
            return last

        def query(g):
            wait(pe, f"q_in{g.tile_slot}", g.loaded())
            wait(pe, "q_sc", g.n(1))
            cols = slice(g.j * WG, (g.j + 1) * WG)
            three(Q[:], [((q_st[:, g.tile_slot, 0], q_st[:, g.tile_slot, 1]), (wup[:, 0, cols], wup[:, 1, cols]))]
                  ).then_inc(s["q_mm"], 1)

        def compressed_values(g):
            wait(pe, "cT_lo", g.n())
            wait(pe, f"c_in{g.tile_slot}", g.loaded())
            wait(pe, "o_out", g.n())
            cp = ck_st[:, g.tile_slot]
            out = O[:].rearrange("p (pair half n) -> p half pair n", half=2, n=P)
            for half in range(2):
                last = three(out[:, half], [((cp[:, half, 0], cp[:, half, 1]),
                                             tuple(pcT[:, g.slot, part].rearrange("p (pair n) -> p pair n", n=P)
                                                   for part in range(2)))])
            last.then_inc(s["cv_mm"], 1)

        def window_scores(g):
            wait(pe, "qT_lo", g.n())
            wait(pe, f"k_in{g.tile_slot}", g.loaded())
            wait(pe, "tanhed", g.n(1))
            ks = k_st[:, g.tile_slot]
            query_parts = (qT[:, g.slot, 0], qT[:, g.slot, 1])
            three(SPV[:], [((ks[:, 0, 0], ks[:, 0, 1]), query_parts)])
            three(SD[:], [((ks[:, 1, 0], ks[:, 1, 1]), query_parts)]).then_inc(s["sc_mm"], 1)

        def sums(g):
            wait(pe, "p_lo", g.n())
            wait(pe, "pm_lo", g.n())
            wait(pe, "pm_hi", g.n())
            wait(pe, "ao1", g.n(1))
            which = (g.tile() % TPB + TPB - 1) // TPB if g.tile_slot == 0 else WHOLE
            for h in range(HG):
                moving = pp[:, g.slot, bass.ds(which, 1), :, h * P:(h + 1) * P].rearrange("p w a n -> p (w a) n")
                last = pe.matmul(RB[:, 0:2 * P].rearrange("p (a n) -> p a n", a=2), sumsel[:, h], moving,
                                 start=(h == 0), stop=(h == HG - 1))
            last.then_inc(s["sm_mm"], 1)

        def window_values(g):
            wait(pe, f"v_in{g.tile_slot}", g.loaded())
            wait(pe, "ao2", g.n(1))
            vs = v_st[:, g.tile_slot]
            three(O[:], [((vs[:, 0, 0], vs[:, 0, 1]), (pp[:, g.slot, WHOLE, 0], pp[:, g.slot, WHOLE, 1])),
                         ((vs[:, 1, 0], vs[:, 1, 1]), (pp[:, g.slot, MASKED, 0], pp[:, g.slot, MASKED, 1]))]
                  ).then_inc(s["pv_mm"], 1)

        def project(g):
            wait(pe, "ao_lo", g.n())
            if g.j == 0:
                wait(pe, "y_st", g.tile())
            for h in range(HG):
                head = g.j * HG + h
                lhs = [aoT[:, g.slot, part, h * P:(h + 1) * P] for part in range(2)]
                last = three(Y[:], [(lhs, (fold[:, head, 0], fold[:, head, 1]))],
                             start=(g.j == 0 and h == 0), stop=(g.j == GPT - 1 and h == HG - 1))
            last.then_inc(s["wp_mm"], 1)

        def transpose_query(g):
            wait(pe, "q_rope", g.n())
            wait(pe, "cT_lo", g.n(2))
            for h in range(HG):
                last = pe.transpose(T[:, h * P:(h + 1) * P], qn[:, g.slot, h], ident)
            last.then_inc(s["qT_mm"], 1)

        def denominators(g):
            wait(pe, "r_lo", g.n())
            for h in range(HG):
                last = pe.matmul(RB[:, h * P:(h + 1) * P], rowsel[:, h], rden[:, g.slot], start=True, stop=True)
            last.then_inc(s["rb_mm"], 1)

        def compressed_scores(g):
            wait(pe, "q32_out", g.n())
            wait(pe, "c_log", g.n(1))
            keys = ckT[:, bass.ds(g.tile() // TPB * NB, NB)]
            for h in range(HG):
                last = pe.matmul(CC[:, h * NB:(h + 1) * NB], q32[:, h * P:(h + 1) * P], keys,
                                 start=True, stop=True)
            last.then_inc(s["cc_mm"], 1)

        def transpose_compressed(g):
            wait(pe, "c_nrm", g.n())
            ahead = At(g.m, g.c + 1, 0)
            if ahead.live:
                wait(pe, "q32_out", ahead.n())
            for pair in range(2):
                cols = slice(pair * P, (pair + 1) * P)
                last = pe.transpose(T[:, cols], pc[:, g.slot, cols], ident)
            last.then_inc(s["cT_mm"], 1)

        wait(pe, "consts", 3)
        steps(pe, (0, query), (3, denominators), (1, compressed_scores), (2, transpose_compressed),
              (3, compressed_values), (2, sums), (1, window_scores), (2, window_values), (4, project),
              (0, transpose_query))

    @block.scalar
    def _(act):
        def probs_high(g):
            wait(act, "exped", g.n())
            wait(act, "pv_mm", g.n(2))
            act.activation(pp[:, g.slot, WHOLE, 0], prob[:, g.slot], ACT.Copy).then_inc(s["p_hi"], 1)

        def squares(g):
            wait(act, "q_mm", g.n())
            wait(act, "q_ms", g.n(2))
            for h in range(HG):
                last = act.activation(sq[:, h], Q[:, h * D:(h + 1) * D], ACT.Square, accum_out=ss[:, g.slot, h:h + 1])
            last.then_inc(s["q_sq"], 1)

        def compressed_high(g):
            wait(act, "cT_mm", g.n())
            wait(act, "cv_mm", g.n(2))
            act.activation(pcT[:, g.slot, 0], T[:, 0:2 * P], ACT.Copy).then_inc(s["cT_hi"], 1)

        def out_high(g):
            wait(act, "ao2", g.n())
            wait(act, "wp_mm", g.n(2))
            act.activation(aoT[:, g.slot, 0], ao[:], ACT.Copy).then_inc(s["ao_hi"], 1)

        def denominator(g):
            wait(act, "sm_mm", g.n())
            wait(act, "rec_st", g.n(1))
            act.activation(den[:], RB[:, 0:P], ACT.Identity, scale=sink_f[:, g.j:g.j + 1],
                           bias=sink_g[:, g.j:g.j + 1]).then_inc(s["den_st"], 1)

        def compressed_exp(g):
            wait(act, "c_sub", g.n())
            act.activation(cs[:, g.slot], cs[:, g.slot], ACT.Exp).then_inc(s["c_exp"], 1)

        def window_out(g):
            wait(act, "pv_mm", g.n())
            wait(act, "ao1", g.n(1))
            act.activation(o_sb[:], O[:], ACT.Copy).then_inc(s["o_out"], 1)

        def reciprocal_high(g):
            wait(act, "rec_st", g.n())
            wait(act, "r_lo", g.n(1))
            act.activation(rec_odd[:], rec[:], ACT.Copy, scale=sink_f_odd[:, g.j:g.j + 1])
            act.activation(rec_hi[:], rec[:], ACT.Copy, scale=sink_f[:, g.j:g.j + 1]).then_inc(s["r_hi"], 1)

        def tanh(g):
            wait(act, "merged", g.n())
            wait(act, "p_lo", g.n(2))
            act.activation(prob[:, g.slot], SD[:], ACT.Tanh, scale=SCALE / CAP).then_inc(s["tanhed"], 1)

        def exp(g):
            wait(act, "tanhed", g.n())
            act.activation(prob[:, g.slot], prob[:, g.slot], ACT.Exp, scale=CAP).then_inc(s["exped"], 1)

        def query_out(g):
            wait(act, "qT_mm", g.n())
            wait(act, "cc_mm", g.n(1))
            wait(act, "qT_lo", g.n(1))
            act.activation(q32[:], T[:], ACT.Copy, scale=qw_col[:, 0:1]).then_inc(s["q32_out"], 1)

        def query_high(g):
            wait(act, "q32_out", g.n())
            wait(act, "sc_mm", g.n(2))
            act.activation(qT[:, g.slot, 0], q32[:], ACT.Copy).then_inc(s["qT_hi"], 1)

        wait(act, "consts", 3)
        for w, (weights, arrived) in enumerate(((wq_gate, gate_in), (wq_up, up_in))):
            act.dma_start(raw_early[:, w], weights[0:EARLY * P, :].rearrange("(h p) c -> p h c", p=P)).then_inc(arrived, 16)
        steps(act, (1, query_out), (0, squares), (1, query_high), (2, compressed_high), (2, denominator),
              (1, compressed_exp), (3, out_high), (1, tanh), (1, exp), (1, probs_high), (2, window_out),
              (2, reciprocal_high))

    @block.vector
    def _(dve):
        def compressed_logits(g):
            wait(dve, "cc_mm", g.n())
            wait(dve, "c_sub", g.n(4))
            mask = kons[:, bass.ds(K_CMASK + (g.tile() % TPB) * NB, NB)].unsqueeze(1).broadcast_to([P, HG, NB])
            dve.scalar_tensor_tensor(logits[:, g.j, :, 0:NB], CC[:, 0:2 * P].rearrange("p (h n) -> p h n", h=HG),
                                     SCALE, mask, ALU.mult, ALU.add).then_inc(s["c_log"], 1)

        def query_low(g):
            wait(dve, "qT_hi", g.n())
            dve.tensor_tensor(qT[:, g.slot, 1], q32[:], qT[:, g.slot, 0].bitcast(F32),
                              ALU.subtract).then_inc(s["qT_lo"], 1)

        def compressed_max(g):
            wait(dve, "c_log", g.n())
            wait(dve, "c_sub", g.n(2))
            dve.tensor_reduce(cmx[:, g.slot], logits[:, g.j], AX.X, ALU.max).then_inc(s["c_max"], 1)

        def add_compressed(g):
            wait(dve, "cv_mm", g.n())
            wait(dve, "ao1", g.n())
            dve.tensor_tensor(ao[:], ao[:], O[:], ALU.add).then_inc(s["ao2"], 1)

        def mean_square(g):
            wait(dve, "q_sq", g.n())
            wait(dve, "q_sc", g.n(2))
            dve.tensor_scalar(rq[:, g.slot], ss[:, g.slot], 1.0 / D, RMS_EPS, ALU.mult, ALU.add
                              ).then_inc(s["q_ms"], 1)

        def compressed_low(g):
            wait(dve, "cT_hi", g.n())
            dve.tensor_tensor(pcT[:, g.slot, 1], T[:, 0:2 * P], pcT[:, g.slot, 0].bitcast(F32),
                              ALU.subtract).then_inc(s["cT_lo"], 1)

        def out_low(g):
            wait(dve, "ao_hi", g.n())
            dve.tensor_tensor(aoT[:, g.slot, 1], ao[:], aoT[:, g.slot, 0].bitcast(F32),
                              ALU.subtract).then_inc(s["ao_lo"], 1)

        def scale_query(g):
            wait(dve, "q_rs", g.n())
            wait(dve, "qT_mm", g.n(2))
            dve.tensor_tensor(qn[:, g.slot], Q[:].rearrange("p (h d) -> p h d", h=HG),
                              rq[:, g.slot].unsqueeze(2).broadcast_to([P, HG, D]), ALU.mult).then_inc(s["q_sc"], 1)

        def merge(g):
            wait(dve, "sc_mm", g.n())
            settled[0] = (settled[0] + 1) % spare.shape[1]
            dve.tensor_tensor(spare[:, settled[0]:settled[0] + 1], low[:, 0:1], low[:, 0:1], ALU.mult)
            up = kons[:, K_UP:K_UP + P].bitcast(U32).unsqueeze(1).broadcast_to([P, HG, P])
            dve.copy_predicated(SD[:].rearrange("p (h n) -> p h n", h=HG), up,
                                SPV[:].rearrange("p (h n) -> p h n", h=HG)).then_inc(s["merged"], 1)

        def reciprocal(g):
            wait(dve, "den_st", g.n())
            dve.scalar_tensor_tensor(den[:], RB[:, P:2 * P], sink_f[:, g.j:g.j + 1], den[:], ALU.mult, ALU.add
                                     ).then_inc(s["den_full"], 1)
            wait(dve, "den_full", g.n())
            wait(dve, "r_lo", g.n(1))
            dve.reciprocal(rec[:], den[:]).then_inc(s["rec_st"], 1)

        def compressed_sum(g):
            wait(dve, "c_exp", g.n())
            dve.tensor_reduce(csm[:, g.slot], cs[:, g.slot], AX.X, ALU.add).then_inc(s["c_sum"], 1)
            wait(dve, "c_sum", g.n())
            wait(dve, "c_nrm", g.n(2))
            dve.reciprocal(crs[:, g.slot], csm[:, g.slot]).then_inc(s["c_rec"], 1)

        def reciprocal_low(g):
            wait(dve, "r_hi", g.n())
            wait(dve, "rb_mm", g.n(2))
            dve.scalar_tensor_tensor(rden[:, g.slot], rec_hi[:].bitcast(F32), kons[:, K_SIGN:K_SIGN + 1], rec_odd[:],
                                     ALU.mult, ALU.add).then_inc(s["r_lo"], 1)

        def tile_out(g):
            if g.j == GPT - 1:
                wait(dve, "wp_mm", g.n())
                wait(dve, "x_done", g.tile())
                dve.tensor_tensor(y_t[:], Y[:], ga[:, bass.ds(g.tile() // TPB, 1), :].rearrange("p b c -> p (b c)"),
                                  ALU.mult).then_inc(s["y_st"], 1)

        def masked_low(g):
            wait(dve, "p_lo", g.n())
            dve.tensor_tensor(pp[:, g.slot, MASKED, 1].rearrange("p (h n) -> p h n", h=HG),
                              pp[:, g.slot, WHOLE, 1].bitcast(F32).rearrange("p (h n) -> p h n", h=HG),
                              low.unsqueeze(1).broadcast_to([P, HG, P]), ALU.mult).then_inc(s["pm_lo"], 1)

        def divide(g):
            wait(dve, "o_out", g.n())
            wait(dve, "rb_mm", g.n())
            wait(dve, "ao_lo", g.n(1))
            dve.tensor_tensor(ao[:], o_sb[:], RB[:], ALU.mult).then_inc(s["ao1"], 1)

        dve.memset(exponent[:], -0.5).then_inc(s["consts"], 1)
        dve.tensor_copy(logits[:].rearrange("p g h n -> p (g h) n")[:, :, NB], sinkb[:]).then_inc(s["consts"], 1)
        dve.tensor_scalar(sink_f_odd[:], sink_f[:], kons[:, K_SIGN + 1:K_SIGN + 2], None, ALU.mult).then_inc(s["consts"], 1)
        wait(dve, "consts", 3)
        steps(dve, (3, reciprocal_low), (2, masked_low), (3, divide), (0, mean_square), (1, compressed_logits),
              (1, query_low), (1, compressed_max), (3, add_compressed), (2, compressed_low), (0, scale_query),
              (1, merge), (1, compressed_sum), (2, reciprocal), (3, out_low), (4, tile_out))

    @block.gpsimd
    def _(pool):
        def masked_high(g):
            wait(pool, "p_hi", g.n())
            pool.tensor_tensor(pp[:, g.slot, MASKED, 0].rearrange("p (h n) -> p h n", h=HG),
                               pp[:, g.slot, WHOLE, 0].bitcast(F32).rearrange("p (h n) -> p h n", h=HG),
                               low.unsqueeze(1).broadcast_to([P, HG, P]), ALU.mult).then_inc(s["pm_hi"], 1)

        def rsqrt(g):
            wait(pool, "q_ms", g.n())
            pool.tensor_tensor(rq[:, g.slot], rq[:, g.slot], exponent[:], ALU.pow).then_inc(s["q_rs"], 1)

        def compressed_less_max(g):
            wait(pool, "c_max", g.n())
            wait(pool, "c_sum", g.n(2))
            wait(pool, "c_nrm", g.n(2))
            pool.tensor_tensor(cs[:, g.slot], logits[:, g.j], cmx[:, g.slot].unsqueeze(2).broadcast_to([P, HG, NB + 1]),
                               ALU.subtract).then_inc(s["c_sub"], 1)

        def rotate(g):
            wait(pool, "q_sc", g.n())
            wait(pool, "q_rope", g.n(1))
            wait(pool, f"rope_in{g.tile_slot}", g.loaded())
            over = lambda lo, n: rope_st[:, g.tile_slot, lo:lo + n].unsqueeze(1).broadcast_to([P, HG, n])
            x = qn[:, g.slot]
            pool.tensor_tensor(ropb[:, :, 0:HALF], x[:, :, HALF:2 * HALF], over(2 * HALF, HALF),
                               ALU.mult).then_inc(s["q_r1"], 1)
            pool.tensor_tensor(ropb[:, :, HALF:], x[:, :, 0:HALF], over(3 * HALF, HALF), ALU.mult).then_inc(s["q_r1"], 1)
            wait(pool, "q_r1", g.n(1, 3) + 2)
            pool.tensor_tensor(x[:, :, 0:2 * HALF], x[:, :, 0:2 * HALF], over(0, 2 * HALF), ALU.mult).then_inc(s["q_r1"], 1)
            wait(pool, "q_r1", g.n(per=3))
            pool.tensor_tensor(x[:, :, 0:2 * HALF], x[:, :, 0:2 * HALF], ropb[:], ALU.add).then_inc(s["q_rope"], 1)

        def probs_low(g):
            wait(pool, "p_hi", g.n())
            pool.tensor_tensor(pp[:, g.slot, WHOLE, 1], prob[:, g.slot], pp[:, g.slot, WHOLE, 0].bitcast(F32),
                               ALU.subtract).then_inc(s["p_lo"], 1)

        def compressed_over_sum(g):
            wait(pool, "c_rec", g.n())
            wait(pool, "cT_mm", g.n(2))
            pool.tensor_tensor(pc[:, g.slot].rearrange("p (h n) -> p h n", h=HG), cs[:, g.slot, :, 0:NB],
                               crs[:, g.slot].unsqueeze(2).broadcast_to([P, HG, NB]), ALU.mult
                               ).then_inc(s["c_nrm"], 1)

        def add_tile(g):
            if g.j == GPT - 1:
                slot = g.tile_slot
                wait(pool, "y_st", g.tiles())
                wait(pool, f"x_in{slot}", g.loaded())
                pool.tensor_tensor(x_t[:, slot], x_t[:, slot], y_t[:], ALU.add).then_inc(s["x_done"], 1)

        wait(pool, "consts", 3)
        steps(pool, (2, compressed_over_sum), (2, masked_high), (0, rsqrt), (5, add_tile), (1, compressed_less_max), (0, rotate),
              (1, probs_low))

    @block.sync
    def _(sp):
        def load(t, slot, nth):
            def free(name, count):
                if since(count):
                    sp.wait_ge(s[name], count)
            free("q_mm", GPT * (t - 1))
            sp.dma_start(q_st[:, slot].bitcast(F32), q_parts[bass.ds(t, 1)].rearrange("t p a n -> (t p) a n")
                         ).then_inc(s[f"q_in{slot}"], 16)
            free("q_rope", GPT * (t - 1))
            sp.dma_start(rope_st[:, slot], table[:, bass.ds(K_ROPE + (t % TPB) * P, P)]).then_inc(s[f"rope_in{slot}"], 16)
            free("sc_mm", GPT * (t - 1))
            sp.dma_start(k_st[:, slot].bitcast(F32), k_parts[bass.ds(t + t // TPB, 2)].rearrange("t p a n -> p t a n")
                         ).then_inc(s[f"k_in{slot}"], 16)
            free("pv_mm", GPT * (t - 1))
            sp.dma_start(v_st[:, slot].rearrange("p a b n -> p (a b) n").bitcast(F32),
                         v_parts[bass.ds(t, 1)].rearrange("t p a n -> (t p) a n")).then_inc(s[f"v_in{slot}"], 16)
            free("cv_mm", GPT * (t - 1))
            sp.dma_start(ck_st[:, slot].rearrange("p a b n -> p (a b) n").bitcast(F32),
                         ck_parts[bass.ds(t // TPB, 1)].rearrange("t p a n -> (t p) a n")).then_inc(s[f"c_in{slot}"], 16)

        def store(t, slot, nth):
            sp.wait_ge(s["x_done"], t + 1)
            sp.dma_start(token_rows(x_mid, t), x_t[:, slot]).then_inc(s[f"x_out{slot}"], 16)
            sp.wait_ge(s[f"x_out{slot}"], 16 * nth + 16)

        def load_x(t, slot):
            sp.dma_start(x_t[:, slot], token_rows(x_tok, t)).then_inc(s[f"x_in{slot}"], 16)

        for t in range(4):
            if t == 3:
                store(0, 0, 0)
                load_x(2, 0)
            load(t, t % 2, t // 2)
            if t < 2:
                load_x(t, t)
        with sp.Fori(2, TILES // 2) as n:
            for slot in range(2):
                t = 2 * n + slot
                store(2 * n + (slot - 3), 1 - slot, n + (slot - 3) // 2)
                load_x(2 * n + (slot - 1), 1 - slot)
                load(t, slot, n)
        for t in range(TILES - 3, TILES):
            store(t, t % 2, t // 2)
            if t == TILES - 3:
                load_x(TILES - 1, (TILES - 1) % 2)


def ffn_prepare(nc, scope, sb, bank, wq_gate, wq_up, s_gate, s_up, wq_down, ident, raw_early, gate_in, up_in,
                wT, wd, sg, inexact, x_mid, xs, x_in):
    sem = semaphores(nc, scope, "f_")
    raw_late = sb(scope, "raw_late", [P, 2, HB - EARLY, C], I32)
    raw_down = sb(scope, "raw_down", [P, 2, HID], I32)
    conv = sb(scope, "conv", [P, 2, 2, C])
    conv_down = raw_down[:].bitcast(F32)
    junk = sb(scope, "junk", [P, 2 * C])
    junk_d = conv[:, 0, 0]
    ones = sb(scope, "ones", [P, P])
    square = sb(scope, "square", [P, HB + 3 * KC])
    flag = sb(scope, "flag", [P, 2])
    down_in = [sem("down_in0"), sem("down_in1")]
    gate_late, up_late = sem("gate_late"), sem("up_late")
    small_in, conved, tr_mm, w_hi, w_lo, squared, flagged, flag_mm = map(sem, (
        "small_in", "conved", "tr_mm", "w_hi", "w_lo", "squared", "flagged", "flag_mm"))
    block = scope.enter_context(nc.Block())
    THIRDS = [(lo, min(lo + 4, HB)) for lo in range(0, HB, 4)]

    def blocks(engine, body):
        for h in range(3):
            body(h, h % 2)
        with engine.Fori(1, EARLY // 2) as i:
            body(2 * i + 1, 1)
            body(2 * i + 2, 0)
        with engine.Fori(EARLY // 2, HB // 2) as i:
            body(2 * i + 1, 1, True)
            body(2 * i + 2, 0, True)

    @block.sync
    def _(sp):
        for w, (weights, arrived) in enumerate(((wq_gate, gate_late), (wq_up, up_late))):
            sp.dma_start(raw_late[:, w], weights[EARLY * P:, :].rearrange("(h p) c -> p h c", p=P)).then_inc(arrived, 16)
        for o in range(2):
            sp.dma_start(raw_down[:, o], wq_down[o * P:(o + 1) * P, :]).then_inc(down_in[o], 16)
        sp.dma_start(sg[:, 0], s_gate.rearrange("(h p) -> p h", p=P), allow_slow_non_contiguous=True).then_inc(small_in, 16)
        sp.dma_start(sg[:, 1], s_up.rearrange("(h p) -> p h", p=P), allow_slow_non_contiguous=True).then_inc(small_in, 16)
        sp.wait_ge(conved, 2 * EARLY)
        for c in range(2):
            load_ffn_chunk(sp, x_mid, xs, x_in, c)
        for o in range(2, KC):
            sp.wait_ge(tr_mm, 2 * HB + 3 * (o - 1))
            sp.dma_start(raw_down[:, o % 2], wq_down[o * P:(o + 1) * P, :]).then_inc(down_in[o % 2], 16)
        sp.wait_ge(small_in, 32)

    @block.vector
    def _(dve):
        def convert(h, parity, late):
            for w, arrived in enumerate((gate_late, up_late) if late else (gate_in, up_in)):
                dve.wait_ge(arrived, 16)
                raw, at = (raw_late, h - EARLY) if late else (raw_early, h)
                if not isinstance(h, int) or h >= 2:
                    dve.wait_ge(tr_mm, 2 * h + (w - 3))
                dve.tensor_scalar(conv[:, parity, w:w + 1], raw[:, w, bass.ds(at, 1)], -ZERO_POINT, None,
                                  ALU.add).then_inc(conved, 1)

        def low(h, parity):
            for w in range(2):
                dve.wait_ge(w_hi, 2 * h + (w + 1))
                out = wT[:, bass.ds(h, 1), w].rearrange("p a s k n -> p (a s) k n")
                dve.tensor_tensor(out[:, 1], bank[2 * parity + w][:].rearrange("p (k n) -> p k n", k=KC),
                                  out[:, 0].bitcast(F32), ALU.subtract).then_inc(w_lo, 1)

        def convert_and_low(h, parity, late=False):
            convert(h, parity, late)
            if since(h):
                low(h - 1, 1 - parity)

        dve.memset(ones[:], 1.0).then_inc(flagged, 1)
        blocks(dve, convert_and_low)
        low(HB - 1, 0)
        def convert_down(o):
            dve.wait_ge(down_in[o % 2], 16 * (o // 2) + 16)
            dve.tensor_scalar(conv_down[:, o % 2], raw_down[:, o % 2], -ZERO_POINT, None, ALU.add).then_inc(conved, 1)

        convert_down(0)
        for o in range(KC):
            if o + 1 < KC:
                convert_down(o + 1)
            for n, (lo, hi) in enumerate(THIRDS):
                q = 3 * o + n
                dve.wait_ge(w_hi, 2 * HB + q + 1)
                dve.tensor_tensor(wd[:, lo:hi, 1, o * P:(o + 1) * P],
                                  bank[4 + q % 4][:, 0:(hi - lo) * P].rearrange("p (h n) -> p h n", n=P),
                                  wd[:, lo:hi, 0, o * P:(o + 1) * P].bitcast(F32), ALU.subtract).then_inc(w_lo, 1)
        dve.wait_ge(squared, HB + 3 * KC)
        dve.tensor_reduce(flag[:, 0:1], square[:], AX.X, ALU.max).then_inc(flagged, 1)
        dve.wait_ge(flagged, 2)
        dve.tensor_scalar(flag[:, 1:2], flag[:, 0:1], 0.0, None, ALU.is_gt).then_inc(flagged, 1)
        dve.wait_ge(flag_mm, 1)
        dve.tensor_copy(inexact[:], bank[0][:, 0:1])

    @block.scalar
    def _(act):
        def high(h, parity):
            for w in range(2):
                act.wait_ge(tr_mm, 2 * h + (w + 1))
                act.activation(wT[:, bass.ds(h, 1), w, 0].rearrange("p a k n -> p (a k) n"),
                               bank[2 * parity + w][:].rearrange("p (k n) -> p k n", k=KC), ACT.Copy).then_inc(w_hi, 1)

        def squares(h):
            act.wait_ge(w_lo, 2 * h + 2)
            if since(h):
                act.wait_ge(squared, h)
            act.activation(junk[:].rearrange("p (w k n) -> p w k n", w=2, k=KC),
                           wT[:, bass.ds(h, 1), :, 1].rearrange("p a w k n -> p (a w) k n").bitcast(F32),
                           ACT.Square, accum_out=square[:, bass.ds(h, 1)]).then_inc(squared, 1)

        def high_and_squares(h, parity, late=False):
            high(h, parity)
            if since(h):
                squares(h - 1)

        blocks(act, high_and_squares)
        squares(HB - 1)

        def down_high(q, o, lo, hi):
            act.wait_ge(tr_mm, 2 * HB + q + 1)
            act.activation(wd[:, lo:hi, 0, o * P:(o + 1) * P],
                           bank[4 + q % 4][:, 0:(hi - lo) * P].rearrange("p (h n) -> p h n", n=P),
                           ACT.Copy).then_inc(w_hi, 1)

        def down_squares(q, o, lo, hi):
            act.wait_ge(w_lo, 2 * HB + q + 1)
            act.wait_ge(squared, HB + q)
            act.activation(junk_d[:, 0:(hi - lo) * P].rearrange("p (h n) -> p h n", n=P),
                           wd[:, lo:hi, 1, o * P:(o + 1) * P].bitcast(F32), ACT.Square,
                           accum_out=square[:, HB + q:HB + q + 1]).then_inc(squared, 1)

        pieces = [(3 * o + n, o, lo, hi) for o in range(KC) for n, (lo, hi) in enumerate(THIRDS)]
        for piece in pieces:
            down_high(*piece)
            if piece[0]:
                down_squares(*pieces[piece[0] - 1])
        down_squares(*pieces[-1])

    @block.tensor
    def _(pe):
        def transpose(h, parity, late=False):
            for w in range(2):
                pe.wait_ge(conved, 2 * h + (w + 1))
                if not isinstance(h, int) or h >= 2:
                    pe.wait_ge(w_lo, 2 * h + (w - 3))
                for k in range(KC):
                    last = pe.transpose(bank[2 * parity + w][:, k * P:(k + 1) * P],
                                        conv[:, parity, w, k * P:(k + 1) * P], ident)
                last.then_inc(tr_mm, 1)

        blocks(pe, transpose)
        for o in range(KC):
            pe.wait_ge(conved, 2 * HB + o + 1)
            for n, (lo, hi) in enumerate(THIRDS):
                q = 3 * o + n
                if q >= 4:
                    pe.wait_ge(w_lo, 2 * HB + q - 3)
                for h in range(lo, hi):
                    last = pe.transpose(bank[4 + q % 4][:, (h - lo) * P:(h - lo + 1) * P],
                                        conv_down[:, o % 2, h * P:(h + 1) * P], ident)
                last.then_inc(tr_mm, 1)
        pe.wait_ge(flagged, 3)
        pe.wait_ge(w_lo, 2 * HB)
        pe.matmul(bank[0][:, 0:1], ones[:], flag[:, 1:2], start=True, stop=True).then_inc(flag_mm, 1)


def load_ffn_chunk(sp, x_mid, xs, x_in, c):
    sp.dma_start(xs[:, c % 2], x_mid[c * W:(c + 1) * W, :].rearrange("(t p) c -> p t c", p=P)).then_inc(x_in[c % 2], 16)


def ffn_block(nc, scope, sb, bank, x_mid, out_tok, ident, arena, xs, x_in, wT, wd, sg, row, modT, inexact):
    sem = semaphores(nc, scope, "g_")
    XS = 2 * CHUNK * C
    gu = arena[:, XS:XS + 2 * W].rearrange("p (s w) -> p s w", s=2)
    z = sb(scope, "z2", [P, CHUNK, C])
    scaled = z[:, 0]
    hfull = sb(scope, "hfull2", [P, W])
    stats = sb(scope, "stats2", [P, CHUNK, 6])
    meanvar = sb(scope, "meanvar2", [P, CHUNK, 2])
    rstd = sb(scope, "rstd2", [P, CHUNK])
    minus_half = sb(scope, "minus_half2", [P, CHUNK])
    hT = sb(scope, "hT2", [P, 2, 2, KC, W], F32R)
    gus = sb(scope, "gus", [P, 2, 2, W], F32R)
    x_out = [sem("x_out0"), sem("x_out1")]
    init, stat, var, rs, z_done, tr_mm, h_hi, h_lo, gu_mm, silued, gued, gu_hi, gu_lo, dn_mm, y1, y2 = map(sem, (
        "init stat var rs z_done tr_mm h_hi h_lo gu_mm silued gued gu_hi gu_lo dn_mm y1 y2".split()))
    block = scope.enter_context(nc.Block())
    Y, GU = bank[0:4], bank[4:8]
    AHEAD = HB - KC

    def channel_bank(c, k):
        return GU[k] if c == 0 else GU[2 * ((HB * (c - 1) + AHEAD + k) % 2)]

    @block.sync
    def _(sp):
        for c in range(2, CHUNKS):
            slot = c % 2
            sp.wait_ge(y2, CHUNK * (c - 1))
            sp.dma_start(out_tok[(c - 2) * W:(c - 1) * W, :].rearrange("(t p) c -> p t c", p=P), xs[:, slot]
                         ).then_inc(x_out[slot], 16)
            sp.wait_ge(x_out[slot], 16 * (c // 2))
            load_ffn_chunk(sp, x_mid, xs, x_in, c)
        for c in range(CHUNKS - 2, CHUNKS):
            for t in range(CHUNK):
                sp.wait_ge(y2, CHUNK * c + t + 1)
                sp.dma_start(out_tok[(c * CHUNK + t) * P:(c * CHUNK + t + 1) * P, :], xs[:, c % 2, t]
                             ).then_inc(x_out[c % 2], 16)
        for slot in range(2):
            sp.wait_ge(x_out[slot], 16 * (CHUNKS // 2 - 1 + CHUNK))

    @block.tensor
    def _(pe):
        def down(c, h, passes):
            pe.wait_ge(gu_lo, HB * c + h + 1)
            for t in range(CHUNK):
                if h == 0 and c:
                    pe.wait_ge(y1, CHUNK * (c - 1) + t + 1)
                for n, (w, x) in enumerate(passes):
                    last = pe.matmul(Y[t][:], gus[:, (HB * c + h) % 2, x, t * P:(t + 1) * P], wd[:, h, w],
                                     start=(h == 0 and n == 0), stop=(h == HB - 1 and n == len(passes) - 1))
            last.then_inc(dn_mm, 1)

        def transpose(c, k):
            pe.wait_ge(z_done, CHUNK * (c + 1))
            for t in range(CHUNK):
                last = pe.transpose(channel_bank(c, k)[:, t * P:(t + 1) * P], z[:, t, k * P:(k + 1) * P], ident)
            last.then_inc(tr_mm, 1)

        def chunks(passes):
            for k in range(KC):
                transpose(0, k)
            for c in range(CHUNKS):
                for h in range(HB):
                    n = HB * c + h
                    if n >= 2:
                        pe.wait_ge(gued, n - 1)
                    ahead = h >= AHEAD and c + 1 < CHUNKS
                    if ahead:
                        transpose(c + 1, h - AHEAD)
                    if n == 0:
                        pe.wait_ge(h_hi, 2 * 2)
                    for w in (1, 0):
                        if w == 0 and ahead:
                            pe.wait_ge(h_hi, 2 * (KC * (c + 1) + h - AHEAD) + 2)
                        for k in range(KC):
                            if h == 0 and w == 1:
                                pe.wait_ge(h_lo, KC * c + k + 1)
                            for q, (a, x) in enumerate(passes):
                                last = pe.matmul(GU[2 * (n % 2) + w][:], wT[:, h, w, a, k], hT[:, c % 2, x, k],
                                                 start=(k == 0 and q == 0), stop=(k == KC - 1 and q == len(passes) - 1))
                    last.then_inc(gu_mm, 1)
                    if n:
                        down((n - 1) // HB, (n - 1) % HB, passes)
            down(CHUNKS - 1, HB - 1, passes)

        low_parts = pe.value_load(inexact[0:1, 0:1], min_val=0, max_val=P)
        with pe.If(low_parts == 0):
            chunks(((0, 0), (0, 1)))
        with pe.If(low_parts > 0):
            chunks(((0, 0), (0, 1), (1, 0)))

    @block.scalar
    def _(act):
        def channels(c, k):
            n, b = KC * c + k, c // (CHUNKS // BATCH)
            act.wait_ge(tr_mm, n + 1)
            if c >= 2:
                act.wait_ge(gu_mm, HB * (c - 1))
            if n:
                act.wait_ge(h_lo, n)
            act.activation(hT[:, c % 2, 0, k], channel_bank(c, k)[:], ACT.Identity, scale=modT[:, KC + k, b:b + 1],
                           bias=modT[:, k, b:b + 1]).then_inc(h_hi, 1)
            act.activation(hfull[:], channel_bank(c, k)[:], ACT.Identity, scale=modT[:, KC + k, b:b + 1],
                           bias=modT[:, k, b:b + 1]).then_inc(h_hi, 1)

        for k in range(KC):
            channels(0, k)
        for c in range(CHUNKS):
            for h in range(HB):
                n = HB * c + h
                if h >= AHEAD and c + 1 < CHUNKS:
                    channels(c + 1, h - AHEAD)
                act.wait_ge(gu_mm, n + 1)
                if n >= 2:
                    act.wait_ge(gu_lo, n - 1)
                act.activation(gu[:, n % 2], GU[2 * (n % 2)][:], ACT.Silu,
                               scale=sg[:, 0, h:h + 1]).then_inc(silued, 1)
                act.wait_ge(gued, n + 1)
                if n >= 2:
                    act.wait_ge(dn_mm, n - 1)
                act.activation(gus[:, n % 2, 0], gu[:, n % 2], ACT.Copy).then_inc(gu_hi, 1)

    @block.vector
    def _(dve):
        dve.memset(minus_half[:], -0.5).then_inc(init, 1)

        def statistics(c):
            slot = c % 2
            dve.wait_ge(x_in[slot], 16 * (c // 2 + 1))
            if c:
                dve.wait_ge(rs, 2 * c)
            for t in range(CHUNK):
                dve.bn_stats(stats[:, t], xs[:, slot, t]).then_inc(stat, 1)
            for t in range(CHUNK):
                dve.wait_ge(stat, CHUNK * c + t + 1)
                dve.bn_aggr(meanvar[:, t], stats[:, t]).then_inc(var, 1)

        def normal(c, tiles):
            dve.wait_ge(rs, 2 * (c + 1))
            if c:
                dve.wait_ge(tr_mm, KC * c)
            for t in tiles:
                dve.tensor_scalar(z[:, t], xs[:, c % 2, t], meanvar[:, t, 0:1], rstd[:, t:t + 1],
                                  ALU.subtract, ALU.mult).then_inc(z_done, 1)

        def channels_low(c, k):
            dve.wait_ge(h_hi, 2 * (KC * c + k) + 2)
            dve.tensor_tensor(hT[:, c % 2, 1, k], hfull[:], hT[:, c % 2, 0, k].bitcast(F32), ALU.subtract
                              ).then_inc(h_lo, 1)

        def tiles_out(c):
            dve.wait_ge(dn_mm, HB * (c + 1))
            if c + 1 < CHUNKS:
                dve.wait_ge(tr_mm, KC * (c + 2))
            for t in range(CHUNK):
                n = CHUNK * c + t
                if n:
                    dve.wait_ge(y2, n)
                dve.tensor_tensor(scaled, Y[t][:], row[:, c // (CHUNKS // BATCH)], ALU.mult).then_inc(y1, 1)
                dve.wait_ge(y1, n + 1)
                dve.tensor_tensor(xs[:, c % 2, t], xs[:, c % 2, t], scaled, ALU.add).then_inc(y2, 1)

        statistics(0)
        normal(0, range(CHUNK))
        for k in range(KC):
            channels_low(0, k)
        for c in range(CHUNKS):
            for h in range(HB):
                n = HB * c + h
                if h >= AHEAD and c + 1 < CHUNKS:
                    channels_low(c + 1, h - AHEAD)
                dve.wait_ge(silued, n + 1)
                dve.scalar_tensor_tensor(gu[:, n % 2], GU[2 * (n % 2) + 1][:], sg[:, 1, h:h + 1],
                                         gu[:, n % 2],
                                         ALU.mult, ALU.mult).then_inc(gued, 1)
                if h == 0 and c:
                    tiles_out(c - 1)
                if c + 1 < CHUNKS:
                    if h == 3:
                        statistics(c + 1)
                    elif h in (4, 5):
                        normal(c + 1, range(2 * h - 8, 2 * h - 6))
        tiles_out(CHUNKS - 1)

    @block.gpsimd
    def _(pool):
        pool.wait_ge(init, 1)
        for c in range(CHUNKS):
            for h in range(HB):
                n = HB * c + h
                if (c, h) == (0, 0) or (h == 3 and c + 1 < CHUNKS):
                    k = c if h == 0 else c + 1
                    pool.wait_ge(var, CHUNK * (k + 1))
                    if k:
                        pool.wait_ge(z_done, CHUNK * k)
                    pool.tensor_scalar(rstd[:], meanvar[:, :, 1], 1.0, LN_EPS, ALU.mult, ALU.add).then_inc(rs, 1)
                    pool.wait_ge(rs, 2 * k + 1)
                    pool.tensor_tensor(rstd[:], rstd[:], minus_half[:], ALU.pow).then_inc(rs, 1)
                pool.wait_ge(gu_hi, n + 1)
                if n >= 2:
                    pool.wait_ge(dn_mm, n - 1)
                pool.tensor_tensor(gus[:, n % 2, 1], gu[:, n % 2], gus[:, n % 2, 0].bitcast(F32),
                                   ALU.subtract).then_inc(gu_lo, 1)


def _table(np):
    t = np.zeros((P, K_ALL), np.float32)
    p = np.arange(P)
    i = (p % (P // M)) * M + p // (P // M)
    t[:, K_IDENT:K_IDENT + P] = np.eye(P)
    t[:, K_LOW:K_LOW + P] = i[:, None] <= i[None, :]
    t[:, K_UP:K_UP + P] = i[:, None] > i[None, :]
    inv = np.float32(1.0) / np.float32(10000.0) ** (np.arange(0, 2 * HALF, 2, dtype=np.float32) / np.float32(2 * HALF))
    ang = np.arange(SEQ, dtype=np.float32)[:, None] * inv[None, :].astype(np.float32)
    cos, sin = np.cos(ang), np.sin(ang)
    rope = np.concatenate([cos, cos, -sin, sin], axis=1).reshape(TPB, P, P)[:, i]
    t[:, K_ROPE:K_IDENT] = rope.transpose(1, 0, 2).reshape(P, TPB * P)
    pos, end = np.arange(SEQ), np.arange(NB) * M + M - 1
    mask = np.where(end[None, :] < pos[:, None], 0.0, -1e30).reshape(TPB, P, NB)[:, i]
    t[:, K_CMASK:K_SIGN] = mask.transpose(1, 0, 2).reshape(P, TPB * NB)
    t[:, K_SIGN], t[:, K_SIGN + 1] = 1 - 2 * (p % 2), p % 2
    for h in range(HG):
        t[:, K_SUMSEL + h * P + 32 * h:K_SUMSEL + h * P + 32 * h + 32] = 1.0
        t[32 * h:32 * h + 2, K_ROWSEL + h * P:K_ROWSEL + (h + 1) * P] = 1.0
    return t


_INS = ["L0_attn_h", "L0_attn_Wq_c", "L0_attn_Wq_up", "L0_attn_Wk", "L0_attn_Wv", "L0_attn_W_comp",
        "L0_attn_q_norm_w", "L0_attn_k_norm_w", "L0_attn_sink", "L0_attn_Wg", "L0_attn_Wo",
        "L0_ffn_wq_gate", "L0_ffn_s_gate", "L0_ffn_wq_up", "L0_ffn_s_up", "L0_ffn_wq_down", "L0_ffn_s_down",
        "L0_c", "L0_wmod"]


def kernel(**inputs):
    import numpy as np
    import concourse.bacc as bacc
    from concourse.bass_utils import run_bass_kernel_spmd

    nc = bacc.Bacc("TRN2", target_bir_lowering=False, num_devices=1)
    arrays, args = {}, []
    for name, a in [(n, np.ascontiguousarray(inputs[n])) for n in _INS] + [("table", _table(np))]:
        arrays[f"in_{name}"] = a
        args.append(nc.dram_tensor(f"in_{name}", a.shape, mybir.dt.from_np(a.dtype), kind="ExternalInput").ap())
    out = nc.dram_tensor("out", (BATCH, SEQ, C), F32, kind="ExternalOutput").ap()
    build_program(nc, *args, out)
    r = run_bass_kernel_spmd(nc, [arrays], core_ids=[0])
    return r.results[0]["out"]
```
